# Optimizing a Trainium2 kernel written in Bass

```python
import numpy as np
import jax
import jax.numpy as jnp

def _softmax(x, axis=-1):
    return jax.nn.softmax(x, axis=axis)

def _gelu(x):
    return jax.nn.gelu(x, approximate=True)

def _silu(x):
    return jax.nn.silu(x)

def _sigmoid(x):
    return jax.nn.sigmoid(x)

def _layernorm(x, axis=-1, eps=1e-05):
    m = jnp.mean(x, axis=axis, keepdims=True)
    v = jnp.var(x, axis=axis, keepdims=True)
    return (x - m) / jnp.sqrt(v + eps)

def _scatter_add(tgt, idx, src, axis=0):
    return tgt.at[idx].add(src)

def _segment_sum(src, seg, n):
    return jax.ops.segment_sum(src, seg, n)
kernel_name = 'mk_xattn_ffn_d2_seqx_r8_a7111a'

def setup_inputs(seed: int=0):
    np.random.seed(seed)
    _w = jnp.asarray

    def _rec_inputs():
        import jax
        import jax.numpy as jnp
        _rk = jax.random.key(seed)
        x = 7.22e-05 + 1 * jax.random.normal(jax.random.fold_in(_rk, 1), (32, 128, 128), jnp.float32)
        _lenS = 128 - jax.random.randint(jax.random.fold_in(_rk, 7), (32,), 0, max(1, 128 // 4) + 1, jnp.int32)
        _lenS2 = 77 - jax.random.randint(jax.random.fold_in(_rk, 8), (32,), 0, max(1, 77 // 4) + 1, jnp.int32)
        _ctx_1024P = jax.random.normal(jax.random.fold_in(_rk, 11), (32, 16, 128), jnp.float32)
        _ctx_1024c = jax.random.dirichlet(jax.random.fold_in(_rk, 511), 0.3 * jnp.ones((16,), jnp.float32), (32, 77))
        _ctx_1024t = jnp.einsum('bsk,bkd->bsd', _ctx_1024c, _ctx_1024P)
        _ctx_1024t = _ctx_1024t * jax.lax.rsqrt(jnp.mean(jnp.square(_ctx_1024t)) + 1e-12) * 0.953939
        ctx_1024 = 4.13588e-05 + 0.999923 * (_ctx_1024t + 0.3 * jax.random.normal(jax.random.fold_in(_rk, 611), (32, 77, 128), jnp.float32))
        _validS = jnp.arange(128)[None, :] < _lenS[:, None]
        _validS2 = jnp.arange(77)[None, :] < _lenS2[:, None]
        _causal = jnp.tril(jnp.ones((128, 128), dtype=bool))
        mask_SxS2_ik0 = jnp.where(jnp.broadcast_to(_validS2[0:1, :], (128, 77)), 0, 1).astype(jnp.int32)
        return (x, ctx_1024, mask_SxS2_ik0)
    x, ctx_1024, mask_SxS2_ik0 = _rec_inputs()

    def _L0_xattn_setup():
        import jax, jax.numpy as jnp
        import numpy as np
        N_HEAD, D_MODEL, D_K, D_V, D_O = (16, 128, 64, 64, 128)
        B, S = (4, 256)
        key = jax.random.key(seed)
        ks = jax.random.split(key, 11)
        s = 0.02
        return {'q': jax.random.normal(ks[0], (B, S, D_MODEL), jnp.float32), 'k': jax.random.normal(ks[1], (B, S, D_MODEL), jnp.float32), 'v': jax.random.normal(ks[2], (B, S, D_MODEL), jnp.float32), 'Wq': jax.random.normal(ks[3], (D_MODEL, N_HEAD * D_K), jnp.float32) * s, 'bq': jnp.zeros((N_HEAD * D_K,), jnp.float32), 'Wk': jax.random.normal(ks[4], (D_MODEL, N_HEAD * D_K), jnp.float32) * s, 'bk': jnp.zeros((N_HEAD * D_K,), jnp.float32), 'Wv': jax.random.normal(ks[5], (D_MODEL, N_HEAD * D_V), jnp.float32) * s, 'bv': jnp.zeros((N_HEAD * D_V,), jnp.float32), 'Wo': jax.random.normal(ks[6], (N_HEAD * D_V, D_O), jnp.float32) * s, 'bo': jnp.zeros((D_O,), jnp.float32)}
    _L0_xattn_all = _L0_xattn_setup()
    _L0_xattn_in = {k: v for k, v in _L0_xattn_all.items() if k in ('Wq', 'bq', 'Wk', 'bk', 'Wv', 'bv', 'Wo', 'bo')}
    del _L0_xattn_all

    def _L0_ffn_setup():
        import jax, jax.numpy as jnp
        import numpy as np
        H = 128
        F = 512
        E = 8
        TOP_K = 2
        B, S = (1, 256)
        key = jax.random.key(seed)
        k0, k1, k2, k3 = jax.random.split(key, 4)
        hidden_states = jax.random.normal(k0, (B, S, H), dtype=jnp.float32)
        gate_w = jax.random.normal(k1, (E, H), dtype=jnp.float32) * 0.02
        gate_up_w = jax.random.normal(k2, (E, 2 * F, H), dtype=jnp.float32) * 0.02
        down_w = jax.random.normal(k3, (E, H, F), dtype=jnp.float32) * 0.02
        return {'hidden_states': hidden_states, 'gate_w': gate_w, 'gate_up_w': gate_up_w, 'down_w': down_w}
    _L0_ffn_all = _L0_ffn_setup()
    _L0_ffn_in = {k: v for k, v in _L0_ffn_all.items() if k in ('gate_w', 'gate_up_w', 'down_w')}
    del _L0_ffn_all

    def _L1_xattn_setup():
        import jax, jax.numpy as jnp
        import numpy as np
        D_MODEL = 128
        NUM_HEADS = 16
        D_K = D_MODEL // NUM_HEADS
        BATCH = 4
        SEQ = 256

        def _split_heads(x):
            b, s, _ = x.shape
            return x.reshape(b, s, NUM_HEADS, D_K).transpose(0, 2, 1, 3)
        key = jax.random.key(seed)
        ks = jax.random.split(key, 12)
        s = 0.02
        inp = {'Q': jax.random.normal(ks[0], (BATCH, SEQ, D_MODEL), jnp.float32), 'K': jax.random.normal(ks[1], (BATCH, SEQ, D_MODEL), jnp.float32), 'V': jax.random.normal(ks[2], (BATCH, SEQ, D_MODEL), jnp.float32), 'mask': jnp.tril(jnp.ones((SEQ, SEQ), jnp.int32)), 'Wq': jax.random.normal(ks[3], (D_MODEL, D_MODEL), jnp.float32) * s, 'bq': jax.random.normal(ks[4], (D_MODEL,), jnp.float32) * s, 'Wk': jax.random.normal(ks[5], (D_MODEL, D_MODEL), jnp.float32) * s, 'bk': jax.random.normal(ks[6], (D_MODEL,), jnp.float32) * s, 'Wv': jax.random.normal(ks[7], (D_MODEL, D_MODEL), jnp.float32) * s, 'bv': jax.random.normal(ks[8], (D_MODEL,), jnp.float32) * s, 'Wo': jax.random.normal(ks[9], (D_MODEL, D_MODEL), jnp.float32) * s, 'bo': jax.random.normal(ks[10], (D_MODEL,), jnp.float32) * s}
        return inp
    _L1_xattn_all = _L1_xattn_setup()
    _L1_xattn_in = {k: v for k, v in _L1_xattn_all.items() if k in ('Wq', 'bq', 'Wk', 'bk', 'Wv', 'bv', 'Wo', 'bo')}
    del _L1_xattn_all

    def _L1_ffn_setup():
        import jax, jax.numpy as jnp
        import numpy as np
        B, S, H = (2, 256, 128)
        N, F, SF, K = (16, 128, 512, 1)
        key = jax.random.key(seed)
        ks = jax.random.split(key, 7)
        std = 0.02
        return {'hidden_states': jax.random.normal(ks[0], (B, S, H), dtype=jnp.float32), 'router_w': jax.random.normal(ks[1], (N, H), dtype=jnp.float32) * std, 'gate_up_proj': jax.random.normal(ks[2], (N, H, 2 * F), dtype=jnp.float32) * std, 'down_proj': jax.random.normal(ks[3], (N, F, H), dtype=jnp.float32) * std, 'shared_gate_w': jax.random.normal(ks[4], (SF, H), dtype=jnp.float32) * std, 'shared_up_w': jax.random.normal(ks[5], (SF, H), dtype=jnp.float32) * std, 'shared_down_w': jax.random.normal(ks[6], (H, SF), dtype=jnp.float32) * std}
    _L1_ffn_all = _L1_ffn_setup()
    _L1_ffn_in = {k: v for k, v in _L1_ffn_all.items() if k in ('router_w', 'gate_up_proj', 'down_proj', 'shared_gate_w', 'shared_up_w', 'shared_down_w')}
    del _L1_ffn_all
    return {'x': x, 'ctx_1024': ctx_1024, 'mask_SxS2_ik0': mask_SxS2_ik0, 'L0_xattn_Wq': _L0_xattn_in['Wq'], 'L0_xattn_bq': _L0_xattn_in['bq'], 'L0_xattn_Wk': _L0_xattn_in['Wk'], 'L0_xattn_bk': _L0_xattn_in['bk'], 'L0_xattn_Wv': _L0_xattn_in['Wv'], 'L0_xattn_bv': _L0_xattn_in['bv'], 'L0_xattn_Wo': _L0_xattn_in['Wo'], 'L0_xattn_bo': _L0_xattn_in['bo'], 'L0_ffn_gate_w': _L0_ffn_in['gate_w'], 'L0_ffn_gate_up_w': _L0_ffn_in['gate_up_w'], 'L0_ffn_down_w': _L0_ffn_in['down_w'], 'L1_xattn_Wq': _L1_xattn_in['Wq'], 'L1_xattn_bq': _L1_xattn_in['bq'], 'L1_xattn_Wk': _L1_xattn_in['Wk'], 'L1_xattn_bk': _L1_xattn_in['bk'], 'L1_xattn_Wv': _L1_xattn_in['Wv'], 'L1_xattn_bv': _L1_xattn_in['bv'], 'L1_xattn_Wo': _L1_xattn_in['Wo'], 'L1_xattn_bo': _L1_xattn_in['bo'], 'L1_ffn_router_w': _L1_ffn_in['router_w'], 'L1_ffn_gate_up_proj': _L1_ffn_in['gate_up_proj'], 'L1_ffn_down_proj': _L1_ffn_in['down_proj'], 'L1_ffn_shared_gate_w': _L1_ffn_in['shared_gate_w'], 'L1_ffn_shared_up_w': _L1_ffn_in['shared_up_w'], 'L1_ffn_shared_down_w': _L1_ffn_in['shared_down_w']}

def reference(x, ctx_1024, mask_SxS2_ik0, L0_xattn_Wq, L0_xattn_bq, L0_xattn_Wk, L0_xattn_bk, L0_xattn_Wv, L0_xattn_bv, L0_xattn_Wo, L0_xattn_bo, L0_ffn_gate_w, L0_ffn_gate_up_w, L0_ffn_down_w, L1_xattn_Wq, L1_xattn_bq, L1_xattn_Wk, L1_xattn_bk, L1_xattn_Wv, L1_xattn_bv, L1_xattn_Wo, L1_xattn_bo, L1_ffn_router_w, L1_ffn_gate_up_proj, L1_ffn_down_proj, L1_ffn_shared_gate_w, L1_ffn_shared_up_w, L1_ffn_shared_down_w):
    import jax
    import jax.numpy as jnp

    def _L0_xattn_ref(q, k, v, Wq, bq, Wk, bk, Wv, bv, Wo, bo):
        import jax, jax.numpy as jnp
        import numpy as np
        N_HEAD, D_MODEL, D_K, D_V, D_O = (16, 128, 64, 64, 128)
        B, S = (4, 256)
        b, n_q, _ = q.shape
        qh = (q @ Wq + bq).reshape(b, -1, N_HEAD, D_K)
        kh = (k @ Wk + bk).reshape(b, -1, N_HEAD, D_K)
        vh = (v @ Wv + bv).reshape(b, -1, N_HEAD, D_V)
        scale = jnp.asarray(np.power(D_K, 0.5), qh.dtype)
        scores = jnp.einsum('bqhd,bkhd->bhqk', qh, kh) / scale
        attn = jax.nn.softmax(scores, axis=-1)
        out = jnp.einsum('bhqk,bkhd->bqhd', attn, vh).reshape(b, n_q, N_HEAD * D_V)
        return out @ Wo + bo

    def _L0_ffn_ref(hidden_states, gate_w, gate_up_w, down_w):
        import jax, jax.numpy as jnp
        import numpy as np
        H = 128
        F = 512
        E = 8
        TOP_K = 2
        B, S = (1, 256)
        b, s, h = hidden_states.shape
        x = hidden_states.reshape(-1, h)
        router_logits = x @ gate_w.T
        probs = jax.nn.softmax(router_logits.astype(jnp.float32), axis=-1)
        topw, sel = jax.lax.top_k(probs, TOP_K)
        topw = topw / jnp.sum(topw, axis=-1, keepdims=True)
        topw = topw.astype(x.dtype)
        combine = jnp.sum(jax.nn.one_hot(sel, E, dtype=x.dtype) * topw[..., None], axis=1)
        gu = jnp.einsum('th,efh->etf', x, gate_up_w)
        gate, up = (gu[..., :F], gu[..., F:])
        hact = up * jax.nn.gelu(gate, approximate=False)
        expert_out = jnp.einsum('etf,ehf->eth', hact, down_w)
        out = jnp.einsum('eth,te->th', expert_out, combine)
        return out.reshape(b, s, h)

    def _L1_xattn_ref(Q, K, V, mask, Wq, bq, Wk, bk, Wv, bv, Wo, bo):
        import jax, jax.numpy as jnp
        import numpy as np
        D_MODEL = 128
        NUM_HEADS = 16
        D_K = D_MODEL // NUM_HEADS
        BATCH = 4
        SEQ = 256

        def _split_heads(x):
            b, s, _ = x.shape
            return x.reshape(b, s, NUM_HEADS, D_K).transpose(0, 2, 1, 3)
        q = _split_heads(Q @ Wq.T + bq)
        k = _split_heads(K @ Wk.T + bk)
        v = _split_heads(V @ Wv.T + bv)
        scale = 1.0 / jnp.sqrt(jnp.asarray(D_K, q.dtype))
        scores = jnp.einsum('bhqd,bhkd->bhqk', q, k) * scale
        scores = jnp.where(mask == 0, jnp.asarray(-jnp.inf, scores.dtype), scores)
        attn = jax.nn.softmax(scores, axis=-1)
        out = jnp.einsum('bhqk,bhkd->bhqd', attn, v)
        b, h, s, dk = out.shape
        out = out.transpose(0, 2, 1, 3).reshape(b, s, h * dk)
        return out @ Wo.T + bo

    def _L1_ffn_ref(hidden_states, router_w, gate_up_proj, down_proj, shared_gate_w, shared_up_w, shared_down_w):
        import jax, jax.numpy as jnp
        import numpy as np
        B, S, H = (2, 256, 128)
        N, F, SF, K = (16, 128, 512, 1)
        b, s, h = hidden_states.shape
        hidden = hidden_states.reshape(-1, h)
        t = hidden.shape[0]
        logits = hidden @ router_w.T
        top_vals, top_idx = jax.lax.top_k(logits, K)
        scores = jnp.full_like(logits, -jnp.inf)
        scores = scores.at[jnp.arange(t)[:, None], top_idx].set(top_vals)
        scores = jax.nn.sigmoid(scores.astype(jnp.float32)).astype(hidden.dtype)
        routed_in = hidden[None, :, :] * scores.T[:, :, None]
        gate_up = jnp.einsum('nth,nhf->ntf', routed_in, gate_up_proj)
        gate, up = jnp.split(gate_up, 2, axis=-1)
        routed_out = jnp.einsum('ntf,nfh->nth', up * jax.nn.silu(gate), down_proj)
        expert_sum = routed_out.sum(axis=0)
        shared = jax.nn.silu(hidden @ shared_gate_w.T) * (hidden @ shared_up_w.T) @ shared_down_w.T
        return (shared + expert_sum).reshape(b, s, h)
    x = x + _L0_xattn_ref(_layernorm(x, axis=-1), ctx_1024, ctx_1024, L0_xattn_Wq, L0_xattn_bq, L0_xattn_Wk, L0_xattn_bk, L0_xattn_Wv, L0_xattn_bv, L0_xattn_Wo, L0_xattn_bo)
    x = x + _L0_ffn_ref(_layernorm(x, axis=-1), L0_ffn_gate_w, L0_ffn_gate_up_w, L0_ffn_down_w)
    x = x + _L1_xattn_ref(_layernorm(x, axis=-1), ctx_1024, ctx_1024, mask_SxS2_ik0, L1_xattn_Wq, L1_xattn_bq, L1_xattn_Wk, L1_xattn_bk, L1_xattn_Wv, L1_xattn_bv, L1_xattn_Wo, L1_xattn_bo)
    x = x + _L1_ffn_ref(_layernorm(x, axis=-1), L1_ffn_router_w, L1_ffn_gate_up_proj, L1_ffn_down_proj, L1_ffn_shared_gate_w, L1_ffn_shared_up_w, L1_ffn_shared_down_w)
    return x

_drawn_inputs = setup_inputs


def setup_inputs(seed=0):
    import zlib

    import numpy as np

    out = dict(_drawn_inputs(seed))
    spreads = {'L0_xattn_bq': (0.0, 0.8),
     'L0_xattn_bk': (0.0, 2.0),
     'L0_xattn_bv': (0.0, 0.1),
     'L0_xattn_bo': (0.0, 0.1)}
    factors = {'L0_xattn_Wq': 8.0,
     'L0_xattn_Wk': 8.0,
     'L0_ffn_gate_w': 7.666,
     'L0_ffn_gate_up_w': 6.661,
     'L0_ffn_down_w': 6.674,
     'L1_xattn_Wq': 8.0,
     'L1_xattn_bq': 30.179,
     'L1_xattn_Wk': 8.0,
     'L1_xattn_bk': 64.0,
     'L1_xattn_bv': 8.0,
     'L1_ffn_router_w': 8.0,
     'L1_ffn_gate_up_proj': 8.0,
     'L1_ffn_down_proj': 8.0,
     'L1_ffn_shared_gate_w': 4.886,
     'L1_ffn_shared_up_w': 4.861,
     'L1_ffn_shared_down_w': 4.869}
    for name, (base, spread) in spreads.items():
        noise = np.random.default_rng([zlib.crc32(name.encode()), seed]).standard_normal(out[name].shape)
        drawn = base * np.exp(spread * noise) if base else spread * noise
        out[name] = jnp.asarray(drawn.astype(out[name].dtype))
    for name, factor in factors.items():
        out[name] = (out[name] * factor).astype(out[name].dtype)
    return out
```

```python
from contextlib import ExitStack

import concourse.bass as bass
from concourse import mybir

F32 = mybir.dt.float32
I32 = mybir.dt.int32
ALU = mybir.AluOpType
ACT = mybir.ActivationFunctionType
AX_X = mybir.AxisListType.X

P = 128
NB = 32
SK = 77
D = 128
PAIRS = NB // 2
NH = 16
DK0 = 64
DK1 = D // NH
C0 = NH * DK0 // P
NE0 = 8
NE1 = 16
SF = 512
GROUP = 4
EPS = 1e-5
SMALL_LOADS = 11
RSQRT_MAGIC = float(0x5F3759DF)
BF16 = mybir.dt.bfloat16
TB = 3


def layernorm(dve, srcs, dsts, scratch, before_write=()):
    n = len(srcs)
    stats, mv, v, h, y, t = scratch
    for k in range(n):
        dve.bn_stats(stats[:, k, :], srcs[k])
    dve.drain()
    for k in range(n):
        dve.bn_aggr(mv[:, k, :], stats[:, k, :])
    dve.drain()
    dve.tensor_scalar(v[:, 0:n], mv[:, 0:n, 1], EPS, None, ALU.add)
    dve.drain()
    dve.tensor_scalar(h[:, 0:n], v[:, 0:n], -0.5, None, ALU.mult)
    dve.tensor_scalar(y[:, 0:n].bitcast(I32), v[:, 0:n].bitcast(I32), -0.5, RSQRT_MAGIC, ALU.mult, ALU.add)
    for _ in range(3):
        dve.drain()
        if n == 1:
            dve.scalar_tensor_tensor(out=t[:, 0:1], in0=y[:, 0:1], scalar=y[:, 0:1], in1=h[:, 0:1], op0=ALU.mult, op1=ALU.mult)
        else:
            dve.tensor_tensor(t[:, 0:n], y[:, 0:n], y[:, 0:n], ALU.mult)
            dve.drain()
            dve.tensor_tensor(t[:, 0:n], t[:, 0:n], h[:, 0:n], ALU.mult)
        dve.drain()
        dve.scalar_tensor_tensor(out=y[:, 0:n], in0=t[:, 0:n], scalar=1.5, in1=y[:, 0:n], op0=ALU.add, op1=ALU.mult)
    dve.drain()
    for wait in before_write:
        dve.wait_ge(*wait)
    for k in range(n):
        last = dve.tensor_scalar(dsts[k], srcs[k], mv[:, k, 0:1], y[:, k:k + 1], ALU.subtract, ALU.mult)
    return last


class Experts:

    def __init__(self, nc, ctx, name, ne, slots, width):
        self.ne, self.slots, self.width = ne, slots, width
        self.rows = slots * NB * P
        self.tiles = self.rows // P + ne
        assert self.tiles % 2 == 0 and self.rows < 2 ** 24

        def sem(what):
            return ctx.enter_context(nc.semaphore(f"{name}_{what}"))

        def sb(what, shape, dt=F32):
            return ctx.enter_context(nc.sbuf_tensor(f"{name}_{what}", shape, dt))

        self.step = sem("route_step")
        self.mask_ready, self.rank_ready, self.place_ready = sem("mask_ready"), sem("rank_ready"), sem("place_ready")
        self.hot_ready, self.hot_used = sem("hot_ready"), sem("hot_used")
        self.list_ready = sem("list_ready")
        self.place_col = sb("place_col", [P, slots * NB])
        self.place_tile = sb("place_tile", [P, slots * NB])
        self.row_list = sb("row_list", [P, self.tiles], I32)
        self.up_at = sb("up_at", [P, self.tiles], I32)
        self.down_at = sb("down_at", [P, self.tiles], I32)
        self.rows_loaded = [sem(f"rows_loaded{s}") for s in range(2)]
        self.rows_stored = [sem(f"rows_stored{s}") for s in range(2)]
        self.idx_in, self.idx_out = sem("idx_in"), sem("idx_out")
        self.tx_ready, self.tx_done = sem("tx_ready"), sem("tx_done")
        self.gate_ready, self.up_ready = sem("gate_ready"), sem("up_ready")
        self.act_done, self.h_done = sem("act_done"), sem("h_done")
        self.th_ready, self.th_done = sem("th_ready"), sem("th_done")
        self.y_ready, self.y_done = sem("y_ready"), sem("y_done")


def build(nc, a, out, stages="ABCD"):
    with ExitStack() as ctx:
        def sb(name, shape, dt=F32):
            return ctx.enter_context(nc.sbuf_tensor(name, shape, dt))

        def sem(name):
            return ctx.enter_context(nc.semaphore(name))

        ps = ctx.enter_context(nc.psum_tensor("ps", [P, 8, 512], F32))
        x_res = sb("x_res", [P, NB, D])
        ctxT = sb("ctxT", [P, NB * SK])
        ident = sb("ident", [P, P])
        w0 = sb("w0", [P, 4, C0 * P])
        wq0, wk0, wv0, wo0 = (w0[:, k, :] for k in range(4))
        bq0 = sb("bq0", [P, C0])
        bk0 = sb("bk0", [P, C0])
        bv0 = sb("bv0", [SK, C0 * P])
        bo0 = sb("bo0", [P, D])
        gw0 = sb("gw0", [P, NE0])
        cpair = sb("cpair", [P, 2 * SK])
        xh = sb("xh", [P, 2, D])
        xhT = sb("xhT", [P, 2 * P])
        qT = sb("qT", [P, C0, 2 * P])
        kbd = sb("kbd", [P, 2, C0, 2 * SK])
        vv = sb("vv", [SK, 2, C0 * P])
        sc = sb("sc", [P, 2, NH * SK])
        smax = sb("smax", [P, 2, NH])
        ssum = sb("ssum", [P, 2, NH])
        rinv = sb("rinv", [P, 2, NH])
        pT = sb("pT", [SK, 4, 4 * P])
        oT = sb("oT", [P, C0, P])
        xf = sb("xf", [P, 2, D])
        xfT = sb("xfT", [P, P])
        logits0 = sb("logits0", [P, NB, NE0])
        ln_a = (sb("lna_st", [P, 2, 6]), sb("lna_mv", [P, 2, 2]), *(sb(f"lna_{k}", [P, 2]) for k in "vhyt"))
        ln_f = (sb("lnf_st", [P, 1, 6]), sb("lnf_mv", [P, 1, 2]), *(sb(f"lnf_{k}", [P, 1]) for k in "vhyt"))

        xrows = nc.dram_tensor("xrows", (2 * NB * P, D), F32, kind="Internal").ap()
        yrows = nc.dram_tensor("yrows", (2 * NB * P, D), F32, kind="Internal").ap()
        L0 = Experts(nc, ctx, "l0", NE0, 2, 512)
        gu0 = sb("gu0", [P, NE0 * 1024])
        dn0 = sb("dn0", [P, NE0 * 512])
        consts = sb("consts", [P, 2 * P + 2 * 2 * NB])
        iota, tri = consts[:, 0:P], consts[:, P:2 * P]
        row_parts = consts[:, 2 * P:]
        ones = sb("ones", [P, P])
        hot_col = sb("hot_col", [P, 2, P], BF16)
        hot_tile = sb("hot_tile", [P, 2, 2, L0.tiles], BF16)
        idx_in = sb("idx_in_slot", [P, 2], I32)
        idx_out = sb("idx_out_slot", [P, 2], I32)
        topw = sb("topw", [P, 2, NB])
        rt_small = sb("rt_small", [P, 6, 2 * NB])
        rt_int = sb("rt_int", [P, 2 * NB], I32)
        ne_small = sb("ne_small", [P, 4, NH])
        w1 = sb("w1", [P, 4, D])
        wq1, wk1, wv1, wo1 = (w1[:, k, :] for k in range(4))
        b1 = sb("b1", [P, 2])
        bv1 = sb("bv1", [SK, D])
        bo1 = sb("bo1", [P, D])
        gw1 = sb("gw1", [P, NE1])
        mask_in = sb("mask_in", [P, SK], I32)
        mask_add = sb("mask_add", [P, SK])
        head_rows = sb("head_rows", [P, NH])
        q1T = qT[:, 0, :]
        k1T = qT[:, 1, 0:2 * SK]
        k1m = kbd[:, :, :, :].rearrange("p s c n -> p s (c n)")
        v1 = qT[0:SK, 2, 0:2 * P].rearrange("p (s d) -> p s d", s=2)
        v1m = gu0[0:SK, 0:2 * NH * D].rearrange("p (s h d) -> p s h d", s=2, h=NH)
        o1T = qT[:, 3, 0:P]
        xs = qT[:, 4, 0:2 * P].rearrange("p (s d) -> p s d", s=2)
        score = sb("score", [P, 4])
        logits1 = sb("logits1", [P, NB, NE1])
        xT_all = w0[:, :, :].rearrange("p a n -> p (a n)")
        gu1 = gu0[:, 4096:4096 + NE1 * 2 * D]
        dn1 = dn0[:, 0:NE1 * D]
        shg, shu, shd = (dn0[:, 2048 + k * SF:2048 + (k + 1) * SF] for k in range(3))
        shared_gate = sb("shared_gate", [P, 2, 512])
        shared_h = qT[:, :, :].rearrange("p c q -> p (c q)").rearrange("p (c n) -> p c n", c=4)
        xrows1 = nc.dram_tensor("xrows1", (NB * P, D), F32, kind="Internal").ap()
        yrows1 = nc.dram_tensor("yrows1", (NB * P, D), F32, kind="Internal").ap()
        L1 = Experts(nc, ctx, "l1", NE1, 1, D)
        xg = xh
        xgT = qT[:, 0:1, :].rearrange("p a (s q) -> p (a s) q", s=2)
        gact = qT[:, 2:6, :].rearrange("p (s a) n -> p s (a n)", s=2)
        hmul = kbd[:, 0, :, :].rearrange("p c n -> p (c n)")[:, 0:1024].rearrange("p (s n) -> p s n", s=2)
        hT = kbd[:, 1, :, :].rearrange("p c n -> p (c n)")[:, 0:1024].rearrange("p (s n) -> p s n", s=2)
        ysb = xf
        r_scratch = sc[:, :, :].rearrange("p s n -> p (s n)")
        hold_mask = sb("hold_mask", [P, NB * NH])
        yin = oT[:, 0:4, :].rearrange("p (s k) d -> p s k d", s=2)

        ld = {k: sem("ld_" + k) for k in ("x", "ctx", "id", "wq", "wk", "wv", "wo", "gw")}
        kz = sem("kbd_zeroed")
        cp_ready = sem("cpair_ready")
        xh_done, xt_ready, xt_done = sem("xh_done"), sem("xt_ready"), sem("xt_done")
        q_ready, q_done = sem("q_ready"), sem("q_done")
        k_ready, k_done = sem("k_ready"), sem("k_done")
        v_ready, v_done = sem("v_ready"), sem("v_done")
        s_ready, max_done, sub_done = sem("s_ready"), sem("max_done"), sem("sub_done")
        exp_done, sum_done, rinv_done, p_done = sem("exp_done"), sem("sum_done"), sem("rinv_done"), sem("p_done")
        t_ready, pt_done = sem("t_ready"), sem("pt_done")
        ot_ready, ot_done = sem("ot_ready"), sem("ot_done")
        wo_ready, wo_part, wo_done = sem("wo_ready"), sem("wo_part"), sem("wo_done")
        xf_done, xf_stored = sem("xf_done"), [sem("xf_stored0"), sem("xf_stored1")]
        rt_ready, rt_done = sem("rt_ready"), sem("rt_done")
        rl_ready, rl_done = sem("rl_ready"), sem("rl_done")
        out_done = sem("out_done")
        ld_moe0 = sem("ld_moe0")
        ones_set = sem("ones_set")
        order_set = sem("order_set")
        w_sub, w_exp = sem("w_sub"), sem("w_exp")
        yin_loaded = [sem(f"yin_loaded{s}") for s in range(2)]
        comb_part, comb_done = sem("comb_part"), sem("comb_done")
        ld_small, ld_moe1 = sem("ld_small"), sem("ld_moe1")
        mask_step, v1z = sem("mask_step"), sem("v1m_zeroed")
        c = {k: sem("c_" + k) for k in (
            "xh", "xt", "xt_moved", "q", "q_moved", "k", "k_moved", "k_masked", "v", "v_moved", "v_spread", "s", "masked", "max", "sub",
            "exp", "sum", "rinv", "p", "t", "pt", "ot", "ot_moved", "wo", "wo_part", "x", "xf", "rt", "rt_moved", "rt_kept", "rl",
            "rl_moved", "top", "top_exp", "score", "xs")}
        xs_stored = [sem("xs_stored0"), sem("xs_stored1")]
        sh = {k: sem("sh_" + k) for k in ("gate", "up", "act", "h", "down", "added")}
        y1_loaded, final_done = [sem(f"y1_loaded{g}") for g in range(NB // GROUP)], sem("final_done")

        block = ctx.enter_context(nc.Block())

        @block.sync
        def _(sp):
            x_tiles = a["x"].rearrange("b s d -> s b d")
            sp.dma_start(x_res[:, 0:4, :], x_tiles[:, 0:4, :]).then_inc(ld["x"], 16)
            sp.dma_start(ident[:, :], a["ident"]).then_inc(ld["id"], 16)
            sp.dma_start(wq0, a["wq0"]).then_inc(ld["wq"], 16)
            sp.dma_start(bq0[:, :], a["bq0"]).then_inc(ld["wq"], 16)
            sp.dma_start(ctxT[:, :], a["ctxT"]).then_inc(ld["ctx"], 16)
            sp.dma_start(wk0, a["wk0"]).then_inc(ld["wk"], 16)
            sp.dma_start(bk0[:, :], a["bk0"]).then_inc(ld["wk"], 16)
            sp.dma_start(wv0, a["wv0"]).then_inc(ld["wv"], 16)
            sp.dma_start(bv0[:, :], a["bv0"].rearrange("(o n) -> o n", o=1).broadcast_to([SK, C0 * P])).then_inc(ld["wv"], 16)
            sp.dma_start(x_res[:, 4:NB, :], x_tiles[:, 4:NB, :]).then_inc(ld["x"], 16)
            sp.dma_start(wo0.rearrange("p (c n) -> p c n", c=C0), a["wo0"].rearrange("(c p) n -> p c n", p=P)).then_inc(ld["wo"], 16)
            sp.dma_start(bo0[:, :], a["bo0"].rearrange("(o n) -> o n", o=1).broadcast_to([P, D])).then_inc(ld["wo"], 16)
            sp.dma_start(gw0[:, :], a["gw0"]).then_inc(ld["gw"], 16)
            sp.dma_start(consts[:, :], a["consts"]).then_inc(ld_small, 16)
            sp.dma_start(gu0[:, :], a["gu0"]).then_inc(ld_moe0, 16)
            sp.dma_start(dn0[:, :], a["dn0"]).then_inc(ld_moe0, 16)
            for k, name in enumerate(("wq1", "wk1", "wv1", "wo1")):
                sp.dma_start(w1[:, k, :], a[name]).then_inc(ld_small, 16)
            sp.dma_start(b1[:, :], a["b1"]).then_inc(ld_small, 16)
            sp.dma_start(bv1[:, :], a["bv1"].rearrange("(o n) -> o n", o=1).broadcast_to([SK, D])).then_inc(ld_small, 16)
            sp.dma_start(bo1[:, :], a["bo1"].rearrange("(o n) -> o n", o=1).broadcast_to([P, D])).then_inc(ld_small, 16)
            sp.dma_start(gw1[:, :], a["gw1"]).then_inc(ld_small, 16)
            sp.dma_start(head_rows[:, :], a["head_rows"]).then_inc(ld_small, 16)
            sp.dma_start(mask_in[:, :], a["mask"]).then_inc(ld_small, 16)
            with sp.Fori(0, PAIRS) as i:
                for s in range(2):
                    sp.wait_ge(xf_done, 2 * i + s + 1)
                    for slot in range(2):
                        sp.dma_start(xrows[bass.ds((2 * i + s) * P + slot * NB * P, P), :], xf[:, s, :]).then_inc(xf_stored[s], 16)
            for s in range(2):
                sp.wait_ge(L0.rows_stored[s], 16 * L0.tiles // 2)

            def load_expert_rows(i, s):
                for k in range(2):
                    sp.dma_start(yin[:, s, k, :], yrows[bass.ds((2 * i + s) * P + k * NB * P, P), :]).then_inc(yin_loaded[s], 16)

            def store_scaled_rows(i, s):
                sp.wait_ge(c["xs"], 2 * i + s + 1)
                sp.dma_start(xrows1[bass.ds((2 * i + s) * P, P), :], xs[:, s, :]).then_inc(xs_stored[s], 16)

            for s in range(2):
                load_expert_rows(0, s)
            sp.dma_start(gu1, a["gu1"]).then_inc(ld_moe1, 16)
            sp.dma_start(dn1, a["dn1"]).then_inc(ld_moe1, 16)
            for weights, name in ((shg, "shg"), (shu, "shu"), (shd, "shd")):
                sp.dma_start(weights, a[name]).then_inc(ld_moe1, 16)
            for s in range(2):
                sp.wait_ge(comb_done, s + 1)
                load_expert_rows(1, s)
            with sp.Fori(2, PAIRS) as i:
                for s in range(2):
                    sp.wait_ge(comb_done, 2 * i + s - 1)
                    load_expert_rows(i, s)
                for s in range(2):
                    store_scaled_rows(i - 2, s)
            for i in (PAIRS - 2, PAIRS - 1):
                for s in range(2):
                    store_scaled_rows(i, s)

            for s in range(2):
                sp.wait_ge(L1.rows_stored[s], 16 * L1.tiles // 2)
            y1 = yrows1.rearrange("(b p) d -> p b d", p=P)
            for g in range(NB // GROUP):
                sp.dma_start(gu0[:, g * GROUP * D:(g + 1) * GROUP * D].rearrange("p (b d) -> p b d", d=D),
                             y1[:, g * GROUP:(g + 1) * GROUP, :]).then_inc(y1_loaded[g], 16)
            sp.wait_ge(final_done, NB // GROUP)
            sp.dma_start(out.rearrange("b s d -> s b d"), x_res[:, :, :]).then_inc(out_done, 16)
            sp.wait_ge(out_done, 16)

        @block.gpsimd
        def _(pool):
            nc.gpsimd.memset(kbd[:, :, :, :], 0.0).then_inc(kz, 1)
            nc.gpsimd.memset(ones[:, :], 1.0).then_inc(ones_set, 1)

            def copy_contexts(i):
                nc.gpsimd.tensor_copy(cpair[:, :], ctxT[:, bass.ds(i * 2 * SK, 2 * SK)]).then_inc(cp_ready, 1)

            def normalise(b, s):
                pool.wait_ge(rinv_done, b + 1)
                p = sc[:, s, :].rearrange("p (h k) -> p h k", h=NH)
                nc.gpsimd.tensor_tensor(p, p, rinv[:, s, :].unsqueeze(2).broadcast_to([P, NH, SK]), ALU.mult).then_inc(p_done, 1)

            pool.wait_ge(ld["ctx"], 16)
            copy_contexts(0)
            normalise(0, 0)
            with pool.Fori(0, PAIRS - 1) as i:
                pool.wait_ge(v_ready, 4 * i + 4)
                copy_contexts(i + 1)
                normalise(2 * i + 1, 1)
                normalise(2 * i + 2, 0)
            normalise(NB - 1, 1)

            def move_rows(L, xrows, yrows):
                def fetch(i, s):
                    j = 2 * i + s
                    count = j + 1 if isinstance(j, int) else pool.to_reg(j + 1)
                    nc.gpsimd.tensor_copy(idx_in[:, s:s + 1], L.row_list[:, bass.ds(j, 1)]).then_inc(L.idx_in, 1)
                    pool.wait_ge(L.list_ready, 1)
                    pool.wait_ge(L.idx_in, count)
                    nc.gpsimd.indirect_dma_start(xg[:, s, :], None, xrows[0:L.rows, :], bass.IndirectOffsetOnAxis(idx_in[:, s:s + 1], 0),
                                                 bounds_check=bound, oob_is_err=False).then_inc(L.rows_loaded[s], 16)

                def store(i, s):
                    j = 2 * i + s
                    nc.gpsimd.tensor_copy(idx_out[:, s:s + 1], L.row_list[:, bass.ds(j, 1)]).then_inc(L.idx_out, 1)
                    pool.wait_ge(L.list_ready, 1)
                    pool.wait_ge(L.y_done, j + 1)
                    pool.wait_ge(L.idx_out, j + 1)
                    nc.gpsimd.indirect_dma_start(yrows[0:L.rows, :], bass.IndirectOffsetOnAxis(idx_out[:, s:s + 1], 0), ysb[:, s, :], None,
                                                 bounds_check=bound, oob_is_err=False).then_inc(L.rows_stored[s], 16)

                def body(i, first=False, last=False):
                    for s in range(2):
                        if not last:
                            pool.wait_ge(L.tx_ready, 2 * i + s + 1)
                            fetch(i + 1, s)
                        if not first:
                            pool.wait_ge(L.rows_stored[s], 16 * i)
                        store(i, s)

                pool.wait_ge(L.list_ready, 1)
                bound = pool.to_reg(L.rows - 1)
                fetch(0, 0)
                fetch(0, 1)
                body(0, first=True)
                with pool.Fori(1, L.tiles // 2 - 1) as i:
                    body(i)
                body(L.tiles // 2 - 1, last=True)

            for s in range(2):
                pool.wait_ge(xf_stored[s], 32 * PAIRS)
            move_rows(L0, xrows, yrows)

            def copy_contexts1(i):
                nc.gpsimd.tensor_copy(cpair[:, :], ctxT[:, bass.ds(i * 2 * SK, 2 * SK)]).then_inc(cp_ready, 1)

            def mask_keys(b, i, s):
                pool.wait_ge(c["k_moved"], i + 1)
                if not (isinstance(b, int) and b < 2):
                    pool.wait_ge(c["s"], b - 1)
                nc.gpsimd.tensor_tensor(k1m[:, s, :].rearrange("p (h k) -> p h k", h=NH),
                                        k1T[:, s * SK:(s + 1) * SK].unsqueeze(1).broadcast_to([P, NH, SK]),
                                        head_rows[:, :].unsqueeze(2).broadcast_to([P, NH, SK]), ALU.mult).then_inc(c["k_masked"], 1)

            def spread_values(b, s):
                if not (isinstance(b, int) and b < 2):
                    pool.wait_ge(c["ot"], b - 1)
                pool.wait_ge(c["v_moved"], b + 1)
                flat = v1m[:, s, :, :].rearrange("p h d -> p (h d)")
                blocks = bass.AP(flat.tensor, flat.offset, [list(flat.ap[0]), [D + DK1, NH], [1, DK1]])
                nc.gpsimd.tensor_tensor(blocks, v1[:, s, :].rearrange("p (h d) -> p h d", h=NH),
                                        bv1[:, :].rearrange("p (h d) -> p h d", h=NH), ALU.add).then_inc(c["v_spread"], 1)

            def normalise1(b, s):
                pool.wait_ge(c["rinv"], b + 1)
                p = sc[:, s, :].rearrange("p (h k) -> p h k", h=NH)
                nc.gpsimd.tensor_tensor(p, p, rinv[:, s, :].unsqueeze(2).broadcast_to([P, NH, SK]), ALU.mult).then_inc(c["p"], 1)

            def keep_xT(b):
                pool.wait_ge(c["rt_moved"], b + 1)
                nc.gpsimd.tensor_copy(xT_all[:, bass.ds(b * P, P)], xfT[:, :]).then_inc(c["rt_kept"], 1)

            nc.gpsimd.memset(v1m[:, :, :, :], 0.0).then_inc(v1z, 1)
            pool.wait_ge(v1z, 1)
            copy_contexts1(0)
            pool.wait_ge(ld_small, 16 * SMALL_LOADS)
            mask_keys(0, 0, 0)
            spread_values(0, 0)
            mask_keys(1, 0, 1)
            normalise1(0, 0)
            spread_values(1, 1)

            def body1(i, first=False, last=False):
                b0, b1 = 2 * i, 2 * i + 1
                if not first:
                    keep_xT(b0 - 1)
                if not last:
                    pool.wait_ge(c["v"], 2 * i + 2)
                    copy_contexts1(i + 1)
                normalise1(b1, 1)
                if not last:
                    mask_keys(b0 + 2, i + 1, 0)
                    spread_values(b0 + 2, 0)
                keep_xT(b0)
                if not last:
                    mask_keys(b1 + 2, i + 1, 1)
                    normalise1(b0 + 2, 0)
                    spread_values(b1 + 2, 1)
                else:
                    keep_xT(b1)

            body1(0, first=True)
            with pool.Fori(1, PAIRS - 1) as i:
                body1(i)
            body1(PAIRS - 1, last=True)

            for s in range(2):
                pool.wait_ge(xs_stored[s], 16 * PAIRS)
            move_rows(L1, xrows1, yrows1)

        @block.scalar
        def _(act):
            def move_xT(i):
                act.wait_ge(xt_ready, i + 1)
                nc.scalar.copy(xhT[:, :], ps[:, 5, 0:2 * P]).then_inc(xt_done, 1)

            def move_q(i):
                for n, bank in enumerate((6, 7, 5, 6)):
                    act.wait_ge(q_ready, 4 * i + n + 1)
                    for c in (2 * n, 2 * n + 1):
                        last = nc.scalar.activation(qT[:, c, :], ps[:, bank, (c % 2) * 256:(c % 2) * 256 + 256],
                                                    ACT.Identity, bias=bq0[:, c:c + 1])
                    last.then_inc(q_done, 1)

            def move_pT(b, g):
                act.wait_ge(t_ready, 4 * b + g + 1)
                nc.scalar.copy(pT[:, g, :], ps[0:SK, TB + g % 2, :]).then_inc(pt_done, 1)

            def exponentials(b, s):
                act.wait_ge(sub_done, b + 1)
                nc.scalar.activation(sc[:, s, :], sc[:, s, :], ACT.Exp, scale=float(DK0) ** -0.5).then_inc(exp_done, 1)

            def move_xfT(b, bank):
                act.wait_ge(rt_ready, b + 1)
                if not (isinstance(b, int) and b == 0):
                    act.wait_ge(rl_ready, b)
                nc.scalar.copy(xfT[:, :], ps[:, bank, 0:P]).then_inc(rt_done, 1)

            def move_logits(b):
                act.wait_ge(rl_ready, b + 1)
                nc.scalar.copy(logits0[:, bass.ds(b, 1), :].rearrange("p o e -> p (o e)"), ps[:, 7, 0:NE0]).then_inc(rl_done, 1)

            def body(i, first=False, last=False):
                b0, b1 = 2 * i, 2 * i + 1
                if not first:
                    move_xfT(b0 - 1, 7)
                act.wait_ge(ot_ready, 2 * b0) if not first else None
                move_pT(b0, 0)
                move_pT(b0, 1)
                move_pT(b0, 2)
                exponentials(b1, 1)
                if not first:
                    move_logits(b0 - 1)
                move_pT(b0, 3)
                if not last:
                    act.wait_ge(s_ready, b1 + 1)
                    if not first:
                        pass
                    move_xT(i + 1)
                    move_q(i + 1)
                move_xfT(b0, 6)
                act.wait_ge(ot_ready, 2 * b1)
                move_pT(b1, 0)
                move_pT(b1, 1)
                move_pT(b1, 2)
                if not last:
                    exponentials(b1 + 1, 0)
                move_logits(b0)
                move_pT(b1, 3)
                if last:
                    move_xfT(b1, 7)
                    move_logits(b1)

            act.wait_ge(ld["wq"], 32)
            move_xT(0)
            move_q(0)
            exponentials(0, 0)
            body(0, first=True)
            with act.Fori(1, PAIRS - 1) as i:
                body(i)
            body(PAIRS - 1, last=True)

            def experts(L, func, up_bank):
                def move_xT(j, s):
                    act.wait_ge(L.tx_ready, j + 1)
                    nc.scalar.copy(xgT[:, s, :], ps[:, 4, 0:P]).then_inc(L.tx_done, 1)

                def gate(j, s):
                    act.wait_ge(L.gate_ready, j + 1)
                    nc.scalar.activation(gact[:, s, 0:L.width], ps[:, 2 * s, 0:L.width], func).then_inc(L.act_done, 1)

                def move_y(i, s, first=False):
                    j = 2 * i + s
                    act.wait_ge(L.y_ready, j + 1)
                    if not first:
                        act.wait_ge(L.rows_stored[s], 16 * i)
                    nc.scalar.copy(ysb[:, s, :], ps[:, 7, 0:D]).then_inc(L.y_done, 1)

                def body(i, first=False, second=False, last=False):
                    j = 2 * i
                    if not first:
                        act.wait_ge(L.up_ready, j)
                    move_xT(j + 1, 1)
                    if not first:
                        act.wait_ge(L.h_done, j - 1)
                    gate(j, 0)
                    if not first:
                        move_y(i - 1, 1, first=second)
                    if not last:
                        act.wait_ge(L.up_ready, j + 1)
                        move_xT(j + 2, 0)
                    if not first:
                        act.wait_ge(L.h_done, j)
                    gate(j + 1, 1)
                    move_y(i, 0, first=first)

                move_xT(0, 0)
                body(0, first=True)
                body(1, second=True)
                with act.Fori(2, L.tiles // 2 - 1) as i:
                    body(i)
                body(L.tiles // 2 - 1, last=True)
                move_y(L.tiles // 2 - 1, 1)

            act.wait_ge(w_sub, 1)
            nc.scalar.activation(rt_small[:, 3, 0:NB], rt_small[:, 3, 0:NB], ACT.Exp)
            nc.scalar.activation(r_scratch[:, 512:512 + NB * NE0], r_scratch[:, 512:512 + NB * NE0], ACT.Exp).then_inc(w_exp, 1)
            experts(L0, ACT.Gelu, None)

            def move1(ready, count, dst, src, done, bias=None):
                act.wait_ge(ready, count)
                if bias is None:
                    nc.scalar.copy(dst, src).then_inc(done, 1)
                else:
                    nc.scalar.activation(dst, src, ACT.Identity, bias=bias).then_inc(done, 1)

            def move_xT1(i):
                move1(c["xt"], i + 1, xhT[:, :], ps[:, 6, 0:2 * P], c["xt_moved"])

            def move_qk1(i):
                move1(c["q"], i + 1, q1T, ps[:, 5, 0:2 * P], c["q_moved"], b1[:, 0:1])
                if not (isinstance(i, int) and i == 0):
                    act.wait_ge(c["k_masked"], 2 * i)
                move1(c["k"], i + 1, k1T, ps[:, 7, 0:2 * SK], c["k_moved"], b1[:, 1:2])

            def move_v1(b, s, bank):
                if not (isinstance(b, int) and b < 2):
                    act.wait_ge(c["v_spread"], b - 1)
                move1(c["v"], b + 1, v1[:, s, :], ps[0:SK, bank, 0:D], c["v_moved"])

            def move_pT1(b, g):
                move1(c["t"], 4 * b + g + 1, pT[:, g, :], ps[0:SK, TB + g % 2, :], c["pt"])

            def exponentials1(b, s):
                act.wait_ge(c["sub"], b + 1)
                nc.scalar.activation(sc[:, s, :], sc[:, s, :], ACT.Exp, scale=float(DK1) ** -0.5).then_inc(c["exp"], 1)

            def move_oT1(b, bank):
                if not (isinstance(b, int) and b == 0):
                    act.wait_ge(c["wo"], b)
                move1(c["ot"], b + 1, o1T, ps[:, bank, 0:P], c["ot_moved"])

            def move_xfT1(b, bank):
                if not (isinstance(b, int) and b == 0):
                    act.wait_ge(c["rl"], b)
                    act.wait_ge(c["rt_kept"], b)
                move1(c["rt"], b + 1, xfT[:, :], ps[:, bank, 0:P], c["rt_moved"])

            def move_logits1(b):
                move1(c["rl"], b + 1, logits1[:, bass.ds(b, 1), :].rearrange("p o e -> p (o e)"), ps[:, 7, 0:NE1], c["rl_moved"])

            def top_exponential(b):
                act.wait_ge(c["top"], b + 1)
                nc.scalar.activation(score[:, 1:2], score[:, 0:1], ACT.Exp, scale=-1.0).then_inc(c["top_exp"], 1)

            def body1(i, first=False, last=False):
                b0, b1_ = 2 * i, 2 * i + 1
                if not first:
                    move_xfT1(b0 - 1, 7)
                    act.wait_ge(c["ot"], b0)
                move_pT1(b0, 0)
                move_pT1(b0, 1)
                move_pT1(b0, 2)
                exponentials1(b1_, 1)
                if not first:
                    move_logits1(b0 - 1)
                move_pT1(b0, 3)
                move_oT1(b0, 5)
                if not first:
                    top_exponential(b0 - 1)
                if not last:
                    move_xT1(i + 1)
                    act.wait_ge(c["s"], b1_ + 1)
                    move_qk1(i + 1)
                    move_v1(b0 + 2, 0, 6)
                move_xfT1(b0, 5)
                act.wait_ge(c["ot"], b1_)
                move_pT1(b1_, 0)
                move_pT1(b1_, 1)
                move_pT1(b1_, 2)
                if not last:
                    exponentials1(b1_ + 1, 0)
                move_logits1(b0)
                move_pT1(b1_, 3)
                move_oT1(b1_, 6)
                top_exponential(b0)
                if not last:
                    move_v1(b1_ + 2, 1, 5)
                if last:
                    move_xfT1(b1_, 7)
                    move_logits1(b1_)
                    top_exponential(b1_)

            move_xT1(0)
            move_qk1(0)
            move_v1(0, 0, 6)
            exponentials1(0, 0)
            move_v1(1, 1, 5)
            body1(0, first=True)
            with act.Fori(1, PAIRS - 1) as i:
                body1(i)
            body1(PAIRS - 1, last=True)

            experts(L1, ACT.Silu, None)

            def shared(g):
                for k in range(4):
                    s = k % 2
                    act.wait_ge(sh["gate"], 4 * g + k + 1)
                    if not (isinstance(g, int) and g == 0 and k < 2):
                        act.wait_ge(sh["h"], 4 * g + k - 1)
                    nc.scalar.activation(shared_gate[:, s, :], ps[:, 2 * s, :], ACT.Silu).then_inc(sh["act"], 1)

            shared(0)
            with act.Fori(1, NB // GROUP) as g:
                shared(g)

        @block.vector
        def _(dve):
            def norm_inputs(i):
                free = () if isinstance(i, int) and i == 0 else ((xt_ready, i),)
                rows = [x_res[:, bass.ds(2 * i + s, 1), :].rearrange("p o d -> p (o d)") for s in range(2)]
                layernorm(dve, rows, [xh[:, s, :] for s in range(2)], ln_a, free).then_inc(xh_done, 1)

            def move_k(i):
                for n, (c0, c1, bank) in enumerate(((0, 3, 7), (3, 6, 5), (6, 8, 6))):
                    dve.wait_ge(k_ready, 3 * i + n + 1)
                    m = c1 - c0
                    for half in range(2):
                        lo = 64 * half
                        for s in range(2):
                            src = ps[lo:lo + 64, bank, 0:m * 2 * SK].rearrange("p (c s k) -> p c s k", c=m, s=2)[:, :, s, :]
                            last = nc.vector.tensor_tensor(kbd[lo:lo + 64, s, c0:c1, half * SK:(half + 1) * SK], src,
                                                           bk0[lo:lo + 64, c0:c1].unsqueeze(2).broadcast_to([64, m, SK]), ALU.add)
                    last.then_inc(k_done, 1)

            def move_v(b, s, banks):
                if not (isinstance(b, int) and b < 2):
                    dve.wait_ge(ot_ready, 2 * b - 2)
                for n, bank in enumerate(banks):
                    dve.wait_ge(v_ready, 2 * b + n + 1)
                    nc.vector.tensor_tensor(vv[:, s, n * 512:(n + 1) * 512], ps[0:SK, bank, :],
                                            bv0[:, n * 512:(n + 1) * 512], ALU.add).then_inc(v_done, 1)

            def subtract_max(b, s):
                dve.wait_ge(s_ready, b + 1)
                if not (isinstance(b, int) and b < 2):
                    dve.wait_ge(t_ready, 4 * b - 4)
                lo = ps[:, 0:2, 0:6 * SK].rearrange("p a (h k) -> p a h k", h=6)
                hi = ps[:, 2, 0:4 * SK].rearrange("p (h k) -> p h k", h=4)
                nc.vector.tensor_reduce(smax[:, s, 0:12].rearrange("p (a h) -> p a h", a=2), lo, AX_X, ALU.max)
                nc.vector.tensor_reduce(smax[:, s, 12:16], hi, AX_X, ALU.max).then_inc(max_done, 1)
                dve.wait_ge(max_done, b + 1)
                d = sc[:, s, :].rearrange("p (h k) -> p h k", h=NH)
                for k in range(2):
                    nc.vector.tensor_tensor(d[:, 6 * k:6 * k + 6, :], ps[:, k, 0:6 * SK].rearrange("p (h k) -> p h k", h=6),
                                            smax[:, s, 6 * k:6 * k + 6].unsqueeze(2).broadcast_to([P, 6, SK]), ALU.subtract)
                nc.vector.tensor_tensor(d[:, 12:16, :], hi, smax[:, s, 12:16].unsqueeze(2).broadcast_to([P, 4, SK]),
                                        ALU.subtract).then_inc(sub_done, 1)

            def sums(b, s):
                dve.wait_ge(exp_done, b + 1)
                nc.vector.tensor_reduce(ssum[:, s, :], sc[:, s, :].rearrange("p (h k) -> p h k", h=NH), AX_X, ALU.add).then_inc(sum_done, 1)
                dve.wait_ge(sum_done, b + 1)
                nc.vector.reciprocal(rinv[:, s, :], ssum[:, s, :]).then_inc(rinv_done, 1)

            def move_oT(b, half):
                dve.wait_ge(ot_ready, 2 * b + half + 1)
                if not (isinstance(b, int) and b == 0) and half == 0:
                    dve.wait_ge(wo_ready, b)
                nc.vector.tensor_copy(oT[:, 4 * half:4 * half + 4, :].rearrange("p c q -> p (c q)"), ps[:, 5 + half, :]).then_inc(ot_done, 1)

            def residual_and_norm(i, s):
                b = 2 * i + s
                row = x_res[:, bass.ds(b, 1), :].rearrange("p o d -> p (o d)")
                nc.vector.tensor_tensor(row, row, bo0[:, :], ALU.add).then_inc(wo_part, 1)
                dve.wait_ge(wo_ready, b + 1)
                dve.wait_ge(wo_part, b + 1)
                nc.vector.tensor_tensor(row, ps[:, 7, 0:D], row, ALU.add).then_inc(wo_done, 1)
                dve.drain()
                free = () if isinstance(i, int) and i == 0 else ((xf_stored[s], 32 * i), (rt_ready, b - 1))
                layernorm(dve, [row], [xf[:, s, :]], ln_f, free).then_inc(xf_done, 1)

            def body(i, last=False):
                b0, b1 = 2 * i, 2 * i + 1
                subtract_max(b1, 1)
                if not last:
                    norm_inputs(i + 1)
                move_oT(b0, 0)
                sums(b1, 1)
                move_oT(b0, 1)
                residual_and_norm(i, 0)
                if not last:
                    move_k(i + 1)
                    move_v(b0 + 2, 0, (7, 5))
                    subtract_max(b0 + 2, 0)
                move_oT(b1, 0)
                if not last:
                    sums(b0 + 2, 0)
                move_oT(b1, 1)
                residual_and_norm(i, 1)
                if not last:
                    move_v(b1 + 2, 1, (5, 6))

            dve.wait_ge(ld["x"], 32)
            norm_inputs(0)
            dve.wait_ge(ld["wk"], 32)
            dve.wait_ge(kz, 1)
            move_k(0)
            dve.wait_ge(ld["wv"], 32)
            move_v(0, 0, (7, 5))
            subtract_max(0, 0)
            sums(0, 0)
            move_v(1, 1, (5, 6))
            dve.wait_ge(ld["wo"], 32)
            body(0)
            with dve.Fori(1, PAIRS - 1) as i:
                body(i)
            body(PAIRS - 1, last=True)

            def route(L, logits, first_expert):
                ne, nt, n = L.ne, L.tiles, NB * L.ne
                count = [0]

                def then(ins):
                    count[0] += 1
                    ins.then_inc(L.step, 1)
                    dve.wait_ge(L.step, count[0])

                def grid(k):
                    return r_scratch[:, k * n:(k + 1) * n].rearrange("p (b e) -> p b e", e=ne)

                def over_e(v):
                    return v.unsqueeze(2).broadcast_to([P, NB, ne])

                def over_b(v):
                    return v.unsqueeze(1).broadcast_to([P, NB, ne])

                masks, eq, rest = [grid(k) for k in range(L.slots)], grid(L.slots), grid(L.slots + 1)
                incl, pos = grid(L.slots + 2), grid(L.slots + 1)
                order = over_b(first_expert)
                tops = [rt_small[:, k, 0:NB] for k in range(2)]
                cand = rt_small[:, 2, 0:NB]
                left = logits
                for k in range(L.slots):
                    then(nc.vector.tensor_reduce(tops[k], left, AX_X, ALU.max))
                    then(nc.vector.tensor_tensor(eq, left, over_e(tops[k]), ALU.is_equal))
                    then(nc.vector.tensor_tensor(eq, eq, order, ALU.mult))
                    then(nc.vector.tensor_reduce(cand, eq, AX_X, ALU.max))
                    then(nc.vector.tensor_tensor(masks[k], order, over_e(cand), ALU.is_equal))
                    if k + 1 < L.slots:
                        then(nc.vector.scalar_tensor_tensor(out=rest, in0=masks[k], scalar=-3e38, in1=left, op0=ALU.mult, op1=ALU.add))
                        left = rest
                both = masks[0]
                if L.slots == 2:
                    then(nc.vector.tensor_tensor(eq, masks[0], masks[1], ALU.add))
                    both = eq
                nc.vector.tensor_copy(hold_mask[:, 0:n].rearrange("p (b e) -> p b e", e=ne), both).then_inc(L.mask_ready, 1)
                if L.slots == 2:
                    then(nc.vector.tensor_tensor(rt_small[:, 3, 0:NB], tops[1], tops[0], ALU.subtract))
                    nc.vector.tensor_tensor(rest, logits, over_e(tops[0]), ALU.subtract).then_inc(w_sub, 1)
                    dve.wait_ge(w_exp, 1)
                    e2, z, p2 = rt_small[:, 3, 0:NB], rt_small[:, 4, 0:NB], rt_small[:, 5, 0:NB]
                    then(nc.vector.tensor_reduce(z, rest, AX_X, ALU.add))
                    then(nc.vector.reciprocal(z, z))
                    then(nc.vector.tensor_tensor(p2, e2, z, ALU.mult))
                    then(nc.vector.tensor_tensor(e2, z, p2, ALU.add))
                    then(nc.vector.reciprocal(e2, e2))
                    then(nc.vector.tensor_tensor(topw[:, 0, :], z, e2, ALU.mult))
                    then(nc.vector.tensor_tensor(topw[:, 1, :], p2, e2, ALU.mult))
                dve.wait_ge(L.rank_ready, 2)
                totals = ps[:, 1, 0:n].rearrange("p (b e) -> p b e", e=ne)
                for e in range(ne):
                    last = nc.vector.tensor_tensor_scan(incl[:, :, e], ones[:, 0:NB], totals[:, :, e], 0.0, ALU.mult, ALU.add)
                then(last)
                fill, begin, end = (ne_small[:, k, 0:ne] for k in range(3))
                then(nc.vector.tensor_tensor(pos, incl, totals, ALU.subtract))
                then(nc.vector.tensor_scalar(rt_int[:, 0:ne], incl[:, NB - 1, :], (P - 1) / 2, 1.0 / P, ALU.add, ALU.mult))
                then(nc.vector.tensor_copy(fill, rt_int[:, 0:ne]))
                then(nc.vector.tensor_tensor_scan(end, ones[:, 0:ne], fill, 0.0, ALU.mult, ALU.add))
                then(nc.vector.tensor_tensor(begin, end, fill, ALU.subtract))
                then(nc.vector.tensor_scalar(begin, begin, float(P), None, ALU.mult))
                then(nc.vector.tensor_tensor(pos, pos, over_b(begin), ALU.add))
                then(nc.vector.tensor_tensor(pos, pos, ps[:, 0, 0:n].rearrange("p (b e) -> p b e", e=ne), ALU.add))
                m = L.slots * NB
                at = rt_small[:, 4, 0:m]
                for k in range(L.slots):
                    then(nc.vector.tensor_tensor(eq, masks[k], pos, ALU.mult))
                    then(nc.vector.tensor_reduce(at[:, k * NB:(k + 1) * NB], eq, AX_X, ALU.add))
                then(nc.vector.tensor_scalar(rt_int[:, 0:m], at, -(P - 1) / 2, 1.0 / P, ALU.add, ALU.mult))
                then(nc.vector.tensor_copy(L.place_tile[:, 0:m], rt_int[:, 0:m]))
                then(nc.vector.scalar_tensor_tensor(out=L.place_col[:, 0:m], in0=L.place_tile[:, 0:m], scalar=-float(P), in1=at,
                                                    op0=ALU.mult, op1=ALU.add))
                past = r_scratch[:, 0:nt * ne].rearrange("p (j e) -> p j e", e=ne)
                then(nc.vector.tensor_tensor(past, iota[:, 0:nt].unsqueeze(2).broadcast_to([P, nt, ne]),
                                             end.unsqueeze(1).broadcast_to([P, nt, ne]), ALU.is_ge))
                expert = r_scratch[:, 1024:1024 + nt]
                then(nc.vector.tensor_reduce(expert, past, AX_X, ALU.add))
                then(nc.vector.tensor_scalar(L.up_at[:, :], expert, float(ne - 1), float(2 * L.width), ALU.min, ALU.mult))
                nc.vector.tensor_scalar(L.down_at[:, :], expert, float(ne - 1), float(L.width), ALU.min, ALU.mult).then_inc(L.place_ready, 1)

            def one_hot(L):
                dve.wait_ge(L.place_ready, 1)

                def hot(i, s):
                    n = 2 * i + s
                    nc.vector.tensor_scalar(hot_col[:, s, :], iota, L.place_col[:, bass.ds(n, 1)], None, ALU.is_equal)
                    nc.vector.scalar_tensor_tensor(out=hot_tile[:, s, :, 0:L.tiles],
                                                   in0=iota[:, 0:L.tiles].unsqueeze(1).broadcast_to([P, 2, L.tiles]),
                                                   scalar=L.place_tile[:, bass.ds(n, 1)],
                                                   in1=row_parts[:, bass.ds(2 * n, 2)].unsqueeze(2).broadcast_to([P, 2, L.tiles]),
                                                   op0=ALU.is_equal, op1=ALU.mult).then_inc(L.hot_ready, 1)

                hot(0, 0)
                hot(0, 1)
                with dve.Fori(1, L.slots * NB // 2) as i:
                    for s in range(2):
                        dve.wait_ge(L.hot_used, 2 * i + s - 1)
                        hot(i, s)
                dve.wait_ge(L.hot_used, L.slots * NB)
                t = r_scratch[:, 0:L.tiles]
                nc.vector.tensor_scalar(t, ps[:, 2, 0:L.tiles], 64.0, -1.0, ALU.mult, ALU.add).then_inc(L.place_ready, 1)
                dve.wait_ge(L.place_ready, 2)
                nc.vector.tensor_tensor(L.row_list[:, :], t, ps[:, 2, L.tiles:2 * L.tiles], ALU.add).then_inc(L.list_ready, 1)

            def experts(L):
                def multiply(j, s):
                    dve.wait_ge(L.act_done, j + 1)
                    dve.wait_ge(L.up_ready, j + 1)
                    nc.vector.tensor_tensor(hmul[:, s, 0:L.width], ps[:, 2 * s + 1, 0:L.width], gact[:, s, 0:L.width], ALU.mult).then_inc(L.h_done, 1)

                def move_hT(j, s):
                    dve.wait_ge(L.th_ready, j + 1)
                    nc.vector.tensor_copy(hT[:, s, 0:L.width], ps[:, 5 + s, 0:L.width]).then_inc(L.th_done, 1)

                def body(i, first=False, second=False):
                    j = 2 * i
                    if not first:
                        if not second:
                            dve.wait_ge(L.y_ready, j - 2)
                        move_hT(j - 1, 1)
                        dve.wait_ge(L.th_ready, j - 1)
                    multiply(j, 0)
                    if not first:
                        dve.wait_ge(L.y_ready, j - 1)
                    move_hT(j, 0)
                    if not first:
                        dve.wait_ge(L.th_ready, j)
                    multiply(j + 1, 1)

                body(0, first=True)
                body(1, second=True)
                with dve.Fori(2, L.tiles // 2) as i:
                    body(i)
                dve.wait_ge(L.y_ready, L.tiles - 2)
                move_hT(L.tiles - 1, 1)

            dve.wait_ge(rl_done, NB)
            dve.wait_ge(ld_small, 16 * SMALL_LOADS)
            dve.wait_ge(ones_set, 1)
            nc.vector.tensor_scalar(ne_small[:, 3, :], iota[:, 0:NH], -1.0, float(NE0), ALU.mult, ALU.add).then_inc(order_set, 1)
            dve.wait_ge(order_set, 1)
            dve.wait_ge(t_ready, 4 * NB)
            route(L0, logits0[:, :, :], ne_small[:, 3, 0:NE0])
            one_hot(L0)
            experts(L0)

            def combine(i, s):
                b = 2 * i + s
                row = x_res[:, bass.ds(b, 1), :].rearrange("p o d -> p (o d)")
                dve.wait_ge(yin_loaded[s], 32 * (i + 1))
                nc.vector.scalar_tensor_tensor(out=row, in0=yin[:, s, 0, :], scalar=topw[:, 0, bass.ds(b, 1)], in1=row,
                                               op0=ALU.mult, op1=ALU.add).then_inc(comb_part, 1)
                dve.wait_ge(comb_part, b + 1)
                nc.vector.scalar_tensor_tensor(out=row, in0=yin[:, s, 1, :], scalar=topw[:, 1, bass.ds(b, 1)], in1=row,
                                               op0=ALU.mult, op1=ALU.add).then_inc(comb_done, 1)

            def row_of(b):
                return x_res[:, bass.ds(b, 1), :].rearrange("p o d -> p (o d)")

            def norm_inputs1(i):
                for s in range(2):
                    combine(i, s)
                dve.drain()
                free = () if isinstance(i, int) and i == 0 else ((c["xt"], i),)
                layernorm(dve, [row_of(2 * i + s) for s in range(2)], [xh[:, s, :] for s in range(2)], ln_a, free).then_inc(c["xh"], 1)

            def subtract_max1(b, s):
                dve.wait_ge(c["s"], b + 1)
                if not (isinstance(b, int) and b < 2):
                    dve.wait_ge(c["t"], 4 * b - 4)
                d = sc[:, s, :].rearrange("p (h k) -> p h k", h=NH)
                for k, n in enumerate((6, 6, 4)):
                    last = nc.vector.tensor_tensor(d[:, 6 * k:6 * k + n, :], ps[:, k, 0:n * SK].rearrange("p (h k) -> p h k", h=n),
                                                   mask_add[:, :].unsqueeze(1).broadcast_to([P, n, SK]), ALU.add)
                last.then_inc(c["masked"], 1)
                dve.wait_ge(c["masked"], b + 1)
                nc.vector.tensor_reduce(smax[:, s, :], d, AX_X, ALU.max).then_inc(c["max"], 1)
                dve.wait_ge(c["max"], b + 1)
                nc.vector.tensor_tensor(d, d, smax[:, s, :].unsqueeze(2).broadcast_to([P, NH, SK]), ALU.subtract).then_inc(c["sub"], 1)

            def sums1(b, s):
                dve.wait_ge(c["exp"], b + 1)
                nc.vector.tensor_reduce(ssum[:, s, :], sc[:, s, :].rearrange("p (h k) -> p h k", h=NH), AX_X, ALU.add).then_inc(c["sum"], 1)
                dve.wait_ge(c["sum"], b + 1)
                nc.vector.reciprocal(rinv[:, s, :], ssum[:, s, :]).then_inc(c["rinv"], 1)

            def residual_and_norm1(i, s):
                b = 2 * i + s
                row = row_of(b)
                nc.vector.tensor_tensor(row, row, bo1[:, :], ALU.add).then_inc(c["wo_part"], 1)
                dve.wait_ge(c["wo"], b + 1)
                dve.wait_ge(c["wo_part"], b + 1)
                nc.vector.tensor_tensor(row, ps[:, 7, 0:D], row, ALU.add).then_inc(c["x"], 1)
                dve.drain()
                free = () if isinstance(i, int) and i == 0 else ((c["rt"], b - 1),)
                layernorm(dve, [row], [xf[:, s, :]], ln_f, free).then_inc(c["xf"], 1)

            def top_logit(b):
                dve.wait_ge(c["rl_moved"], b + 1)
                nc.vector.tensor_reduce(score[:, 0:1], logits1[:, bass.ds(b, 1), :].rearrange("p o e -> p (o e)"), AX_X, ALU.max).then_inc(c["top"], 1)

            def scale_rows(i, s):
                b = 2 * i + s
                dve.wait_ge(c["top_exp"], b + 1)
                nc.vector.tensor_scalar(score[:, 2:3], score[:, 1:2], 1.0, None, ALU.add).then_inc(c["score"], 1)
                dve.wait_ge(c["score"], 2 * b + 1)
                nc.vector.reciprocal(score[:, 3:4], score[:, 2:3]).then_inc(c["score"], 1)
                dve.wait_ge(c["score"], 2 * b + 2)
                if not (isinstance(i, int) and i == 0):
                    dve.wait_ge(xs_stored[s], 16 * i)
                nc.vector.tensor_scalar(xs[:, s, :], xf[:, s, :], score[:, 3:4], None, ALU.mult).then_inc(c["xs"], 1)

            def body1(i, first=False, last=False):
                b0, b1_ = 2 * i, 2 * i + 1
                subtract_max1(b1_, 1)
                if not last:
                    norm_inputs1(i + 1)
                sums1(b1_, 1)
                if not first:
                    top_logit(b0 - 1)
                    scale_rows(i - 1, 1)
                residual_and_norm1(i, 0)
                if not last:
                    subtract_max1(b0 + 2, 0)
                    sums1(b0 + 2, 0)
                top_logit(b0)
                scale_rows(i, 0)
                residual_and_norm1(i, 1)
                if last:
                    top_logit(b1_)
                    scale_rows(i, 1)

            dve.wait_ge(ld_small, 16 * SMALL_LOADS)
            nc.vector.tensor_scalar(mask_add[:, :], mask_in[:, :], 0.0, -3e38, ALU.is_equal, ALU.mult).then_inc(mask_step, 1)
            dve.wait_ge(mask_step, 1)
            none_left = rt_small[:, 0, 0:1]
            nc.vector.tensor_reduce(none_left, mask_add[:, :], AX_X, ALU.max).then_inc(mask_step, 1)
            dve.wait_ge(mask_step, 2)
            nc.vector.tensor_scalar(none_left, none_left, 10.0, None, ALU.mult).then_inc(mask_step, 1)
            dve.wait_ge(mask_step, 3)
            nc.vector.tensor_tensor(none_left, none_left, none_left, ALU.subtract).then_inc(mask_step, 1)
            dve.wait_ge(mask_step, 4)
            nc.vector.tensor_scalar(bo1[:, :], bo1[:, :], none_left, None, ALU.add).then_inc(mask_step, 1)
            dve.wait_ge(mask_step, 5)
            norm_inputs1(0)
            dve.wait_ge(ld_small, 16 * SMALL_LOADS)
            subtract_max1(0, 0)
            sums1(0, 0)
            body1(0, first=True)
            with dve.Fori(1, PAIRS - 1) as i:
                body1(i)
            body1(PAIRS - 1, last=True)

            dve.wait_ge(c["rl_moved"], NB)
            dve.wait_ge(c["t"], 4 * NB)
            nc.vector.tensor_scalar(ne_small[:, 3, :], iota[:, 0:NH], -1.0, float(NE1), ALU.mult, ALU.add).then_inc(order_set, 1)
            dve.wait_ge(order_set, 2)
            route(L1, logits1[:, :, :], ne_small[:, 3, 0:NE1])
            one_hot(L1)
            experts(L1)

            def shared(g):
                for k in range(4):
                    s = k % 2
                    dve.wait_ge(sh["act"], 4 * g + k + 1)
                    dve.wait_ge(sh["up"], 4 * g + k + 1)
                    if k == 0 and not (isinstance(g, int) and g == 0):
                        dve.wait_ge(sh["down"], g)
                    nc.vector.tensor_tensor(shared_h[:, k, :], ps[:, 2 * s + 1, :], shared_gate[:, s, :], ALU.mult).then_inc(sh["h"], 1)
                dve.wait_ge(sh["down"], g + 1)
                rows = x_res[:, bass.ds(GROUP * g, GROUP), :]
                nc.vector.tensor_tensor(rows, ps[:, 4, :].rearrange("p (b d) -> p b d", d=D), rows, ALU.add).then_inc(sh["added"], 1)

            shared(0)
            with dve.Fori(1, NB // GROUP) as g:
                shared(g)
            for g in range(NB // GROUP):
                dve.wait_ge(y1_loaded[g], 16)
                dve.wait_ge(sh["added"], g + 1)
                rows = x_res[:, g * GROUP:(g + 1) * GROUP, :]
                nc.vector.tensor_tensor(rows, rows, gu0[:, g * GROUP * D:(g + 1) * GROUP * D].rearrange("p (b d) -> p b d", d=D),
                                        ALU.add).then_inc(final_done, 1)

        @block.tensor
        def _(pe):
            def transpose_inputs(i):
                pe.wait_ge(xh_done, i + 1)
                for s in range(2):
                    mm = nc.tensor.transpose(ps[:, 5, s * P:(s + 1) * P], xh[:, s, :], ident[:, :])
                mm.then_inc(xt_ready, 1)

            def queries(i, bank_free):
                pe.wait_ge(xt_done, i + 1)
                for n, bank in enumerate((6, 7, 5, 6)):
                    if bank_free[n]:
                        pe.wait_ge(*bank_free[n])
                    for c in (2 * n, 2 * n + 1):
                        mm = nc.tensor.matmul(ps[:, bank, (c % 2) * 256:(c % 2) * 256 + 256], wq0[:, c * P:(c + 1) * P], xhT[:, :],
                                              start=True, stop=True)
                    mm.then_inc(q_ready, 1)

            def keys(i):
                pe.wait_ge(cp_ready, i + 1)
                for n, (c0, c1, bank) in enumerate(((0, 3, 7), (3, 6, 5), (6, 8, 6))):
                    pe.wait_ge(q_done, 4 * i + n + 2)
                    for c in range(c0, c1):
                        o = (c - c0) * 2 * SK
                        mm = nc.tensor.matmul(ps[:, bank, o:o + 2 * SK], wk0[:, c * P:(c + 1) * P], cpair[:, :], start=True, stop=True)
                    mm.then_inc(k_ready, 1)

            def values(s, banks, bank_free):
                for n, bank in enumerate(banks):
                    pe.wait_ge(*bank_free[n])
                    nc.tensor.matmul(ps[0:SK, bank, :], cpair[:, s * SK:(s + 1) * SK], wv0[:, n * 512:(n + 1) * 512],
                                     start=True, stop=True).then_inc(v_ready, 1)

            def scores(b, s, i):
                pe.wait_ge(q_done, 4 * i + 4)
                pe.wait_ge(k_done, 3 * i + 3)
                if not (isinstance(b, int) and b == 0):
                    pe.wait_ge(sub_done, b)
                for c in range(C0):
                    o = (c % 3) * 2 * SK
                    mm = nc.tensor.matmul(ps[:, c // 3, o:o + 2 * SK], qT[:, c, s * P:(s + 1) * P], kbd[:, s, c, :], start=True, stop=True)
                mm.then_inc(s_ready, 1)

            def transpose_probs(b, s, g):
                if g == 0:
                    pe.wait_ge(p_done, b + 1)
                if g >= 2:
                    pe.wait_ge(pt_done, 4 * b + g - 1)
                for k in range(4):
                    h = 4 * g + k
                    mm = nc.tensor.transpose(ps[0:SK, TB + g % 2, k * P:(k + 1) * P], sc[:, s, h * SK:(h + 1) * SK], ident[:, :])
                mm.then_inc(t_ready, 1)

            def weigh_values(b, s, g):
                pe.wait_ge(pt_done, 4 * b + g + 1)
                for k in range(4):
                    h = 4 * g + k
                    lo = 64 * (h % 2)
                    o = ((h // 2) % 4) * P
                    mm = nc.tensor.matmul(ps[lo:lo + 64, 5 + g // 2, o:o + P], vv[:, s, h * DK0:(h + 1) * DK0],
                                          pT[:, g, k * P:(k + 1) * P], start=True, stop=True)
                if g % 2:
                    mm.then_inc(ot_ready, 1)

            def attend(b, s, bank5_free, bank6_free, router):
                transpose_probs(b, s, 0)
                transpose_probs(b, s, 1)
                pe.wait_ge(v_done, 2 * b + 2)
                pe.wait_ge(*bank5_free)
                weigh_values(b, s, 0)
                transpose_probs(b, s, 2)
                weigh_values(b, s, 1)
                if router is not None:
                    router_logits(router)
                transpose_probs(b, s, 3)
                pe.wait_ge(*bank6_free)
                weigh_values(b, s, 2)
                weigh_values(b, s, 3)

            def project(b, bank_free):
                if bank_free:
                    pe.wait_ge(*bank_free)
                pe.wait_ge(ot_done, 2 * b + 2)
                for c in range(C0):
                    mm = nc.tensor.matmul(ps[:, 7, 0:D], oT[:, c, :], wo0[:, c * D:(c + 1) * D], start=c == 0, stop=c == C0 - 1)
                mm.then_inc(wo_ready, 1)

            def transpose_rows(b, s, bank, bank_free):
                pe.wait_ge(*bank_free)
                pe.wait_ge(xf_done, b + 1)
                nc.tensor.transpose(ps[:, bank, 0:P], xf[:, s, :], ident[:, :]).then_inc(rt_ready, 1)

            def router_logits(b):
                pe.wait_ge(rt_done, b + 1)
                nc.tensor.matmul(ps[:, 7, 0:NE0], xfT[:, :], gw0[:, :], start=True, stop=True).then_inc(rl_ready, 1)

            def body(i, first=False, last=False):
                b0, b1 = 2 * i, 2 * i + 1
                scores(b1, 1, i)
                if not first:
                    transpose_rows(b0 - 1, 1, 7, (wo_done, b0))
                attend(b0, 0, (v_done, 2 * b1 + 1), (v_done, 2 * b1 + 2), None if first else b0 - 1)
                project(b0, (rl_done, b0) if not first else None)
                if not last:
                    pe.wait_ge(ot_done, 2 * b0 + 1)
                    transpose_inputs(i + 1)
                    queries(i + 1, [(ot_done, 2 * b0 + 2), (wo_done, b0 + 1), None, (q_done, 4 * i + 5)])
                    keys(i + 1)
                    values(0, (7, 5), [(k_done, 3 * i + 4), (k_done, 3 * i + 5)])
                    transpose_rows(b0, 0, 6, (k_done, 3 * i + 6))
                    scores(b0 + 2, 0, i + 1)
                    attend(b1, 1, (v_done, 2 * b0 + 6), (rt_done, b0 + 1), b0)
                else:
                    transpose_rows(b0, 0, 6, (ot_done, 2 * b0 + 2))
                    attend(b1, 1, (ot_done, 2 * b0 + 1), (rt_done, b0 + 1), b0)
                project(b1, (rl_done, b1))
                if not last:
                    values(1, (5, 6), [(ot_done, 2 * b1 + 1), (ot_done, 2 * b1 + 2)])
                else:
                    transpose_rows(b1, 1, 7, (wo_done, b1 + 1))
                    router_logits(b1)

            pe.wait_ge(ld["id"], 16)
            transpose_inputs(0)
            pe.wait_ge(ld["wq"], 32)
            queries(0, [None, None, None, (q_done, 1)])
            pe.wait_ge(ld["wk"], 32)
            keys(0)
            pe.wait_ge(ld["wv"], 32)
            values(0, (7, 5), [(k_done, 1), (k_done, 2)])
            scores(0, 0, 0)
            values(1, (5, 6), [(v_done, 2), (k_done, 3)])
            pe.wait_ge(ld["wo"], 32)
            pe.wait_ge(ld["gw"], 16)
            body(0, first=True)
            with pe.Fori(1, PAIRS - 1) as i:
                body(i)
            body(PAIRS - 1, last=True)

            def ranks(L):
                pe.wait_ge(L.mask_ready, 1)
                n = NB * L.ne
                nc.tensor.matmul(ps[:, 0, 0:n], tri, hold_mask[:, 0:n], start=True, stop=True).then_inc(L.rank_ready, 1)
                nc.tensor.matmul(ps[:, 1, 0:n], ones[:, :], hold_mask[:, 0:n], start=True, stop=True).then_inc(L.rank_ready, 1)

            def row_numbers(L):
                last_n = L.slots * NB - 1

                def add(i, s):
                    n = 2 * i + s
                    pe.wait_ge(L.hot_ready, n + 1)
                    const = isinstance(n, int)
                    nc.tensor.matmul(ps[:, 2, 0:2 * L.tiles], hot_col[:, s, :],
                                     hot_tile[:, s, :, :].rearrange("p a j -> p (a j)")[:, 0:2 * L.tiles] if L.tiles == hot_tile.shape[3]
                                     else hot_tile[:, s, :, 0:L.tiles],
                                     start=const and n == 0, stop=const and n == last_n).then_inc(L.hot_used, 1)

                add(0, 0)
                add(0, 1)
                with pe.Fori(1, L.slots * NB // 2 - 1) as i:
                    add(i, 0)
                    add(i, 1)
                add(L.slots * NB // 2 - 1, 0)
                add(L.slots * NB // 2 - 1, 1)

            def experts(L, up_w, down_w):
                w, chunks = L.width, L.width // P

                def turn_rows(i, s):
                    pe.wait_ge(L.rows_loaded[s], 16 * (i + 1))
                    nc.tensor.transpose(ps[:, 4, 0:P], xg[:, s, :], ident[:, :]).then_inc(L.tx_ready, 1)

                def gate_or_up(j, s, half, ready):
                    at = pe.value_load(L.up_at[0:1, bass.ds(j, 1)], min_val=0, max_val=(L.ne - 1) * 2 * w)
                    nc.tensor.matmul(ps[:, 2 * s + half, 0:w], xgT[:, s, :], up_w[:, bass.ds(at + half * w, w)],
                                     start=True, stop=True).then_inc(ready, 1)

                def turn_hidden(j, s):
                    pe.wait_ge(L.h_done, j + 1)
                    for c in range(chunks):
                        mm = nc.tensor.transpose(ps[:, 5 + s, c * P:(c + 1) * P], hmul[:, s, c * P:(c + 1) * P], ident[:, :])
                    mm.then_inc(L.th_ready, 1)

                def down(j, s):
                    at = pe.value_load(L.down_at[0:1, bass.ds(j, 1)], min_val=0, max_val=(L.ne - 1) * w)
                    pe.wait_ge(L.th_done, j + 1)
                    for c in range(chunks):
                        mm = nc.tensor.matmul(ps[:, 7, 0:D], hT[:, s, c * P:(c + 1) * P], down_w[:, bass.ds(at + c * D, D)],
                                              start=c == 0, stop=c == chunks - 1)
                    mm.then_inc(L.y_ready, 1)

                def tile(i, s, first=False, second=False, last=False):
                    j = 2 * i + s
                    if not last:
                        pe.wait_ge(L.tx_done, j + 1)
                        turn_rows(i + s, 1 - s)
                    else:
                        pe.wait_ge(L.tx_done, j + 1)
                    if not (first or second):
                        pe.wait_ge(L.h_done, j - 1)
                    gate_or_up(j, s, 0, L.gate_ready)
                    if not first:
                        if not (second or isinstance(j, int) and j < 4):
                            pe.wait_ge(L.th_done, j - 2)
                        turn_hidden(j - 1, 1 - s)
                    gate_or_up(j, s, 1, L.up_ready)
                    if not first:
                        if not second:
                            pe.wait_ge(L.y_done, j - 1)
                        down(j - 1, 1 - s)

                turn_rows(0, 0)
                tile(0, 0, first=True)
                tile(0, 1, second=True)
                tile(1, 0)
                tile(1, 1)
                with pe.Fori(2, L.tiles // 2 - 1) as i:
                    tile(i, 0)
                    tile(i, 1)
                tile(L.tiles // 2 - 1, 0)
                tile(L.tiles // 2 - 1, 1, last=True)
                turn_hidden(L.tiles - 1, 1)
                pe.wait_ge(L.y_done, L.tiles - 1)
                down(L.tiles - 1, 1)

            pe.wait_ge(ld_small, 16 * SMALL_LOADS)
            pe.wait_ge(ones_set, 1)
            ranks(L0)
            row_numbers(L0)
            pe.wait_ge(ld_moe0, 32)
            experts(L0, gu0, dn0)

            def transpose_inputs1(i):
                pe.wait_ge(c["xh"], i + 1)
                for s in range(2):
                    mm = nc.tensor.transpose(ps[:, 6, s * P:(s + 1) * P], xh[:, s, :], ident[:, :])
                mm.then_inc(c["xt"], 1)

            def queries_and_keys1(i):
                pe.wait_ge(c["xt_moved"], i + 1)
                nc.tensor.matmul(ps[:, 5, 0:2 * P], wq1, xhT[:, :], start=True, stop=True).then_inc(c["q"], 1)
                pe.wait_ge(cp_ready, PAIRS + i + 1)
                nc.tensor.matmul(ps[:, 7, 0:2 * SK], wk1, cpair[:, :], start=True, stop=True).then_inc(c["k"], 1)

            def values1(s, bank, bank_free):
                pe.wait_ge(*bank_free)
                nc.tensor.matmul(ps[0:SK, bank, 0:D], cpair[:, s * SK:(s + 1) * SK], wv1, start=True, stop=True).then_inc(c["v"], 1)

            def scores1(b, s):
                pe.wait_ge(c["k_masked"], b + 1)
                if not (isinstance(b, int) and b == 0):
                    pe.wait_ge(c["masked"], b)
                for k, n in enumerate((6, 6, 4)):
                    mm = nc.tensor.matmul(ps[:, k, 0:n * SK], q1T[:, s * P:(s + 1) * P], k1m[:, s, 6 * k * SK:(6 * k + n) * SK],
                                          start=True, stop=True)
                mm.then_inc(c["s"], 1)

            def transpose_probs1(b, s, g):
                if g == 0:
                    pe.wait_ge(c["p"], b + 1)
                if g >= 2:
                    pe.wait_ge(c["pt"], 4 * b + g - 1)
                for k in range(4):
                    h = 4 * g + k
                    mm = nc.tensor.transpose(ps[0:SK, TB + g % 2, k * P:(k + 1) * P], sc[:, s, h * SK:(h + 1) * SK], ident[:, :])
                mm.then_inc(c["t"], 1)

            def weigh_values1(b, s, g, bank):
                pe.wait_ge(c["pt"], 4 * b + g + 1)
                for k in range(4):
                    h = 4 * g + k
                    mm = nc.tensor.matmul(ps[:, bank, 0:P], v1m[:, s, h, :], pT[:, g, k * P:(k + 1) * P], start=h == 0, stop=h == NH - 1)
                if g == 3:
                    mm.then_inc(c["ot"], 1)

            def attend1(b, s, bank, bank_free, router):
                transpose_probs1(b, s, 0)
                transpose_probs1(b, s, 1)
                pe.wait_ge(c["v_spread"], b + 1)
                pe.wait_ge(*bank_free)
                weigh_values1(b, s, 0, bank)
                transpose_probs1(b, s, 2)
                weigh_values1(b, s, 1, bank)
                if router is not None:
                    router_logits1(router)
                transpose_probs1(b, s, 3)
                weigh_values1(b, s, 2, bank)
                weigh_values1(b, s, 3, bank)

            def project1(b, bank_free):
                if bank_free:
                    pe.wait_ge(*bank_free)
                pe.wait_ge(c["ot_moved"], b + 1)
                nc.tensor.matmul(ps[:, 7, 0:D], o1T, wo1, start=True, stop=True).then_inc(c["wo"], 1)

            def transpose_rows1(b, s, bank, bank_free):
                pe.wait_ge(*bank_free)
                pe.wait_ge(c["xf"], b + 1)
                nc.tensor.transpose(ps[:, bank, 0:P], xf[:, s, :], ident[:, :]).then_inc(c["rt"], 1)

            def router_logits1(b):
                pe.wait_ge(c["rt_moved"], b + 1)
                nc.tensor.matmul(ps[:, 7, 0:NE1], xfT[:, :], gw1[:, :], start=True, stop=True).then_inc(c["rl"], 1)

            def body1(i, first=False, last=False):
                b0, b1_ = 2 * i, 2 * i + 1
                scores1(b1_, 1)
                if not first:
                    transpose_rows1(b0 - 1, 1, 7, (c["x"], b0))
                attend1(b0, 0, 5, (c["v_moved"], b1_ + 1), None if first else b0 - 1)
                project1(b0, (c["rl_moved"], b0) if not first else (c["k_moved"], 1))
                if not last:
                    transpose_inputs1(i + 1)
                    pe.wait_ge(c["ot_moved"], b0 + 1)
                    pe.wait_ge(c["x"], b0 + 1)
                    queries_and_keys1(i + 1)
                    values1(0, 6, (c["xt_moved"], i + 2))
                    transpose_rows1(b0, 0, 5, (c["q_moved"], i + 2))
                    pe.wait_ge(c["q_moved"], i + 2)
                    scores1(b0 + 2, 0)
                    pe.wait_ge(c["k_moved"], i + 2)
                    attend1(b1_, 1, 6, (c["v_moved"], b0 + 3), b0)
                else:
                    transpose_rows1(b0, 0, 5, (c["ot_moved"], b0 + 1))
                    pe.wait_ge(c["x"], b0 + 1)
                    attend1(b1_, 1, 6, (c["ot_moved"], b0 + 1), b0)
                project1(b1_, (c["rl_moved"], b1_))
                if not last:
                    values1(1, 5, (c["rt_moved"], b0 + 1))
                else:
                    transpose_rows1(b1_, 1, 7, (c["x"], b1_ + 1))
                    router_logits1(b1_)

            pe.wait_ge(L0.y_done, L0.tiles)
            pe.wait_ge(L0.th_done, L0.tiles)
            pe.wait_ge(ld_small, 16 * SMALL_LOADS)
            transpose_inputs1(0)
            queries_and_keys1(0)
            values1(0, 6, (c["xt_moved"], 1))
            pe.wait_ge(c["q_moved"], 1)
            scores1(0, 0)
            values1(1, 5, (c["q_moved"], 1))
            body1(0, first=True)
            with pe.Fori(1, PAIRS - 1) as i:
                body1(i)
            body1(PAIRS - 1, last=True)

            ranks(L1)
            row_numbers(L1)
            pe.wait_ge(ld_moe1, 16 * 5)
            experts(L1, gu1, dn1)

            def shared(g):
                rows = xT_all[:, bass.ds(g * GROUP * P, GROUP * P)]
                for k in range(4):
                    s = k % 2
                    if not (isinstance(g, int) and g == 0 and k < 2):
                        pe.wait_ge(sh["h"], 4 * g + k - 1)
                    nc.tensor.matmul(ps[:, 2 * s, :], shg[:, k * P:(k + 1) * P], rows, start=True, stop=True).then_inc(sh["gate"], 1)
                    nc.tensor.matmul(ps[:, 2 * s + 1, :], shu[:, k * P:(k + 1) * P], rows, start=True, stop=True).then_inc(sh["up"], 1)
                pe.wait_ge(sh["h"], 4 * g + 4)
                if not (isinstance(g, int) and g == 0):
                    pe.wait_ge(sh["added"], g)
                for t in range(GROUP):
                    for k in range(4):
                        mm = nc.tensor.matmul(ps[:, 4, t * D:(t + 1) * D], shared_h[:, k, t * P:(t + 1) * P], shd[:, k * D:(k + 1) * D],
                                              start=k == 0, stop=k == 3)
                mm.then_inc(sh["down"], 1)

            pe.wait_ge(L1.h_done, L1.tiles)
            pe.wait_ge(c["rt_kept"], NB)
            shared(0)
            with pe.Fori(1, NB // GROUP) as g:
                shared(g)


def lay_out(inputs):
    import numpy as np
    d = {k: np.asarray(v) for k, v in inputs.items()}
    iota = np.broadcast_to(np.arange(P, dtype=np.float32), (P, P))
    number = 1 + np.arange(P)[:, None] + P * np.arange(2 * NB)[None, :]
    consts = np.concatenate([iota, np.triu(np.ones((P, P), np.float32), 1), np.stack([number // 64, number % 64], 2).reshape(P, -1)], 1).astype(np.float32)
    turned = lambda w: np.ascontiguousarray(np.asarray(w).T)
    up = np.asarray(d["L0_ffn_gate_up_w"])
    down = np.asarray(d["L0_ffn_down_w"])
    return {
        "x": d["x"], "ctxT": np.ascontiguousarray(d["ctx_1024"].reshape(-1, D).T), "ident": np.eye(P, dtype=np.float32),
        "wq0": d["L0_xattn_Wq"], "bq0": np.ascontiguousarray(d["L0_xattn_bq"].reshape(C0, P).T),
        "wk0": d["L0_xattn_Wk"], "bk0": np.ascontiguousarray(d["L0_xattn_bk"].reshape(C0, P).T),
        "wv0": d["L0_xattn_Wv"], "bv0": d["L0_xattn_bv"], "wo0": d["L0_xattn_Wo"], "bo0": d["L0_xattn_bo"],
        "gw0": np.ascontiguousarray(d["L0_ffn_gate_w"].T), "consts": consts,
        "wq1": turned(d["L1_xattn_Wq"]), "wk1": turned(d["L1_xattn_Wk"]), "wv1": turned(d["L1_xattn_Wv"]),
        "wo1": turned(d["L1_xattn_Wo"]), "b1": np.ascontiguousarray(np.stack([d["L1_xattn_bq"], d["L1_xattn_bk"]], 1)),
        "bv1": d["L1_xattn_bv"], "bo1": d["L1_xattn_bo"], "gw1": turned(d["L1_ffn_router_w"]),
        "head_rows": np.repeat(np.eye(NH, dtype=np.float32), DK1, axis=0), "mask": d["mask_SxS2_ik0"],
        "gu1": np.ascontiguousarray(np.asarray(d["L1_ffn_gate_up_proj"]).transpose(1, 0, 2).reshape(D, -1)),
        "dn1": np.ascontiguousarray(np.asarray(d["L1_ffn_down_proj"]).transpose(1, 0, 2).reshape(P, -1)),
        "shg": turned(d["L1_ffn_shared_gate_w"]), "shu": turned(d["L1_ffn_shared_up_w"]),
        "shd": np.ascontiguousarray(np.asarray(d["L1_ffn_shared_down_w"]).reshape(D, 4, P).transpose(2, 1, 0).reshape(P, -1)),
        "gu0": np.ascontiguousarray(up.transpose(2, 0, 1).reshape(D, -1)),
        "dn0": np.ascontiguousarray(down.transpose(2, 0, 1).reshape(4, P, NE0, D).transpose(1, 2, 0, 3).reshape(P, -1)),
    }


def kernel(**inputs):
    import concourse.bacc as bacc
    from concourse.bass_utils import run_bass_kernel_spmd

    nc = bacc.Bacc("TRN2", target_bir_lowering=False, num_devices=1)
    arrays = lay_out(inputs)
    args = {n: nc.dram_tensor(f"in_{n}", v.shape, mybir.dt.from_np(v.dtype), kind="ExternalInput").ap() for n, v in arrays.items()}
    out = nc.dram_tensor("out_x", (NB, P, D), F32, kind="ExternalOutput").ap()
    build(nc, args, out)
    r = run_bass_kernel_spmd(nc, [{f"in_{n}": v for n, v in arrays.items()}], core_ids=[0])
    return r.results[0]["out_x"]
```

```python
from contextlib import ExitStack

import concourse.bass as bass
from concourse import mybir

F32 = mybir.dt.float32
I32 = mybir.dt.int32
ALU = mybir.AluOpType
ACT = mybir.ActivationFunctionType
AX_X = mybir.AxisListType.X

P = 128
NB = 32
SK = 77
D = 128
PAIRS = NB // 2
NH = 16
DK0 = 64
DK1 = D // NH
C0 = NH * DK0 // P
NE0 = 8
NE1 = 16
SF = 512
GROUP = 4
EPS = 1e-5
SMALL_LOADS = 11
TURN = 8
HALF = TURN // 2
EARLY = 5
RSQRT_MAGIC = float(0x5F3759DF)
TB = 3


def layernorm(dve, srcs, dsts, scratch, before_write=()):
    n = len(srcs)
    stats, mv, v, h, y, t = scratch
    for k in range(n):
        dve.bn_stats(stats[:, k, :], srcs[k])
    dve.drain()
    for k in range(n):
        dve.bn_aggr(mv[:, k, :], stats[:, k, :])
    dve.drain()
    dve.tensor_scalar(v[:, 0:n], mv[:, 0:n, 1], EPS, None, ALU.add)
    dve.drain()
    dve.tensor_scalar(h[:, 0:n], v[:, 0:n], -0.5, None, ALU.mult)
    dve.tensor_scalar(y[:, 0:n].bitcast(I32), v[:, 0:n].bitcast(I32), -0.5, RSQRT_MAGIC, ALU.mult, ALU.add)
    for _ in range(3):
        dve.drain()
        if n == 1:
            dve.scalar_tensor_tensor(out=t[:, 0:1], in0=y[:, 0:1], scalar=y[:, 0:1], in1=h[:, 0:1], op0=ALU.mult, op1=ALU.mult)
        else:
            dve.tensor_tensor(t[:, 0:n], y[:, 0:n], y[:, 0:n], ALU.mult)
            dve.drain()
            dve.tensor_tensor(t[:, 0:n], t[:, 0:n], h[:, 0:n], ALU.mult)
        dve.drain()
        dve.scalar_tensor_tensor(out=y[:, 0:n], in0=t[:, 0:n], scalar=1.5, in1=y[:, 0:n], op0=ALU.add, op1=ALU.mult)
    dve.drain()
    for wait in before_write:
        dve.wait_ge(*wait)
    for k in range(n):
        last = dve.tensor_scalar(dsts[k], srcs[k], mv[:, k, 0:1], y[:, k:k + 1], ALU.subtract, ALU.mult)
    return last


def past(j, n):
    return not isinstance(j, int) or j >= n


class Experts:

    def __init__(self, nc, ctx, name, ne, slots, width):
        self.ne, self.slots, self.width = ne, slots, width
        self.rows = slots * NB * P
        self.tiles = self.rows // P + ne
        assert self.tiles % TURN == 0 and self.tiles * P < 2 ** 24

        def sem(what):
            return ctx.enter_context(nc.semaphore(f"{name}_{what}"))

        def sb(what, shape, dt=F32):
            return ctx.enter_context(nc.sbuf_tensor(f"{name}_{what}", shape, dt))

        self.step = sem("route_step")
        self.mask_ready, self.rank_ready = sem("mask_ready"), sem("rank_ready")
        self.place_ready, self.tiles_ready = sem("place_ready"), sem("tiles_ready")
        self.zero_filled, self.rows_placed = sem("zero_filled"), sem("rows_placed")
        self.place = sb("place", [P, slots * NB], I32)
        self.up_at = sb("up_at", [P, self.tiles], I32)
        self.down_at = sb("down_at", [P, self.tiles], I32)
        self.rows_loaded = [sem(f"rows_loaded{s}") for s in range(2)]
        self.rows_stored = [sem(f"rows_stored{s}") for s in range(2)]
        self.tx_ready, self.tx_done = sem("tx_ready"), sem("tx_done")
        self.gate_ready, self.up_ready = sem("gate_ready"), sem("up_ready")
        self.act_done, self.h_done = sem("act_done"), sem("h_done")
        self.th_ready, self.th_done = sem("th_ready"), sem("th_done")
        self.y_ready, self.y_done = sem("y_ready"), sem("y_done")


def build(nc, a, out, stages="ABCD"):
    with ExitStack() as ctx:
        def sb(name, shape, dt=F32):
            return ctx.enter_context(nc.sbuf_tensor(name, shape, dt))

        def sem(name):
            return ctx.enter_context(nc.semaphore(name))

        ps = ctx.enter_context(nc.psum_tensor("ps", [P, 8, 512], F32))
        x_res = sb("x_res", [P, NB, D])
        ctxT = sb("ctxT", [P, NB * SK])
        ident = sb("ident", [P, P])
        w0 = sb("w0", [P, 4, C0 * P])
        wq0, wk0, wv0, wo0 = (w0[:, k, :] for k in range(4))
        bq0 = sb("bq0", [P, C0])
        bk0 = sb("bk0", [P, C0])
        bv0 = sb("bv0", [SK, C0 * P])
        bo0 = sb("bo0", [P, D])
        gw0 = sb("gw0", [P, NE0])
        cpair = sb("cpair", [P, 2 * SK])
        xh = sb("xh", [P, 2, D])
        xhT = sb("xhT", [P, 2 * P])
        qT = sb("qT", [P, C0, 2 * P])
        kbd = sb("kbd", [P, 2, C0, 2 * SK])
        vv = sb("vv", [SK, 2, C0 * P])
        sc = sb("sc", [P, 2, NH * SK])
        smax = sb("smax", [P, 2, NH])
        ssum = sb("ssum", [P, 2, NH])
        rinv = sb("rinv", [P, 2, NH])
        pT = sb("pT", [SK, 4, 4 * P])
        oT = sb("oT", [P, C0, P])
        xf = sb("xf", [P, 2, D])
        xfT = sb("xfT", [P, P])
        logits0 = sb("logits0", [P, NB, NE0])
        ln_a = (sb("lna_st", [P, 2, 6]), sb("lna_mv", [P, 2, 2]), *(sb(f"lna_{k}", [P, 2]) for k in "vhyt"))
        ln_f = (sb("lnf_st", [P, 1, 6]), sb("lnf_mv", [P, 1, 2]), *(sb(f"lnf_{k}", [P, 1]) for k in "vhyt"))

        L0 = Experts(nc, ctx, "l0", NE0, 2, 512)
        rows_all = sb("rows_all", [P, NB, D])
        zeros = sb("zeros", [P, D])
        xrows = nc.dram_tensor("xrows", (L0.tiles * P, D), F32, kind="Internal").ap()
        yrows = nc.dram_tensor("yrows", (L0.tiles * P, D), F32, kind="Internal").ap()
        gu0 = sb("gu0", [P, NE0 * 1024])
        dn0 = sb("dn0", [P, NE0 * 512])
        consts = sb("consts", [P, 2 * P])
        iota, tri = consts[:, 0:P], consts[:, P:2 * P]
        ones = sb("ones", [P, P])
        pair_place = sb("pair_place", [P, 2, 2], I32)
        topw = sb("topw", [P, 2, NB])
        rt_small = sb("rt_small", [P, 6, 2 * NB])
        rt_int = sb("rt_int", [P, 2 * NB], I32)
        ne_small = sb("ne_small", [P, 4, NH])
        w1 = sb("w1", [P, 4, D])
        wq1, wk1, wv1, wo1 = (w1[:, k, :] for k in range(4))
        b1 = sb("b1", [P, 2])
        bv1 = sb("bv1", [SK, D])
        bo1 = sb("bo1", [P, D])
        gw1 = sb("gw1", [P, NE1])
        mask_in = sb("mask_in", [P, SK], I32)
        mask_add = sb("mask_add", [P, SK])
        head_rows = sb("head_rows", [P, NH])
        q1T = qT[:, 0, :]
        k1T = qT[:, 1, 0:2 * SK]
        k1m = kbd[:, :, :, :].rearrange("p s c n -> p s (c n)")
        v1 = qT[0:SK, 2, 0:2 * P].rearrange("p (s d) -> p s d", s=2)
        v1m = gu0[0:SK, 0:2 * NH * D].rearrange("p (s h d) -> p s h d", s=2, h=NH)
        o1T = qT[:, 3, 0:P]
        xs = qT[:, 4, 0:2 * P].rearrange("p (s d) -> p s d", s=2)
        score = sb("score", [P, 4])
        logits1 = sb("logits1", [P, NB, NE1])
        xT_all = w0[:, :, :].rearrange("p a n -> p (a n)")
        y1 = gu0[:, 0:NB * D].rearrange("p (b d) -> p b d", d=D)
        gu1 = gu0[:, NB * D:NB * D + NE1 * 2 * D]
        dn1 = dn0[:, 0:NE1 * D]
        shg, shu, shd = (dn0[:, 2048 + k * SF:2048 + (k + 1) * SF] for k in range(3))
        shared_gate = sb("shared_gate", [P, 2, 512])
        shared_h = qT[:, :, :].rearrange("p c q -> p (c q)").rearrange("p (c n) -> p c n", c=4)
        L1 = Experts(nc, ctx, "l1", NE1, 1, D)
        xrows1 = nc.dram_tensor("xrows1", (L1.tiles * P, D), F32, kind="Internal").ap()
        yrows1 = nc.dram_tensor("yrows1", (L1.tiles * P, D), F32, kind="Internal").ap()
        r_scratch = sc[:, :, :].rearrange("p s n -> p (s n)")
        xg = r_scratch[:, 0:TURN * D].rearrange("p (t d) -> p t d", d=D)
        ysb = r_scratch[:, TURN * D:2 * TURN * D].rearrange("p (t d) -> p t d", d=D)
        xgT = qT[:, 0:1, :].rearrange("p a (s q) -> p (a s) q", s=2)
        gact = qT[:, 2:6, :].rearrange("p (s a) n -> p s (a n)", s=2)
        hmul = kbd[:, 0, :, :].rearrange("p c n -> p (c n)")[:, 0:1024].rearrange("p (s n) -> p s n", s=2)
        hT = kbd[:, 1, :, :].rearrange("p c n -> p (c n)")[:, 0:1024].rearrange("p (s n) -> p s n", s=2)
        hold_mask = sb("hold_mask", [P, NB * NH])
        yin = oT[:, 0:4, :].rearrange("p (s k) d -> p s k d", s=2)

        ld = {k: sem("ld_" + k) for k in ("x", "ctx", "id", "wq", "wk", "wv", "wo", "gw")}
        kz = sem("kbd_zeroed")
        cp_ready = sem("cpair_ready")
        xh_done, xt_ready, xt_done = sem("xh_done"), sem("xt_ready"), sem("xt_done")
        q_ready, q_done = sem("q_ready"), sem("q_done")
        k_ready, k_done = sem("k_ready"), sem("k_done")
        v_ready, v_done = sem("v_ready"), sem("v_done")
        s_ready, max_done, sub_done = sem("s_ready"), sem("max_done"), sem("sub_done")
        exp_done, sum_done, rinv_done, p_done = sem("exp_done"), sem("sum_done"), sem("rinv_done"), sem("p_done")
        t_ready, pt_done = sem("t_ready"), sem("pt_done")
        ot_ready, ot_done = sem("ot_ready"), sem("ot_done")
        wo_ready, wo_part, wo_done = sem("wo_ready"), sem("wo_part"), sem("wo_done")
        xf_done, xf_stored = sem("xf_done"), [sem("xf_stored0"), sem("xf_stored1")]
        rt_ready, rt_done = sem("rt_ready"), sem("rt_done")
        rl_ready, rl_done = sem("rl_ready"), sem("rl_done")
        out_done = sem("out_done")
        ld_moe0 = sem("ld_moe0")
        ones_set = sem("ones_set")
        order_set = sem("order_set")
        w_sub, w_exp = sem("w_sub"), sem("w_exp")
        yin_loaded = [sem(f"yin_loaded{s}") for s in range(2)]
        comb_part, comb_done = sem("comb_part"), sem("comb_done")
        zeros_set, pair_place_ready = sem("zeros_set"), sem("pair_place_ready")
        ld_small, ld_moe1 = sem("ld_small"), sem("ld_moe1")
        mask_step, v1z = sem("mask_step"), sem("v1m_zeroed")
        c = {k: sem("c_" + k) for k in (
            "xh", "xt", "xt_moved", "q", "q_moved", "k", "k_moved", "k_masked", "v", "v_moved", "v_spread", "s", "masked", "max", "sub",
            "exp", "sum", "rinv", "p", "t", "pt", "ot", "ot_moved", "wo", "wo_part", "x", "xf", "rt", "rt_moved", "rt_kept", "rl",
            "rl_moved", "top", "top_exp", "score", "xs")}
        xs_stored = [sem("xs_stored0"), sem("xs_stored1")]
        sh = {k: sem("sh_" + k) for k in ("gate", "up", "act", "h", "down", "added")}
        y1_loaded, final_done = [sem(f"y1_loaded{g}") for g in range(NB // GROUP)], sem("final_done")

        block = ctx.enter_context(nc.Block())

        @block.sync
        def _(sp):
            x_tiles = a["x"].rearrange("b s d -> s b d")
            sp.dma_start(x_res[:, 0:4, :], x_tiles[:, 0:4, :]).then_inc(ld["x"], 16)
            sp.dma_start(ident[:, :], a["ident"]).then_inc(ld["id"], 16)
            sp.dma_start(wq0, a["wq0"]).then_inc(ld["wq"], 16)
            sp.dma_start(bq0[:, :], a["bq0"]).then_inc(ld["wq"], 16)
            sp.dma_start(ctxT[:, :], a["ctxT"]).then_inc(ld["ctx"], 16)
            sp.dma_start(wk0, a["wk0"]).then_inc(ld["wk"], 16)
            sp.dma_start(bk0[:, :], a["bk0"]).then_inc(ld["wk"], 16)
            sp.dma_start(wv0, a["wv0"]).then_inc(ld["wv"], 16)
            sp.dma_start(bv0[:, :], a["bv0"].rearrange("(o n) -> o n", o=1).broadcast_to([SK, C0 * P])).then_inc(ld["wv"], 16)
            sp.dma_start(x_res[:, 4:NB, :], x_tiles[:, 4:NB, :]).then_inc(ld["x"], 16)
            sp.dma_start(wo0.rearrange("p (c n) -> p c n", c=C0), a["wo0"].rearrange("(c p) n -> p c n", p=P)).then_inc(ld["wo"], 16)
            sp.dma_start(bo0[:, :], a["bo0"].rearrange("(o n) -> o n", o=1).broadcast_to([P, D])).then_inc(ld["wo"], 16)
            sp.dma_start(gw0[:, :], a["gw0"]).then_inc(ld["gw"], 16)
            sp.dma_start(consts[:, :], a["consts"]).then_inc(ld_small, 16)
            sp.dma_start(gu0[:, :], a["gu0"]).then_inc(ld_moe0, 16)
            sp.dma_start(dn0[:, :], a["dn0"]).then_inc(ld_moe0, 16)
            for k, name in enumerate(("wq1", "wk1", "wv1", "wo1")):
                sp.dma_start(w1[:, k, :], a[name]).then_inc(ld_small, 16)
            sp.dma_start(b1[:, :], a["b1"]).then_inc(ld_small, 16)
            sp.dma_start(bv1[:, :], a["bv1"].rearrange("(o n) -> o n", o=1).broadcast_to([SK, D])).then_inc(ld_small, 16)
            sp.dma_start(bo1[:, :], a["bo1"].rearrange("(o n) -> o n", o=1).broadcast_to([P, D])).then_inc(ld_small, 16)
            sp.dma_start(gw1[:, :], a["gw1"]).then_inc(ld_small, 16)
            sp.dma_start(head_rows[:, :], a["head_rows"]).then_inc(ld_small, 16)
            sp.dma_start(mask_in[:, :], a["mask"]).then_inc(ld_small, 16)
            sp.wait_ge(zeros_set, 1)
            for L, rows in ((L0, xrows), (L1, xrows1)):
                sp.dma_start(rows.rearrange("(t p) d -> p t d", p=P),
                             zeros[:, :].unsqueeze(1).broadcast_to([P, L.tiles, D])).then_inc(L.zero_filled, 16)

            with sp.Fori(0, PAIRS) as i:
                for s in range(2):
                    sp.wait_ge(xf_done, 2 * i + s + 1)
                    sp.dma_start(rows_all[:, bass.ds(2 * i + s, 1), :], xf[:, s:s + 1, :]).then_inc(xf_stored[s], 16)

            def move_tiles(L, xrows, yrows):
                def tiles_of(rows, g):
                    return rows[bass.ds(g * HALF * P, HALF * P), :].rearrange("(t p) d -> p t d", p=P)

                def load(g, h):
                    sp.dma_start(xg[:, h * HALF:(h + 1) * HALF, :], tiles_of(xrows, g)).then_inc(L.rows_loaded[h], 16)

                def body(i, last=False):
                    for h in range(2):
                        g = 2 * i + h
                        if not last:
                            sp.wait_ge(L.tx_ready, HALF * (g + 1))
                            load(g + 2, h)
                        sp.wait_ge(L.y_done, HALF * (g + 1))
                        sp.dma_start(tiles_of(yrows, g), ysb[:, h * HALF:(h + 1) * HALF, :]).then_inc(L.rows_stored[h], 16)

                sp.wait_ge(L.tiles_ready, 1)
                sp.wait_ge(L.rows_placed, 16 * L.slots * NB)
                load(0, 0)
                load(1, 1)
                with sp.Fori(0, L.tiles // TURN - 1) as i:
                    body(i)
                body(L.tiles // TURN - 1, last=True)
                for h in range(2):
                    sp.wait_ge(L.rows_stored[h], 16 * L.tiles // TURN)

            move_tiles(L0, xrows, yrows)
            sp.dma_start(gu1, a["gu1"]).then_inc(ld_moe1, 16)
            sp.dma_start(dn1, a["dn1"]).then_inc(ld_moe1, 16)
            for weights, name in ((shg, "shg"), (shu, "shu"), (shd, "shd")):
                sp.dma_start(weights, a[name]).then_inc(ld_moe1, 16)
            with sp.Fori(0, PAIRS) as i:
                for s in range(2):
                    sp.wait_ge(c["xs"], 2 * i + s + 1)
                    sp.dma_start(rows_all[:, bass.ds(2 * i + s, 1), :], xs[:, s:s + 1, :]).then_inc(xs_stored[s], 16)

            move_tiles(L1, xrows1, yrows1)
            for g in range(NB // GROUP):
                sp.wait_ge(final_done, g + 1)
                sp.dma_start(out[g * GROUP:(g + 1) * GROUP].rearrange("b s d -> s b d"),
                             x_res[:, g * GROUP:(g + 1) * GROUP, :]).then_inc(out_done, 16)
            sp.wait_ge(out_done, 16 * NB // GROUP)

        @block.gpsimd
        def _(pool):
            nc.gpsimd.memset(kbd[:, :, :, :], 0.0).then_inc(kz, 1)
            nc.gpsimd.memset(zeros[:, :], 0.0).then_inc(zeros_set, 1)
            nc.gpsimd.memset(ones[:, :], 1.0).then_inc(ones_set, 1)

            def copy_contexts(i):
                nc.gpsimd.tensor_copy(cpair[:, :], ctxT[:, bass.ds(i * 2 * SK, 2 * SK)]).then_inc(cp_ready, 1)

            def normalise(b, s):
                pool.wait_ge(rinv_done, b + 1)
                p = sc[:, s, :].rearrange("p (h k) -> p h k", h=NH)
                nc.gpsimd.tensor_tensor(p, p, rinv[:, s, :].unsqueeze(2).broadcast_to([P, NH, SK]), ALU.mult).then_inc(p_done, 1)

            pool.wait_ge(ld["ctx"], 16)
            copy_contexts(0)
            normalise(0, 0)
            with pool.Fori(0, PAIRS - 1) as i:
                pool.wait_ge(v_ready, 4 * i + 4)
                copy_contexts(i + 1)
                normalise(2 * i + 1, 1)
                normalise(2 * i + 2, 0)
            normalise(NB - 1, 1)

            def place_rows(L, stored, xrows):
                for s in range(2):
                    pool.wait_ge(stored[s], 16 * PAIRS)
                pool.wait_ge(L.zero_filled, 16)
                pool.wait_ge(L.place_ready, 1)
                for n in range(L.slots * NB):
                    nc.gpsimd.indirect_dma_start(xrows, bass.IndirectOffsetOnAxis(L.place[:, n:n + 1], 0), rows_all[:, n % NB, :],
                                                 None).then_inc(L.rows_placed, 16)

            place_rows(L0, xf_stored, xrows)

            def copy_contexts1(i):
                nc.gpsimd.tensor_copy(cpair[:, :], ctxT[:, bass.ds(i * 2 * SK, 2 * SK)]).then_inc(cp_ready, 1)

            def mask_keys(b, i, s):
                pool.wait_ge(c["k_moved"], i + 1)
                if not (isinstance(b, int) and b < 2):
                    pool.wait_ge(c["s"], b - 1)
                nc.gpsimd.tensor_tensor(k1m[:, s, :].rearrange("p (h k) -> p h k", h=NH),
                                        k1T[:, s * SK:(s + 1) * SK].unsqueeze(1).broadcast_to([P, NH, SK]),
                                        head_rows[:, :].unsqueeze(2).broadcast_to([P, NH, SK]), ALU.mult).then_inc(c["k_masked"], 1)

            def spread_values(b, s):
                if not (isinstance(b, int) and b < 2):
                    pool.wait_ge(c["ot"], b - 1)
                pool.wait_ge(c["v_moved"], b + 1)
                flat = v1m[:, s, :, :].rearrange("p h d -> p (h d)")
                blocks = bass.AP(flat.tensor, flat.offset, [list(flat.ap[0]), [D + DK1, NH], [1, DK1]])
                nc.gpsimd.tensor_tensor(blocks, v1[:, s, :].rearrange("p (h d) -> p h d", h=NH),
                                        bv1[:, :].rearrange("p (h d) -> p h d", h=NH), ALU.add).then_inc(c["v_spread"], 1)

            def normalise1(b, s):
                pool.wait_ge(c["rinv"], b + 1)
                p = sc[:, s, :].rearrange("p (h k) -> p h k", h=NH)
                nc.gpsimd.tensor_tensor(p, p, rinv[:, s, :].unsqueeze(2).broadcast_to([P, NH, SK]), ALU.mult).then_inc(c["p"], 1)

            def keep_xT(b):
                pool.wait_ge(c["rt_moved"], b + 1)
                nc.gpsimd.tensor_copy(xT_all[:, bass.ds(b * P, P)], xfT[:, :]).then_inc(c["rt_kept"], 1)

            def fetch_results(i, s):
                if not (isinstance(i, int) and i == 0):
                    pool.wait_ge(comb_done, 2 * i + s - 1)
                copied = 2 * i + s + 1 if isinstance(i, int) else pool.to_reg(2 * i + s + 1)
                nc.gpsimd.tensor_copy(pair_place[:, s, :].unsqueeze(1),
                                      L0.place[:, :].rearrange("p (k b) -> p b k", k=2)[:, bass.ds(2 * i + s, 1), :]
                                      ).then_inc(pair_place_ready, 1)
                pool.wait_ge(L0.rows_stored[0], 16 * L0.tiles // TURN)
                pool.wait_ge(pair_place_ready, copied)
                for k in range(2):
                    nc.gpsimd.indirect_dma_start(yin[:, s, k, :], None, yrows,
                                                 bass.IndirectOffsetOnAxis(pair_place[:, s, k:k + 1], 0)).then_inc(yin_loaded[s], 16)

            for h in range(2):
                pool.wait_ge(L0.rows_stored[h], 16 * L0.tiles // TURN)
            fetch_results(0, 0)
            fetch_results(0, 1)
            nc.gpsimd.memset(v1m[:, :, :, :], 0.0).then_inc(v1z, 1)
            pool.wait_ge(v1z, 1)
            copy_contexts1(0)
            pool.wait_ge(ld_small, 16 * SMALL_LOADS)
            mask_keys(0, 0, 0)
            spread_values(0, 0)
            mask_keys(1, 0, 1)
            fetch_results(1, 0)
            fetch_results(1, 1)
            normalise1(0, 0)
            spread_values(1, 1)

            def body1(i, first=False, last=False, fetch=True):
                b0, b1 = 2 * i, 2 * i + 1
                if not first:
                    keep_xT(b0 - 1)
                if not last:
                    pool.wait_ge(c["v"], 2 * i + 2)
                    copy_contexts1(i + 1)
                normalise1(b1, 1)
                if fetch:
                    fetch_results(i + 2, 0)
                    fetch_results(i + 2, 1)
                if not last:
                    mask_keys(b0 + 2, i + 1, 0)
                    spread_values(b0 + 2, 0)
                keep_xT(b0)
                if not last:
                    mask_keys(b1 + 2, i + 1, 1)
                    normalise1(b0 + 2, 0)
                    spread_values(b1 + 2, 1)
                else:
                    keep_xT(b1)

            body1(0, first=True)
            with pool.Fori(1, PAIRS - 2) as i:
                body1(i)
            body1(PAIRS - 2, fetch=False)
            body1(PAIRS - 1, last=True, fetch=False)

            place_rows(L1, xs_stored, xrows1)
            for h in range(2):
                pool.wait_ge(L1.rows_stored[h], 16 * L1.tiles // TURN)
            for b in range(NB):
                nc.gpsimd.indirect_dma_start(y1[:, b, :], None, yrows1, bass.IndirectOffsetOnAxis(L1.place[:, b:b + 1], 0)
                                             ).then_inc(y1_loaded[b // GROUP], 16)

        @block.scalar
        def _(act):
            def move_xT(i):
                act.wait_ge(xt_ready, i + 1)
                nc.scalar.copy(xhT[:, :], ps[:, 5, 0:2 * P]).then_inc(xt_done, 1)

            def move_q(i):
                for n, bank in enumerate((6, 7, 5, 6)):
                    act.wait_ge(q_ready, 4 * i + n + 1)
                    for c in (2 * n, 2 * n + 1):
                        last = nc.scalar.activation(qT[:, c, :], ps[:, bank, (c % 2) * 256:(c % 2) * 256 + 256],
                                                    ACT.Identity, bias=bq0[:, c:c + 1])
                    last.then_inc(q_done, 1)

            def move_pT(b, g):
                act.wait_ge(t_ready, 4 * b + g + 1)
                nc.scalar.copy(pT[:, g, :], ps[0:SK, TB + g % 2, :]).then_inc(pt_done, 1)

            def exponentials(b, s):
                act.wait_ge(sub_done, b + 1)
                nc.scalar.activation(sc[:, s, :], sc[:, s, :], ACT.Exp, scale=float(DK0) ** -0.5).then_inc(exp_done, 1)

            def move_xfT(b, bank):
                act.wait_ge(rt_ready, b + 1)
                if not (isinstance(b, int) and b == 0):
                    act.wait_ge(rl_ready, b)
                nc.scalar.copy(xfT[:, :], ps[:, bank, 0:P]).then_inc(rt_done, 1)

            def move_logits(b):
                act.wait_ge(rl_ready, b + 1)
                nc.scalar.copy(logits0[:, bass.ds(b, 1), :].rearrange("p o e -> p (o e)"), ps[:, 7, 0:NE0]).then_inc(rl_done, 1)

            def body(i, first=False, last=False):
                b0, b1 = 2 * i, 2 * i + 1
                if not first:
                    move_xfT(b0 - 1, 7)
                act.wait_ge(ot_ready, 2 * b0) if not first else None
                move_pT(b0, 0)
                move_pT(b0, 1)
                move_pT(b0, 2)
                exponentials(b1, 1)
                if not first:
                    move_logits(b0 - 1)
                move_pT(b0, 3)
                if not last:
                    act.wait_ge(s_ready, b1 + 1)
                    if not first:
                        pass
                    move_xT(i + 1)
                    move_q(i + 1)
                move_xfT(b0, 6)
                act.wait_ge(ot_ready, 2 * b1)
                move_pT(b1, 0)
                move_pT(b1, 1)
                move_pT(b1, 2)
                if not last:
                    exponentials(b1 + 1, 0)
                move_logits(b0)
                move_pT(b1, 3)
                if last:
                    move_xfT(b1, 7)
                    move_logits(b1)

            act.wait_ge(ld["wq"], 32)
            move_xT(0)
            move_q(0)
            exponentials(0, 0)
            body(0, first=True)
            with act.Fori(1, PAIRS - 1) as i:
                body(i)
            body(PAIRS - 1, last=True)

            def experts(L, func):
                def move_xT(j, s):
                    act.wait_ge(L.tx_ready, j + 1)
                    if past(j, 2):
                        act.wait_ge(L.up_ready, j - 1)
                    nc.scalar.copy(xgT[:, s, :], ps[:, 4, 0:P]).then_inc(L.tx_done, 1)

                def gate(j, s):
                    act.wait_ge(L.gate_ready, j + 1)
                    if past(j, 2):
                        act.wait_ge(L.h_done, j - 1)
                    nc.scalar.activation(gact[:, s, 0:L.width], ps[:, 2 * s, 0:L.width], func).then_inc(L.act_done, 1)

                def move_y(j, t, i):
                    act.wait_ge(L.y_ready, j + 1)
                    if t % HALF == 0 and past(j, TURN):
                        act.wait_ge(L.rows_stored[t // HALF], 16 * i)
                    nc.scalar.copy(ysb[:, t, :], ps[:, 7, 0:D]).then_inc(L.y_done, 1)

                def body(i, first=False, last=False):
                    for t in range(TURN):
                        j = TURN * i + t
                        if not (last and t == TURN - 1):
                            move_xT(j + 1, (t + 1) % 2)
                        gate(j, t % 2)
                        if t:
                            move_y(j - 1, t - 1, i)
                        elif not first:
                            move_y(j - 1, TURN - 1, i - 1)

                move_xT(0, 0)
                body(0, first=True)
                with act.Fori(1, L.tiles // TURN - 1) as i:
                    body(i)
                body(L.tiles // TURN - 1, last=True)
                move_y(L.tiles - 1, TURN - 1, L.tiles // TURN - 1)

            act.wait_ge(w_sub, 1)
            nc.scalar.activation(rt_small[:, 3, 0:NB], rt_small[:, 3, 0:NB], ACT.Exp)
            nc.scalar.activation(r_scratch[:, 512:512 + NB * NE0], r_scratch[:, 512:512 + NB * NE0], ACT.Exp).then_inc(w_exp, 1)
            experts(L0, ACT.Gelu)

            def move1(ready, count, dst, src, done, bias=None):
                act.wait_ge(ready, count)
                if bias is None:
                    nc.scalar.copy(dst, src).then_inc(done, 1)
                else:
                    nc.scalar.activation(dst, src, ACT.Identity, bias=bias).then_inc(done, 1)

            def move_xT1(i):
                move1(c["xt"], i + 1, xhT[:, :], ps[:, 6, 0:2 * P], c["xt_moved"])

            def move_qk1(i):
                move1(c["q"], i + 1, q1T, ps[:, 5, 0:2 * P], c["q_moved"], b1[:, 0:1])
                if not (isinstance(i, int) and i == 0):
                    act.wait_ge(c["k_masked"], 2 * i)
                move1(c["k"], i + 1, k1T, ps[:, 7, 0:2 * SK], c["k_moved"], b1[:, 1:2])

            def move_v1(b, s, bank):
                if not (isinstance(b, int) and b < 2):
                    act.wait_ge(c["v_spread"], b - 1)
                move1(c["v"], b + 1, v1[:, s, :], ps[0:SK, bank, 0:D], c["v_moved"])

            def move_pT1(b, g):
                move1(c["t"], 4 * b + g + 1, pT[:, g, :], ps[0:SK, TB + g % 2, :], c["pt"])

            def exponentials1(b, s):
                act.wait_ge(c["sub"], b + 1)
                nc.scalar.activation(sc[:, s, :], sc[:, s, :], ACT.Exp, scale=float(DK1) ** -0.5).then_inc(c["exp"], 1)

            def move_oT1(b, bank):
                if not (isinstance(b, int) and b == 0):
                    act.wait_ge(c["wo"], b)
                move1(c["ot"], b + 1, o1T, ps[:, bank, 0:P], c["ot_moved"])

            def move_xfT1(b, bank):
                if not (isinstance(b, int) and b == 0):
                    act.wait_ge(c["rl"], b)
                    act.wait_ge(c["rt_kept"], b)
                move1(c["rt"], b + 1, xfT[:, :], ps[:, bank, 0:P], c["rt_moved"])

            def move_logits1(b):
                move1(c["rl"], b + 1, logits1[:, bass.ds(b, 1), :].rearrange("p o e -> p (o e)"), ps[:, 7, 0:NE1], c["rl_moved"])

            def top_exponential(b):
                act.wait_ge(c["top"], b + 1)
                nc.scalar.activation(score[:, 1:2], score[:, 0:1], ACT.Exp, scale=-1.0).then_inc(c["top_exp"], 1)

            def body1(i, first=False, last=False):
                b0, b1_ = 2 * i, 2 * i + 1
                if not first:
                    move_xfT1(b0 - 1, 7)
                    act.wait_ge(c["ot"], b0)
                move_pT1(b0, 0)
                move_pT1(b0, 1)
                move_pT1(b0, 2)
                exponentials1(b1_, 1)
                if not first:
                    move_logits1(b0 - 1)
                move_pT1(b0, 3)
                move_oT1(b0, 5)
                if not first:
                    top_exponential(b0 - 1)
                if not last:
                    move_xT1(i + 1)
                    act.wait_ge(c["s"], b1_ + 1)
                    move_qk1(i + 1)
                    move_v1(b0 + 2, 0, 6)
                move_xfT1(b0, 5)
                act.wait_ge(c["ot"], b1_)
                move_pT1(b1_, 0)
                move_pT1(b1_, 1)
                move_pT1(b1_, 2)
                if not last:
                    exponentials1(b1_ + 1, 0)
                move_logits1(b0)
                move_pT1(b1_, 3)
                move_oT1(b1_, 6)
                top_exponential(b0)
                if not last:
                    move_v1(b1_ + 2, 1, 5)
                if last:
                    move_xfT1(b1_, 7)
                    move_logits1(b1_)
                    top_exponential(b1_)

            move_xT1(0)
            move_qk1(0)
            move_v1(0, 0, 6)
            exponentials1(0, 0)
            move_v1(1, 1, 5)
            body1(0, first=True)
            with act.Fori(1, PAIRS - 1) as i:
                body1(i)
            body1(PAIRS - 1, last=True)

            def shared(g):
                for k in range(4):
                    s = k % 2
                    act.wait_ge(sh["gate"], 4 * g + k + 1)
                    if not (isinstance(g, int) and g == 0 and k < 2):
                        act.wait_ge(sh["h"], 4 * g + k - 1)
                    nc.scalar.activation(shared_gate[:, s, :], ps[:, 2 * s, :], ACT.Silu).then_inc(sh["act"], 1)

            shared(0)
            with act.Fori(1, EARLY) as g:
                shared(g)
            act.wait_ge(sh["down"], EARLY)
            experts(L1, ACT.Silu)
            with act.Fori(EARLY, NB // GROUP) as g:
                shared(g)

        @block.vector
        def _(dve):
            def norm_inputs(i):
                free = () if isinstance(i, int) and i == 0 else ((xt_ready, i),)
                rows = [x_res[:, bass.ds(2 * i + s, 1), :].rearrange("p o d -> p (o d)") for s in range(2)]
                layernorm(dve, rows, [xh[:, s, :] for s in range(2)], ln_a, free).then_inc(xh_done, 1)

            def move_k(i):
                for n, (c0, c1, bank) in enumerate(((0, 3, 7), (3, 6, 5), (6, 8, 6))):
                    dve.wait_ge(k_ready, 3 * i + n + 1)
                    m = c1 - c0
                    for half in range(2):
                        lo = 64 * half
                        for s in range(2):
                            src = ps[lo:lo + 64, bank, 0:m * 2 * SK].rearrange("p (c s k) -> p c s k", c=m, s=2)[:, :, s, :]
                            last = nc.vector.tensor_tensor(kbd[lo:lo + 64, s, c0:c1, half * SK:(half + 1) * SK], src,
                                                           bk0[lo:lo + 64, c0:c1].unsqueeze(2).broadcast_to([64, m, SK]), ALU.add)
                    last.then_inc(k_done, 1)

            def move_v(b, s, banks):
                if not (isinstance(b, int) and b < 2):
                    dve.wait_ge(ot_ready, 2 * b - 2)
                for n, bank in enumerate(banks):
                    dve.wait_ge(v_ready, 2 * b + n + 1)
                    nc.vector.tensor_tensor(vv[:, s, n * 512:(n + 1) * 512], ps[0:SK, bank, :],
                                            bv0[:, n * 512:(n + 1) * 512], ALU.add).then_inc(v_done, 1)

            def subtract_max(b, s):
                dve.wait_ge(s_ready, b + 1)
                if not (isinstance(b, int) and b < 2):
                    dve.wait_ge(t_ready, 4 * b - 4)
                lo = ps[:, 0:2, 0:6 * SK].rearrange("p a (h k) -> p a h k", h=6)
                hi = ps[:, 2, 0:4 * SK].rearrange("p (h k) -> p h k", h=4)
                nc.vector.tensor_reduce(smax[:, s, 0:12].rearrange("p (a h) -> p a h", a=2), lo, AX_X, ALU.max)
                nc.vector.tensor_reduce(smax[:, s, 12:16], hi, AX_X, ALU.max).then_inc(max_done, 1)
                dve.wait_ge(max_done, b + 1)
                d = sc[:, s, :].rearrange("p (h k) -> p h k", h=NH)
                for k in range(2):
                    nc.vector.tensor_tensor(d[:, 6 * k:6 * k + 6, :], ps[:, k, 0:6 * SK].rearrange("p (h k) -> p h k", h=6),
                                            smax[:, s, 6 * k:6 * k + 6].unsqueeze(2).broadcast_to([P, 6, SK]), ALU.subtract)
                nc.vector.tensor_tensor(d[:, 12:16, :], hi, smax[:, s, 12:16].unsqueeze(2).broadcast_to([P, 4, SK]),
                                        ALU.subtract).then_inc(sub_done, 1)

            def sums(b, s):
                dve.wait_ge(exp_done, b + 1)
                nc.vector.tensor_reduce(ssum[:, s, :], sc[:, s, :].rearrange("p (h k) -> p h k", h=NH), AX_X, ALU.add).then_inc(sum_done, 1)
                dve.wait_ge(sum_done, b + 1)
                nc.vector.reciprocal(rinv[:, s, :], ssum[:, s, :]).then_inc(rinv_done, 1)

            def move_oT(b, half):
                dve.wait_ge(ot_ready, 2 * b + half + 1)
                if not (isinstance(b, int) and b == 0) and half == 0:
                    dve.wait_ge(wo_ready, b)
                nc.vector.tensor_copy(oT[:, 4 * half:4 * half + 4, :].rearrange("p c q -> p (c q)"), ps[:, 5 + half, :]).then_inc(ot_done, 1)

            def residual_and_norm(i, s):
                b = 2 * i + s
                row = x_res[:, bass.ds(b, 1), :].rearrange("p o d -> p (o d)")
                nc.vector.tensor_tensor(row, row, bo0[:, :], ALU.add).then_inc(wo_part, 1)
                dve.wait_ge(wo_ready, b + 1)
                dve.wait_ge(wo_part, b + 1)
                nc.vector.tensor_tensor(row, ps[:, 7, 0:D], row, ALU.add).then_inc(wo_done, 1)
                dve.drain()
                free = () if isinstance(i, int) and i == 0 else ((xf_stored[s], 16 * i), (rt_ready, b - 1))
                layernorm(dve, [row], [xf[:, s, :]], ln_f, free).then_inc(xf_done, 1)

            def body(i, last=False):
                b0, b1 = 2 * i, 2 * i + 1
                subtract_max(b1, 1)
                if not last:
                    norm_inputs(i + 1)
                move_oT(b0, 0)
                sums(b1, 1)
                move_oT(b0, 1)
                residual_and_norm(i, 0)
                if not last:
                    move_k(i + 1)
                    move_v(b0 + 2, 0, (7, 5))
                    subtract_max(b0 + 2, 0)
                move_oT(b1, 0)
                if not last:
                    sums(b0 + 2, 0)
                move_oT(b1, 1)
                residual_and_norm(i, 1)
                if not last:
                    move_v(b1 + 2, 1, (5, 6))

            dve.wait_ge(ld["x"], 32)
            norm_inputs(0)
            dve.wait_ge(ld["wk"], 32)
            dve.wait_ge(kz, 1)
            move_k(0)
            dve.wait_ge(ld["wv"], 32)
            move_v(0, 0, (7, 5))
            subtract_max(0, 0)
            sums(0, 0)
            move_v(1, 1, (5, 6))
            dve.wait_ge(ld["wo"], 32)
            body(0)
            with dve.Fori(1, PAIRS - 1) as i:
                body(i)
            body(PAIRS - 1, last=True)

            def route(L, logits, first_expert):
                ne, nt, n = L.ne, L.tiles, NB * L.ne
                count = [0]

                def then(ins):
                    count[0] += 1
                    ins.then_inc(L.step, 1)
                    dve.wait_ge(L.step, count[0])

                def grid(k):
                    return r_scratch[:, k * n:(k + 1) * n].rearrange("p (b e) -> p b e", e=ne)

                def over_e(v):
                    return v.unsqueeze(2).broadcast_to([P, NB, ne])

                def over_b(v):
                    return v.unsqueeze(1).broadcast_to([P, NB, ne])

                masks, eq, rest = [grid(k) for k in range(L.slots)], grid(L.slots), grid(L.slots + 1)
                incl, pos = grid(L.slots + 2), grid(L.slots + 1)
                order = over_b(first_expert)
                tops = [rt_small[:, k, 0:NB] for k in range(2)]
                cand = rt_small[:, 2, 0:NB]
                left = logits
                for k in range(L.slots):
                    then(nc.vector.tensor_reduce(tops[k], left, AX_X, ALU.max))
                    then(nc.vector.tensor_tensor(eq, left, over_e(tops[k]), ALU.is_equal))
                    then(nc.vector.tensor_tensor(eq, eq, order, ALU.mult))
                    then(nc.vector.tensor_reduce(cand, eq, AX_X, ALU.max))
                    then(nc.vector.tensor_tensor(masks[k], order, over_e(cand), ALU.is_equal))
                    if k + 1 < L.slots:
                        then(nc.vector.scalar_tensor_tensor(out=rest, in0=masks[k], scalar=-3e38, in1=left, op0=ALU.mult, op1=ALU.add))
                        left = rest
                both = masks[0]
                if L.slots == 2:
                    then(nc.vector.tensor_tensor(eq, masks[0], masks[1], ALU.add))
                    both = eq
                nc.vector.tensor_copy(hold_mask[:, 0:n].rearrange("p (b e) -> p b e", e=ne), both).then_inc(L.mask_ready, 1)
                if L.slots == 2:
                    then(nc.vector.tensor_tensor(rt_small[:, 3, 0:NB], tops[1], tops[0], ALU.subtract))
                    nc.vector.tensor_tensor(rest, logits, over_e(tops[0]), ALU.subtract).then_inc(w_sub, 1)
                    dve.wait_ge(w_exp, 1)
                    e2, z, p2 = rt_small[:, 3, 0:NB], rt_small[:, 4, 0:NB], rt_small[:, 5, 0:NB]
                    then(nc.vector.tensor_reduce(z, rest, AX_X, ALU.add))
                    then(nc.vector.reciprocal(z, z))
                    then(nc.vector.tensor_tensor(p2, e2, z, ALU.mult))
                    then(nc.vector.tensor_tensor(e2, z, p2, ALU.add))
                    then(nc.vector.reciprocal(e2, e2))
                    then(nc.vector.tensor_tensor(topw[:, 0, :], z, e2, ALU.mult))
                    then(nc.vector.tensor_tensor(topw[:, 1, :], p2, e2, ALU.mult))
                dve.wait_ge(L.rank_ready, 2)
                totals = ps[:, 7, 0:n].rearrange("p (b e) -> p b e", e=ne)
                for e in range(ne):
                    last = nc.vector.tensor_tensor_scan(incl[:, :, e], ones[:, 0:NB], totals[:, :, e], 0.0, ALU.mult, ALU.add)
                then(last)
                fill, begin, end = (ne_small[:, k, 0:ne] for k in range(3))
                then(nc.vector.tensor_tensor(pos, incl, totals, ALU.subtract))
                then(nc.vector.tensor_scalar(rt_int[:, 0:ne], incl[:, NB - 1, :], (P - 1) / 2, 1.0 / P, ALU.add, ALU.mult))
                then(nc.vector.tensor_copy(fill, rt_int[:, 0:ne]))
                then(nc.vector.tensor_tensor_scan(end, ones[:, 0:ne], fill, 0.0, ALU.mult, ALU.add))
                then(nc.vector.tensor_tensor(begin, end, fill, ALU.subtract))
                then(nc.vector.tensor_scalar(begin, begin, float(P), None, ALU.mult))
                then(nc.vector.tensor_tensor(pos, pos, over_b(begin), ALU.add))
                then(nc.vector.tensor_tensor(pos, pos, ps[:, 6, 0:n].rearrange("p (b e) -> p b e", e=ne), ALU.add))
                m = L.slots * NB
                at = rt_small[:, 4, 0:m]
                for k in range(L.slots):
                    then(nc.vector.tensor_tensor(eq, masks[k], pos, ALU.mult))
                    then(nc.vector.tensor_reduce(at[:, k * NB:(k + 1) * NB], eq, AX_X, ALU.add))
                then(nc.vector.tensor_copy(L.place[:, 0:m], at))
                nc.vector.tensor_copy(ne_small[:, 0, 0:1], at[:, 0:1]).then_inc(L.place_ready, 1)
                past = r_scratch[:, 0:nt * ne].rearrange("p (j e) -> p j e", e=ne)
                then(nc.vector.tensor_tensor(past, iota[:, 0:nt].unsqueeze(2).broadcast_to([P, nt, ne]),
                                             end.unsqueeze(1).broadcast_to([P, nt, ne]), ALU.is_ge))
                expert = r_scratch[:, 1024:1024 + nt]
                then(nc.vector.tensor_reduce(expert, past, AX_X, ALU.add))
                then(nc.vector.tensor_scalar(L.up_at[:, :], expert, float(ne - 1), float(2 * L.width), ALU.min, ALU.mult))
                nc.vector.tensor_scalar(L.down_at[:, :], expert, float(ne - 1), float(L.width), ALU.min, ALU.mult).then_inc(L.tiles_ready, 1)

            def experts(L):
                def multiply(j, s):
                    dve.wait_ge(L.act_done, j + 1)
                    dve.wait_ge(L.up_ready, j + 1)
                    if past(j, 2):
                        dve.wait_ge(L.th_ready, j - 1)
                    nc.vector.tensor_tensor(hmul[:, s, 0:L.width], ps[:, 2 * s + 1, 0:L.width], gact[:, s, 0:L.width], ALU.mult).then_inc(L.h_done, 1)

                def move_hT(j, s):
                    dve.wait_ge(L.th_ready, j + 1)
                    if past(j, 2):
                        dve.wait_ge(L.y_ready, j - 1)
                    nc.vector.tensor_copy(hT[:, s, 0:L.width], ps[:, 5 + s, 0:L.width]).then_inc(L.th_done, 1)

                def body(i, first=False):
                    for t in range(TURN):
                        j = TURN * i + t
                        if not (first and t == 0):
                            move_hT(j - 1, (t - 1) % 2)
                        multiply(j, t % 2)

                body(0, first=True)
                with dve.Fori(1, L.tiles // TURN) as i:
                    body(i)
                move_hT(L.tiles - 1, (L.tiles - 1) % 2)

            dve.wait_ge(rl_done, NB)
            dve.wait_ge(ld_small, 16 * SMALL_LOADS)
            dve.wait_ge(ones_set, 1)
            nc.vector.tensor_scalar(ne_small[:, 3, :], iota[:, 0:NH], -1.0, float(NE0), ALU.mult, ALU.add).then_inc(order_set, 1)
            dve.wait_ge(order_set, 1)
            dve.wait_ge(t_ready, 4 * NB)
            route(L0, logits0[:, :, :], ne_small[:, 3, 0:NE0])
            experts(L0)

            def combine(i, s):
                b = 2 * i + s
                row = x_res[:, bass.ds(b, 1), :].rearrange("p o d -> p (o d)")
                dve.wait_ge(yin_loaded[s], 32 * (i + 1))
                nc.vector.scalar_tensor_tensor(out=row, in0=yin[:, s, 0, :], scalar=topw[:, 0, bass.ds(b, 1)], in1=row,
                                               op0=ALU.mult, op1=ALU.add).then_inc(comb_part, 1)
                dve.wait_ge(comb_part, b + 1)
                nc.vector.scalar_tensor_tensor(out=row, in0=yin[:, s, 1, :], scalar=topw[:, 1, bass.ds(b, 1)], in1=row,
                                               op0=ALU.mult, op1=ALU.add).then_inc(comb_done, 1)

            def row_of(b):
                return x_res[:, bass.ds(b, 1), :].rearrange("p o d -> p (o d)")

            def norm_inputs1(i):
                for s in range(2):
                    combine(i, s)
                dve.drain()
                free = () if isinstance(i, int) and i == 0 else ((c["xt"], i),)
                layernorm(dve, [row_of(2 * i + s) for s in range(2)], [xh[:, s, :] for s in range(2)], ln_a, free).then_inc(c["xh"], 1)

            def subtract_max1(b, s):
                dve.wait_ge(c["s"], b + 1)
                if not (isinstance(b, int) and b < 2):
                    dve.wait_ge(c["t"], 4 * b - 4)
                d = sc[:, s, :].rearrange("p (h k) -> p h k", h=NH)
                for k, n in enumerate((6, 6, 4)):
                    last = nc.vector.tensor_tensor(d[:, 6 * k:6 * k + n, :], ps[:, k, 0:n * SK].rearrange("p (h k) -> p h k", h=n),
                                                   mask_add[:, :].unsqueeze(1).broadcast_to([P, n, SK]), ALU.add)
                last.then_inc(c["masked"], 1)
                dve.wait_ge(c["masked"], b + 1)
                nc.vector.tensor_reduce(smax[:, s, :], d, AX_X, ALU.max).then_inc(c["max"], 1)
                dve.wait_ge(c["max"], b + 1)
                nc.vector.tensor_tensor(d, d, smax[:, s, :].unsqueeze(2).broadcast_to([P, NH, SK]), ALU.subtract).then_inc(c["sub"], 1)

            def sums1(b, s):
                dve.wait_ge(c["exp"], b + 1)
                nc.vector.tensor_reduce(ssum[:, s, :], sc[:, s, :].rearrange("p (h k) -> p h k", h=NH), AX_X, ALU.add).then_inc(c["sum"], 1)
                dve.wait_ge(c["sum"], b + 1)
                nc.vector.reciprocal(rinv[:, s, :], ssum[:, s, :]).then_inc(c["rinv"], 1)

            def residual_and_norm1(i, s):
                b = 2 * i + s
                row = row_of(b)
                nc.vector.tensor_tensor(row, row, bo1[:, :], ALU.add).then_inc(c["wo_part"], 1)
                dve.wait_ge(c["wo"], b + 1)
                dve.wait_ge(c["wo_part"], b + 1)
                nc.vector.tensor_tensor(row, ps[:, 7, 0:D], row, ALU.add).then_inc(c["x"], 1)
                dve.drain()
                free = () if isinstance(i, int) and i == 0 else ((c["rt"], b - 1),)
                layernorm(dve, [row], [xf[:, s, :]], ln_f, free).then_inc(c["xf"], 1)

            def top_logit(b):
                dve.wait_ge(c["rl_moved"], b + 1)
                nc.vector.tensor_reduce(score[:, 0:1], logits1[:, bass.ds(b, 1), :].rearrange("p o e -> p (o e)"), AX_X, ALU.max).then_inc(c["top"], 1)

            def scale_rows(i, s):
                b = 2 * i + s
                dve.wait_ge(c["top_exp"], b + 1)
                nc.vector.tensor_scalar(score[:, 2:3], score[:, 1:2], 1.0, None, ALU.add).then_inc(c["score"], 1)
                dve.wait_ge(c["score"], 2 * b + 1)
                nc.vector.reciprocal(score[:, 3:4], score[:, 2:3]).then_inc(c["score"], 1)
                dve.wait_ge(c["score"], 2 * b + 2)
                if not (isinstance(i, int) and i == 0):
                    dve.wait_ge(xs_stored[s], 16 * i)
                nc.vector.tensor_scalar(xs[:, s, :], xf[:, s, :], score[:, 3:4], None, ALU.mult).then_inc(c["xs"], 1)

            def body1(i, first=False, last=False):
                b0, b1_ = 2 * i, 2 * i + 1
                subtract_max1(b1_, 1)
                if not last:
                    norm_inputs1(i + 1)
                sums1(b1_, 1)
                if not first:
                    top_logit(b0 - 1)
                    scale_rows(i - 1, 1)
                residual_and_norm1(i, 0)
                if not last:
                    subtract_max1(b0 + 2, 0)
                    sums1(b0 + 2, 0)
                top_logit(b0)
                scale_rows(i, 0)
                residual_and_norm1(i, 1)
                if last:
                    top_logit(b1_)
                    scale_rows(i, 1)

            dve.wait_ge(ld_small, 16 * SMALL_LOADS)
            nc.vector.tensor_scalar(mask_add[:, :], mask_in[:, :], 0.0, -3e38, ALU.is_equal, ALU.mult).then_inc(mask_step, 1)
            dve.wait_ge(mask_step, 1)
            none_left = rt_small[:, 0, 0:1]
            nc.vector.tensor_reduce(none_left, mask_add[:, :], AX_X, ALU.max).then_inc(mask_step, 1)
            dve.wait_ge(mask_step, 2)
            nc.vector.tensor_scalar(none_left, none_left, 10.0, None, ALU.mult).then_inc(mask_step, 1)
            dve.wait_ge(mask_step, 3)
            nc.vector.tensor_tensor(none_left, none_left, none_left, ALU.subtract).then_inc(mask_step, 1)
            dve.wait_ge(mask_step, 4)
            nc.vector.tensor_scalar(bo1[:, :], bo1[:, :], none_left, None, ALU.add).then_inc(mask_step, 1)
            dve.wait_ge(mask_step, 5)
            norm_inputs1(0)
            dve.wait_ge(ld_small, 16 * SMALL_LOADS)
            subtract_max1(0, 0)
            sums1(0, 0)
            body1(0, first=True)
            with dve.Fori(1, PAIRS - 1) as i:
                body1(i)
            body1(PAIRS - 1, last=True)

            dve.wait_ge(c["rl_moved"], NB)
            dve.wait_ge(c["t"], 4 * NB)
            nc.vector.tensor_scalar(ne_small[:, 3, :], iota[:, 0:NH], -1.0, float(NE1), ALU.mult, ALU.add).then_inc(order_set, 1)
            dve.wait_ge(order_set, 2)
            route(L1, logits1[:, :, :], ne_small[:, 3, 0:NE1])

            def shared(g):
                for k in range(4):
                    s = k % 2
                    dve.wait_ge(sh["act"], 4 * g + k + 1)
                    dve.wait_ge(sh["up"], 4 * g + k + 1)
                    if k == 0 and not (isinstance(g, int) and g == 0):
                        dve.wait_ge(sh["down"], g)
                    nc.vector.tensor_tensor(shared_h[:, k, :], ps[:, 2 * s + 1, :], shared_gate[:, s, :], ALU.mult).then_inc(sh["h"], 1)
                dve.wait_ge(sh["down"], g + 1)
                rows = x_res[:, bass.ds(GROUP * g, GROUP), :]
                nc.vector.tensor_tensor(rows, ps[:, 4, :].rearrange("p (b d) -> p b d", d=D), rows, ALU.add).then_inc(sh["added"], 1)

            for s in range(2):
                dve.wait_ge(xs_stored[s], 16 * PAIRS)
            shared(0)
            with dve.Fori(1, EARLY) as g:
                shared(g)
            experts(L1)
            with dve.Fori(EARLY, NB // GROUP) as g:
                shared(g)
            for g in range(NB // GROUP):
                dve.wait_ge(y1_loaded[g], 16 * GROUP)
                dve.wait_ge(sh["added"], g + 1)
                rows = x_res[:, g * GROUP:(g + 1) * GROUP, :]
                nc.vector.tensor_tensor(rows, rows, y1[:, g * GROUP:(g + 1) * GROUP, :],
                                        ALU.add).then_inc(final_done, 1)

        @block.tensor
        def _(pe):
            def transpose_inputs(i):
                pe.wait_ge(xh_done, i + 1)
                for s in range(2):
                    mm = nc.tensor.transpose(ps[:, 5, s * P:(s + 1) * P], xh[:, s, :], ident[:, :])
                mm.then_inc(xt_ready, 1)

            def queries(i, bank_free):
                pe.wait_ge(xt_done, i + 1)
                for n, bank in enumerate((6, 7, 5, 6)):
                    if bank_free[n]:
                        pe.wait_ge(*bank_free[n])
                    for c in (2 * n, 2 * n + 1):
                        mm = nc.tensor.matmul(ps[:, bank, (c % 2) * 256:(c % 2) * 256 + 256], wq0[:, c * P:(c + 1) * P], xhT[:, :],
                                              start=True, stop=True)
                    mm.then_inc(q_ready, 1)

            def keys(i):
                pe.wait_ge(cp_ready, i + 1)
                for n, (c0, c1, bank) in enumerate(((0, 3, 7), (3, 6, 5), (6, 8, 6))):
                    pe.wait_ge(q_done, 4 * i + n + 2)
                    for c in range(c0, c1):
                        o = (c - c0) * 2 * SK
                        mm = nc.tensor.matmul(ps[:, bank, o:o + 2 * SK], wk0[:, c * P:(c + 1) * P], cpair[:, :], start=True, stop=True)
                    mm.then_inc(k_ready, 1)

            def values(s, banks, bank_free):
                for n, bank in enumerate(banks):
                    pe.wait_ge(*bank_free[n])
                    nc.tensor.matmul(ps[0:SK, bank, :], cpair[:, s * SK:(s + 1) * SK], wv0[:, n * 512:(n + 1) * 512],
                                     start=True, stop=True).then_inc(v_ready, 1)

            def scores(b, s, i):
                pe.wait_ge(q_done, 4 * i + 4)
                pe.wait_ge(k_done, 3 * i + 3)
                if not (isinstance(b, int) and b == 0):
                    pe.wait_ge(sub_done, b)
                for c in range(C0):
                    o = (c % 3) * 2 * SK
                    mm = nc.tensor.matmul(ps[:, c // 3, o:o + 2 * SK], qT[:, c, s * P:(s + 1) * P], kbd[:, s, c, :], start=True, stop=True)
                mm.then_inc(s_ready, 1)

            def transpose_probs(b, s, g):
                if g == 0:
                    pe.wait_ge(p_done, b + 1)
                if g >= 2:
                    pe.wait_ge(pt_done, 4 * b + g - 1)
                for k in range(4):
                    h = 4 * g + k
                    mm = nc.tensor.transpose(ps[0:SK, TB + g % 2, k * P:(k + 1) * P], sc[:, s, h * SK:(h + 1) * SK], ident[:, :])
                mm.then_inc(t_ready, 1)

            def weigh_values(b, s, g):
                pe.wait_ge(pt_done, 4 * b + g + 1)
                for k in range(4):
                    h = 4 * g + k
                    lo = 64 * (h % 2)
                    o = ((h // 2) % 4) * P
                    mm = nc.tensor.matmul(ps[lo:lo + 64, 5 + g // 2, o:o + P], vv[:, s, h * DK0:(h + 1) * DK0],
                                          pT[:, g, k * P:(k + 1) * P], start=True, stop=True)
                if g % 2:
                    mm.then_inc(ot_ready, 1)

            def attend(b, s, bank5_free, bank6_free, router):
                transpose_probs(b, s, 0)
                transpose_probs(b, s, 1)
                pe.wait_ge(v_done, 2 * b + 2)
                pe.wait_ge(*bank5_free)
                weigh_values(b, s, 0)
                transpose_probs(b, s, 2)
                weigh_values(b, s, 1)
                if router is not None:
                    router_logits(router)
                transpose_probs(b, s, 3)
                pe.wait_ge(*bank6_free)
                weigh_values(b, s, 2)
                weigh_values(b, s, 3)

            def project(b, bank_free):
                if bank_free:
                    pe.wait_ge(*bank_free)
                pe.wait_ge(ot_done, 2 * b + 2)
                for c in range(C0):
                    mm = nc.tensor.matmul(ps[:, 7, 0:D], oT[:, c, :], wo0[:, c * D:(c + 1) * D], start=c == 0, stop=c == C0 - 1)
                mm.then_inc(wo_ready, 1)

            def transpose_rows(b, s, bank, bank_free):
                pe.wait_ge(*bank_free)
                pe.wait_ge(xf_done, b + 1)
                nc.tensor.transpose(ps[:, bank, 0:P], xf[:, s, :], ident[:, :]).then_inc(rt_ready, 1)

            def router_logits(b):
                pe.wait_ge(rt_done, b + 1)
                nc.tensor.matmul(ps[:, 7, 0:NE0], xfT[:, :], gw0[:, :], start=True, stop=True).then_inc(rl_ready, 1)

            def body(i, first=False, last=False):
                b0, b1 = 2 * i, 2 * i + 1
                scores(b1, 1, i)
                if not first:
                    transpose_rows(b0 - 1, 1, 7, (wo_done, b0))
                attend(b0, 0, (v_done, 2 * b1 + 1), (v_done, 2 * b1 + 2), None if first else b0 - 1)
                project(b0, (rl_done, b0) if not first else None)
                if not last:
                    pe.wait_ge(ot_done, 2 * b0 + 1)
                    transpose_inputs(i + 1)
                    queries(i + 1, [(ot_done, 2 * b0 + 2), (wo_done, b0 + 1), None, (q_done, 4 * i + 5)])
                    keys(i + 1)
                    values(0, (7, 5), [(k_done, 3 * i + 4), (k_done, 3 * i + 5)])
                    transpose_rows(b0, 0, 6, (k_done, 3 * i + 6))
                    scores(b0 + 2, 0, i + 1)
                    attend(b1, 1, (v_done, 2 * b0 + 6), (rt_done, b0 + 1), b0)
                else:
                    transpose_rows(b0, 0, 6, (ot_done, 2 * b0 + 2))
                    attend(b1, 1, (ot_done, 2 * b0 + 1), (rt_done, b0 + 1), b0)
                project(b1, (rl_done, b1))
                if not last:
                    values(1, (5, 6), [(ot_done, 2 * b1 + 1), (ot_done, 2 * b1 + 2)])
                else:
                    transpose_rows(b1, 1, 7, (wo_done, b1 + 1))
                    router_logits(b1)

            pe.wait_ge(ld["id"], 16)
            transpose_inputs(0)
            pe.wait_ge(ld["wq"], 32)
            queries(0, [None, None, None, (q_done, 1)])
            pe.wait_ge(ld["wk"], 32)
            keys(0)
            pe.wait_ge(ld["wv"], 32)
            values(0, (7, 5), [(k_done, 1), (k_done, 2)])
            scores(0, 0, 0)
            values(1, (5, 6), [(v_done, 2), (k_done, 3)])
            pe.wait_ge(ld["wo"], 32)
            pe.wait_ge(ld["gw"], 16)
            body(0, first=True)
            with pe.Fori(1, PAIRS - 1) as i:
                body(i)
            body(PAIRS - 1, last=True)

            def ranks(L):
                pe.wait_ge(L.mask_ready, 1)
                n = NB * L.ne
                nc.tensor.matmul(ps[:, 6, 0:n], tri, hold_mask[:, 0:n], start=True, stop=True).then_inc(L.rank_ready, 1)
                nc.tensor.matmul(ps[:, 7, 0:n], ones[:, :], hold_mask[:, 0:n], start=True, stop=True).then_inc(L.rank_ready, 1)

            def experts(L, up_w, down_w):
                w, chunks = L.width, L.width // P

                def turn_rows(j, t, i):
                    if past(j, 1):
                        pe.wait_ge(L.tx_done, j)
                    if t % HALF == 0:
                        pe.wait_ge(L.rows_loaded[t // HALF], 16 * (i + 1))
                    nc.tensor.transpose(ps[:, 4, 0:P], xg[:, t, :], ident[:, :]).then_inc(L.tx_ready, 1)

                def turn_hidden(j, s):
                    pe.wait_ge(L.h_done, j + 1)
                    if past(j, 2):
                        pe.wait_ge(L.th_done, j - 1)
                    for c in range(chunks):
                        mm = nc.tensor.transpose(ps[:, 5 + s, c * P:(c + 1) * P], hmul[:, s, c * P:(c + 1) * P], ident[:, :])
                    mm.then_inc(L.th_ready, 1)

                def down(j, s):
                    at = pe.value_load(L.down_at[0:1, bass.ds(j, 1)], min_val=0, max_val=(L.ne - 1) * w)
                    pe.wait_ge(L.th_done, j + 1)
                    if past(j, 1):
                        pe.wait_ge(L.y_done, j)
                    for c in range(chunks):
                        mm = nc.tensor.matmul(ps[:, 7, 0:D], hT[:, s, c * P:(c + 1) * P], down_w[:, bass.ds(at + c * D, D)],
                                              start=c == 0, stop=c == chunks - 1)
                    mm.then_inc(L.y_ready, 1)

                def body(i, first=False, last=False):
                    for t in range(TURN):
                        j, s = TURN * i + t, t % 2
                        if t < TURN - 1:
                            turn_rows(j + 1, t + 1, i)
                        elif not last:
                            turn_rows(j + 1, 0, i + 1)
                        at = pe.value_load(L.up_at[0:1, bass.ds(j, 1)], min_val=0, max_val=(L.ne - 1) * 2 * w)
                        pe.wait_ge(L.tx_done, j + 1)
                        if past(j, 2):
                            pe.wait_ge(L.h_done, j - 1)
                        nc.tensor.matmul(ps[:, 2 * s, 0:w], xgT[:, s, :], up_w[:, bass.ds(at, w)],
                                         start=True, stop=True).then_inc(L.gate_ready, 1)
                        if not (first and t == 0):
                            turn_hidden(j - 1, 1 - s)
                        nc.tensor.matmul(ps[:, 2 * s + 1, 0:w], xgT[:, s, :], up_w[:, bass.ds(at + w, w)],
                                         start=True, stop=True).then_inc(L.up_ready, 1)
                        if not (first and t == 0):
                            down(j - 1, 1 - s)

                pe.wait_ge(L.tiles_ready, 1)
                turn_rows(0, 0, 0)
                body(0, first=True)
                with pe.Fori(1, L.tiles // TURN - 1) as i:
                    body(i)
                body(L.tiles // TURN - 1, last=True)
                turn_hidden(L.tiles - 1, 1)
                down(L.tiles - 1, 1)

            pe.wait_ge(ld_small, 16 * SMALL_LOADS)
            pe.wait_ge(ones_set, 1)
            ranks(L0)
            pe.wait_ge(ld_moe0, 32)
            experts(L0, gu0, dn0)

            def transpose_inputs1(i):
                pe.wait_ge(c["xh"], i + 1)
                for s in range(2):
                    mm = nc.tensor.transpose(ps[:, 6, s * P:(s + 1) * P], xh[:, s, :], ident[:, :])
                mm.then_inc(c["xt"], 1)

            def queries_and_keys1(i):
                pe.wait_ge(c["xt_moved"], i + 1)
                nc.tensor.matmul(ps[:, 5, 0:2 * P], wq1, xhT[:, :], start=True, stop=True).then_inc(c["q"], 1)
                pe.wait_ge(cp_ready, PAIRS + i + 1)
                nc.tensor.matmul(ps[:, 7, 0:2 * SK], wk1, cpair[:, :], start=True, stop=True).then_inc(c["k"], 1)

            def values1(s, bank, bank_free):
                pe.wait_ge(*bank_free)
                nc.tensor.matmul(ps[0:SK, bank, 0:D], cpair[:, s * SK:(s + 1) * SK], wv1, start=True, stop=True).then_inc(c["v"], 1)

            def scores1(b, s):
                pe.wait_ge(c["k_masked"], b + 1)
                if not (isinstance(b, int) and b == 0):
                    pe.wait_ge(c["masked"], b)
                for k, n in enumerate((6, 6, 4)):
                    mm = nc.tensor.matmul(ps[:, k, 0:n * SK], q1T[:, s * P:(s + 1) * P], k1m[:, s, 6 * k * SK:(6 * k + n) * SK],
                                          start=True, stop=True)
                mm.then_inc(c["s"], 1)

            def transpose_probs1(b, s, g):
                if g == 0:
                    pe.wait_ge(c["p"], b + 1)
                if g >= 2:
                    pe.wait_ge(c["pt"], 4 * b + g - 1)
                for k in range(4):
                    h = 4 * g + k
                    mm = nc.tensor.transpose(ps[0:SK, TB + g % 2, k * P:(k + 1) * P], sc[:, s, h * SK:(h + 1) * SK], ident[:, :])
                mm.then_inc(c["t"], 1)

            def weigh_values1(b, s, g, bank):
                pe.wait_ge(c["pt"], 4 * b + g + 1)
                for k in range(4):
                    h = 4 * g + k
                    mm = nc.tensor.matmul(ps[:, bank, 0:P], v1m[:, s, h, :], pT[:, g, k * P:(k + 1) * P], start=h == 0, stop=h == NH - 1)
                if g == 3:
                    mm.then_inc(c["ot"], 1)

            def attend1(b, s, bank, bank_free, router):
                transpose_probs1(b, s, 0)
                transpose_probs1(b, s, 1)
                pe.wait_ge(c["v_spread"], b + 1)
                pe.wait_ge(*bank_free)
                weigh_values1(b, s, 0, bank)
                transpose_probs1(b, s, 2)
                weigh_values1(b, s, 1, bank)
                if router is not None:
                    router_logits1(router)
                transpose_probs1(b, s, 3)
                weigh_values1(b, s, 2, bank)
                weigh_values1(b, s, 3, bank)

            def project1(b, bank_free):
                if bank_free:
                    pe.wait_ge(*bank_free)
                pe.wait_ge(c["ot_moved"], b + 1)
                nc.tensor.matmul(ps[:, 7, 0:D], o1T, wo1, start=True, stop=True).then_inc(c["wo"], 1)

            def transpose_rows1(b, s, bank, bank_free):
                pe.wait_ge(*bank_free)
                pe.wait_ge(c["xf"], b + 1)
                nc.tensor.transpose(ps[:, bank, 0:P], xf[:, s, :], ident[:, :]).then_inc(c["rt"], 1)

            def router_logits1(b):
                pe.wait_ge(c["rt_moved"], b + 1)
                nc.tensor.matmul(ps[:, 7, 0:NE1], xfT[:, :], gw1[:, :], start=True, stop=True).then_inc(c["rl"], 1)

            def body1(i, first=False, last=False):
                b0, b1_ = 2 * i, 2 * i + 1
                scores1(b1_, 1)
                if not first:
                    transpose_rows1(b0 - 1, 1, 7, (c["x"], b0))
                attend1(b0, 0, 5, (c["v_moved"], b1_ + 1), None if first else b0 - 1)
                project1(b0, (c["rl_moved"], b0) if not first else (c["k_moved"], 1))
                if not last:
                    transpose_inputs1(i + 1)
                    pe.wait_ge(c["ot_moved"], b0 + 1)
                    pe.wait_ge(c["x"], b0 + 1)
                    queries_and_keys1(i + 1)
                    values1(0, 6, (c["xt_moved"], i + 2))
                    transpose_rows1(b0, 0, 5, (c["q_moved"], i + 2))
                    pe.wait_ge(c["q_moved"], i + 2)
                    scores1(b0 + 2, 0)
                    pe.wait_ge(c["k_moved"], i + 2)
                    attend1(b1_, 1, 6, (c["v_moved"], b0 + 3), b0)
                else:
                    transpose_rows1(b0, 0, 5, (c["ot_moved"], b0 + 1))
                    pe.wait_ge(c["x"], b0 + 1)
                    attend1(b1_, 1, 6, (c["ot_moved"], b0 + 1), b0)
                project1(b1_, (c["rl_moved"], b1_))
                if not last:
                    values1(1, 5, (c["rt_moved"], b0 + 1))
                else:
                    transpose_rows1(b1_, 1, 7, (c["x"], b1_ + 1))
                    router_logits1(b1_)

            pe.wait_ge(L0.y_done, L0.tiles)
            pe.wait_ge(L0.th_done, L0.tiles)
            pe.wait_ge(ld_small, 16 * SMALL_LOADS)
            transpose_inputs1(0)
            queries_and_keys1(0)
            values1(0, 6, (c["xt_moved"], 1))
            pe.wait_ge(c["q_moved"], 1)
            scores1(0, 0)
            values1(1, 5, (c["q_moved"], 1))
            body1(0, first=True)
            with pe.Fori(1, PAIRS - 1) as i:
                body1(i)
            body1(PAIRS - 1, last=True)

            ranks(L1)
            pe.wait_ge(ld_moe1, 16 * 5)

            def shared(g):
                rows = xT_all[:, bass.ds(g * GROUP * P, GROUP * P)]
                for k in range(4):
                    s = k % 2
                    if not (isinstance(g, int) and g == 0 and k < 2):
                        pe.wait_ge(sh["h"], 4 * g + k - 1)
                    nc.tensor.matmul(ps[:, 2 * s, :], shg[:, k * P:(k + 1) * P], rows, start=True, stop=True).then_inc(sh["gate"], 1)
                    nc.tensor.matmul(ps[:, 2 * s + 1, :], shu[:, k * P:(k + 1) * P], rows, start=True, stop=True).then_inc(sh["up"], 1)
                pe.wait_ge(sh["h"], 4 * g + 4)
                if not (isinstance(g, int) and g == 0):
                    pe.wait_ge(sh["added"], g)
                for t in range(GROUP):
                    for k in range(4):
                        mm = nc.tensor.matmul(ps[:, 4, t * D:(t + 1) * D], shared_h[:, k, t * P:(t + 1) * P], shd[:, k * D:(k + 1) * D],
                                              start=k == 0, stop=k == 3)
                mm.then_inc(sh["down"], 1)

            pe.wait_ge(c["rt_kept"], NB)
            shared(0)
            with pe.Fori(1, EARLY) as g:
                shared(g)
            pe.wait_ge(sh["added"], EARLY)
            experts(L1, gu1, dn1)
            pe.wait_ge(L1.tx_done, L1.tiles)
            pe.wait_ge(L1.h_done, L1.tiles)
            with pe.Fori(EARLY, NB // GROUP) as g:
                shared(g)


def lay_out(inputs):
    import numpy as np
    d = {k: np.asarray(v) for k, v in inputs.items()}
    iota = np.broadcast_to(np.arange(P, dtype=np.float32), (P, P))
    consts = np.concatenate([iota, np.triu(np.ones((P, P), np.float32), 1)], 1)
    turned = lambda w: np.ascontiguousarray(np.asarray(w).T)
    up = np.asarray(d["L0_ffn_gate_up_w"])
    down = np.asarray(d["L0_ffn_down_w"])
    return {
        "x": d["x"], "ctxT": np.ascontiguousarray(d["ctx_1024"].reshape(-1, D).T), "ident": np.eye(P, dtype=np.float32),
        "wq0": d["L0_xattn_Wq"], "bq0": np.ascontiguousarray(d["L0_xattn_bq"].reshape(C0, P).T),
        "wk0": d["L0_xattn_Wk"], "bk0": np.ascontiguousarray(d["L0_xattn_bk"].reshape(C0, P).T),
        "wv0": d["L0_xattn_Wv"], "bv0": d["L0_xattn_bv"], "wo0": d["L0_xattn_Wo"], "bo0": d["L0_xattn_bo"],
        "gw0": np.ascontiguousarray(d["L0_ffn_gate_w"].T), "consts": consts,
        "wq1": turned(d["L1_xattn_Wq"]), "wk1": turned(d["L1_xattn_Wk"]), "wv1": turned(d["L1_xattn_Wv"]),
        "wo1": turned(d["L1_xattn_Wo"]), "b1": np.ascontiguousarray(np.stack([d["L1_xattn_bq"], d["L1_xattn_bk"]], 1)),
        "bv1": d["L1_xattn_bv"], "bo1": d["L1_xattn_bo"], "gw1": turned(d["L1_ffn_router_w"]),
        "head_rows": np.repeat(np.eye(NH, dtype=np.float32), DK1, axis=0), "mask": d["mask_SxS2_ik0"],
        "gu1": np.ascontiguousarray(np.asarray(d["L1_ffn_gate_up_proj"]).transpose(1, 0, 2).reshape(D, -1)),
        "dn1": np.ascontiguousarray(np.asarray(d["L1_ffn_down_proj"]).transpose(1, 0, 2).reshape(P, -1)),
        "shg": turned(d["L1_ffn_shared_gate_w"]), "shu": turned(d["L1_ffn_shared_up_w"]),
        "shd": np.ascontiguousarray(np.asarray(d["L1_ffn_shared_down_w"]).reshape(D, 4, P).transpose(2, 1, 0).reshape(P, -1)),
        "gu0": np.ascontiguousarray(up.transpose(2, 0, 1).reshape(D, -1)),
        "dn0": np.ascontiguousarray(down.transpose(2, 0, 1).reshape(4, P, NE0, D).transpose(1, 2, 0, 3).reshape(P, -1)),
    }


def kernel(**inputs):
    import concourse.bacc as bacc
    from concourse.bass_utils import run_bass_kernel_spmd

    nc = bacc.Bacc("TRN2", target_bir_lowering=False, num_devices=1)
    arrays = lay_out(inputs)
    args = {n: nc.dram_tensor(f"in_{n}", v.shape, mybir.dt.from_np(v.dtype), kind="ExternalInput").ap() for n, v in arrays.items()}
    out = nc.dram_tensor("out_x", (NB, P, D), F32, kind="ExternalOutput").ap()
    build(nc, args, out)
    r = run_bass_kernel_spmd(nc, [{f"in_{n}": v for n, v in arrays.items()}], core_ids=[0])
    return r.results[0]["out_x"]
```

```python
from contextlib import ExitStack

import concourse.bass as bass
from concourse import mybir

F32 = mybir.dt.float32
I32 = mybir.dt.int32
BF16 = mybir.dt.bfloat16
ALU = mybir.AluOpType
ACT = mybir.ActivationFunctionType
AX_X = mybir.AxisListType.X

P = 128
NB = 32
SK = 77
D = 128
PAIRS = NB // 2
NH = 16
DK0 = 64
DK1 = D // NH
C0 = NH * DK0 // P
NE0 = 8
NE1 = 16
SF = 512
GROUP = 4
HALF_HEADS = NH // 2
EPS = 1e-5
SMALL_LOADS = 11
TURN = 8
HALF = TURN // 2
SCALE = 8
RL = 400
EARLY = 5
POOLED = 2
VALUE_BANKS = ((7, 3), (4, 5))
KEY_GROUPS = ((0, 3, 5), (3, 6, 6), (6, 8, 3))
RSQRT_MAGIC = float(0x5F3759DF)
TB = 3


def statistics(dve, srcs, scratch):
    n = len(srcs)
    stats, mv, v, h, y, t = scratch
    for k in range(n):
        dve.bn_stats(stats[:, k, :], srcs[k])
    dve.drain()
    for k in range(n):
        dve.bn_aggr(mv[:, k, :], stats[:, k, :])
    dve.drain()
    dve.tensor_scalar(v[:, 0:n], mv[:, 0:n, 1], EPS, None, ALU.add)
    dve.drain()


def layernorm(dve, srcs, dsts, scratch, before_write=()):
    n = len(srcs)
    stats, mv, v, h, y, t = scratch
    dve.tensor_scalar(h[:, 0:n], v[:, 0:n], -0.5, None, ALU.mult)
    dve.tensor_scalar(y[:, 0:n].bitcast(I32), v[:, 0:n].bitcast(I32), -0.5, RSQRT_MAGIC, ALU.mult, ALU.add)
    for _ in range(3):
        dve.drain()
        dve.tensor_tensor(t[:, 0:n], y[:, 0:n], y[:, 0:n], ALU.mult)
        dve.drain()
        dve.tensor_tensor(t[:, 0:n], t[:, 0:n], h[:, 0:n], ALU.mult)
        dve.drain()
        dve.scalar_tensor_tensor(out=y[:, 0:n], in0=t[:, 0:n], scalar=1.5, in1=y[:, 0:n], op0=ALU.add, op1=ALU.mult)
    dve.drain()
    for wait in before_write:
        dve.wait_ge(*wait)
    for k in range(n):
        last = dve.tensor_scalar(dsts[k], srcs[k], mv[:, k, 0:1], y[:, k:k + 1], ALU.subtract, ALU.mult)
    return last


def past(j, n):
    return not isinstance(j, int) or j >= n


class Experts:

    def __init__(self, nc, ctx, name, ne, slots, width, per_step):
        self.ne, self.slots, self.width = ne, slots, width
        self.rows = slots * NB * P
        self.tiles = self.rows // P + ne
        self.per_step = per_step
        self.steps = TURN // per_step
        assert self.tiles % TURN == 0 and self.tiles * P < 2 ** 24

        def sem(what):
            return ctx.enter_context(nc.semaphore(f"{name}_{what}"))

        def sb(what, shape, dt=F32):
            return ctx.enter_context(nc.sbuf_tensor(f"{name}_{what}", shape, dt))

        self.step = sem("route_step")
        self.mask_ready, self.rank_ready = sem("mask_ready"), sem("rank_ready")
        self.place_ready, self.tiles_ready = sem("place_ready"), sem("tiles_ready")
        self.zero_filled, self.rows_placed = sem("zero_filled"), sem("rows_placed")
        self.place = sb("place", [P, slots * NB], I32)
        self.weights_at = sb("weights_at", [P, self.tiles], I32)
        self.rows_loaded = [sem(f"rows_loaded{s}") for s in range(2)]
        self.rows_stored = [sem(f"rows_stored{s}") for s in range(2)]
        self.tx_ready, self.tx_done = sem("tx_ready"), sem("tx_done")
        self.gate_ready, self.up_ready = sem("gate_ready"), sem("up_ready")
        self.act_done, self.h_done = sem("act_done"), sem("h_done")
        self.th_ready, self.th_done = sem("th_ready"), [sem("th_done_dve"), sem("th_done_act")]
        self.y_ready, self.y_done = sem("y_ready"), sem("y_done")


def build(nc, a, out):
    with ExitStack() as ctx:
        def sb(name, shape, dt=F32):
            return ctx.enter_context(nc.sbuf_tensor(name, shape, dt))

        def sem(name):
            return ctx.enter_context(nc.semaphore(name))

        ps = ctx.enter_context(nc.psum_tensor("ps", [P, 8, 512], F32))
        x_res = sb("x_res", [P, NB, D])
        ctxT = sb("ctxT", [P, NB * SK])
        ident = sb("ident", [P, P])
        w0 = sb("w0", [P, 4, C0 * P])
        wq0, wk0, wv0, wo0 = (w0[:, k, :] for k in range(4))
        bq0 = sb("bq0", [P, C0])
        bk0 = sb("bk0", [P, C0])
        bv0 = sb("bv0", [P, C0])
        bo0 = sb("bo0", [P, D])
        gw0 = sb("gw0", [P, NE0])
        cpair = sb("cpair", [P, 2 * SK])
        xh = sb("xh", [P, 2, D])
        xT = sb("xT", [P, 4 * P])
        xhT, xfT = xT[:, 0:2 * P], xT[:, 2 * P:4 * P]
        qT = sb("qT", [P, C0, 2 * P])
        kbd = sb("kbd", [P, 2, C0, 2 * SK])
        vv = sb("vv", [SK, 2, C0 * P])
        sc = sb("sc", [P, 2, NH * SK])
        smax = sb("smax", [P, 2, NH])
        ssum = sb("ssum", [P, 2, NH])
        rinv = sb("rinv", [P, 2, NH])
        pT = sb("pT", [SK, 4, 4 * P])
        oT = sb("oT", [P, C0, P])
        xf = sb("xf", [P, 2, D])
        logits0 = sb("logits0", [P, NB, NE0])
        ln_a = (sb("lna_st", [P, 4, 6]), sb("lna_mv", [P, 4, 2]), *(sb(f"lna_{k}", [P, 4]) for k in "vhyt"))

        L0 = Experts(nc, ctx, "l0", NE0, 2, 512, 1)
        rows_all = sb("rows_all", [P, NB, D])
        zeros = sb("zeros", [P, D])
        xrows = nc.dram_tensor("xrows", (L0.tiles * P, D), F32, kind="Internal").ap()
        yrows = nc.dram_tensor("yrows", (L0.tiles * P, D), F32, kind="Internal").ap()
        gu0 = sb("gu0", [P, NE0 * 1024])
        dn0 = sb("dn0", [P, NE0 * 512])
        consts = sb("consts", [P, 2 * P])
        iota, tri = consts[:, 0:P], consts[:, P:2 * P]
        ones = sb("ones", [P, P])
        pair_place = sb("pair_place", [P, 2, 2], I32)
        topw = sb("topw", [P, 2, NB])
        rt_small = sb("rt_small", [P, 6, 2 * NB])
        rt_int = sb("rt_int", [P, 2 * NB], I32)
        ne_small = sb("ne_small", [P, 4, NH])
        w1 = sb("w1", [P, 4, D])
        wq1, wk1, wv1, wo1 = (w1[:, k, :] for k in range(4))
        b1 = sb("b1", [P, 2])
        bv1 = sb("bv1", [SK, D])
        bo1 = sb("bo1", [P, D])
        gw1 = sb("gw1", [P, NE1])
        mask_in = sb("mask_in", [P, SK], I32)
        mask_add = sb("mask_add", [P, SK])
        mask_heads = sb("mask_heads", [P, 6, SK], BF16)
        ident_bf = sb("ident_bf", [P, P], BF16)
        head_rows = sb("head_rows", [P, NH])
        q1T = qT[:, 0, :]
        k1T = qT[:, 1, 0:2 * SK]
        k1m = kbd[:, :, :, :].rearrange("p s c n -> p s (c n)")
        v1 = qT[0:SK, 2, 0:2 * P].rearrange("p (s d) -> p s d", s=2)
        v1m = gu0[0:SK, 0:2 * NH * D].rearrange("p (s h d) -> p s h d", s=2, h=NH)
        o1T = qT[:, 3, 0:P]
        logits1 = sb("logits1", [P, NB, NE1])
        xT_all = w0[:, :, :].rearrange("p a n -> p (a n)")
        y1 = gu0[:, 0:NB * D].rearrange("p (b d) -> p b d", d=D)
        gu1 = gu0[:, NB * D:NB * D + NE1 * 2 * D]
        dn1 = dn0[:, 0:NE1 * D]
        shg, shu, shd = (dn0[:, 2048 + k * SF:2048 + (k + 1) * SF] for k in range(3))
        shared_gate = sb("shared_gate", [P, 2, 512])
        shared_copy = sb("shared_copy", [P, 2, 512])
        shared_h = qT[:, :, :].rearrange("p c q -> p (c q)").rearrange("p (c n) -> p c n", c=4)
        L1 = Experts(nc, ctx, "l1", NE1, 1, D, 2)
        xrows1 = nc.dram_tensor("xrows1", (L1.tiles * P, D), F32, kind="Internal").ap()
        yrows1 = nc.dram_tensor("yrows1", (L1.tiles * P, D), F32, kind="Internal").ap()
        r_scratch = sc[:, :, :].rearrange("p s n -> p (s n)")
        xg = r_scratch[:, 0:TURN * D].rearrange("p (t d) -> p t d", d=D)
        ysb = r_scratch[:, TURN * D:2 * TURN * D].rearrange("p (t d) -> p t d", d=D)
        xgT = qT[:, 0:2, :]
        gact = qT[:, 2:6, :].rearrange("p (s a) n -> p s (a n)", s=2)
        hmul = kbd[:, 0, :, :].rearrange("p c n -> p (c n)")[:, 0:1024].rearrange("p (s n) -> p s n", s=2)
        hT = kbd[:, 1, :, :].rearrange("p c n -> p (c n)")[:, 0:1024].rearrange("p (s n) -> p s n", s=2)
        hold_mask = sb("hold_mask", [P, NB * NH])
        yin = oT[:, 0:4, :].rearrange("p (s k) d -> p s k d", s=2)

        ld = {k: sem("ld_" + k) for k in ("x0", "x", "ctx", "id", "wq", "wk", "wv", "wo", "gw")}
        kz = sem("kbd_zeroed")
        cp_ready = sem("cpair_ready")
        xh_done, xt_ready, xt_done = sem("xh_done"), sem("xt_ready"), sem("xt_done")
        q_ready, q_done = sem("q_ready"), sem("q_done")
        k_ready, k_done = sem("k_ready"), sem("k_done")
        v_ready, v_done = sem("v_ready"), sem("v_done")
        s_ready, max_done, sub_done = sem("s_ready"), sem("max_done"), sem("sub_done")
        exp_done, sum_done, rinv_done, p_done = sem("exp_done"), sem("sum_done"), sem("rinv_done"), sem("p_done")
        t_ready, pt_done = sem("t_ready"), sem("pt_done")
        ot_ready, ot_done = sem("ot_ready"), sem("ot_done")
        wo_ready, wo_part, wo_done = sem("wo_ready"), sem("wo_part"), sem("wo_done")
        xf_stored = sem("xf_stored")
        bias_spread, bias_ready, bias_added = sem("bias_spread"), sem("bias_ready"), sem("bias_added")
        rl_ready, rl_done = sem("rl_ready"), sem("rl_done")
        out_done = sem("out_done")
        ld_moe0 = sem("ld_moe0")
        ones_set = sem("ones_set")
        order_set = sem("order_set")
        w_sub, w_exp = sem("w_sub"), sem("w_exp")
        yin_loaded = [sem(f"yin_loaded{s}") for s in range(2)]
        comb_part, comb_done = sem("comb_part"), sem("comb_done")
        zeros_set, pair_place_ready = sem("zeros_set"), sem("pair_place_ready")
        ld_small, ld_moe1 = sem("ld_small"), sem("ld_moe1")
        mask_step, v1z = sem("mask_step"), sem("v1m_zeroed")
        c = {k: sem("c_" + k) for k in (
            "xh", "xt", "xt_moved", "xt_kept", "q", "q_moved", "k", "k_moved", "k_masked", "v", "v_moved", "v_spread", "s", "max", "sub",
            "exp", "sum", "rinv", "p", "t", "pt", "ot", "ot_moved", "wo", "wo_part", "x", "rl", "rl_moved", "stored")}
        top_exp, rows_scaled = sem("top_exp"), sem("rows_scaled")
        sh = {k: sem("sh_" + k) for k in ("gate", "up", "act", "h", "down", "added")}
        y1_loaded, final_done = [sem(f"y1_loaded{g}") for g in range(NB // GROUP)], sem("final_done")

        block = ctx.enter_context(nc.Block())

        @block.sync
        def _(sp):
            x_tiles = a["x"].rearrange("b s d -> s b d")
            sp.dma_start(x_res[:, 0:2, :], x_tiles[:, 0:2, :]).then_inc(ld["x0"], 16)
            sp.dma_start(ident[:, :], a["ident"]).then_inc(ld["id"], 16)
            sp.dma_start(wq0, a["wq0"]).then_inc(ld["wq"], 16)
            sp.dma_start(bq0[:, :], a["bq0"]).then_inc(ld["wq"], 16)
            sp.dma_start(ctxT[:, :], a["ctxT"]).then_inc(ld["ctx"], 16)
            sp.dma_start(wk0, a["wk0"]).then_inc(ld["wk"], 16)
            sp.dma_start(bk0[:, :], a["bk0"]).then_inc(ld["wk"], 16)
            sp.dma_start(wv0, a["wv0"]).then_inc(ld["wv"], 16)
            sp.dma_start(bv0[:, :], a["bv0"]).then_inc(ld["wv"], 16)
            sp.dma_start(x_res[:, 2:NB, :], x_tiles[:, 2:NB, :]).then_inc(ld["x"], 16)
            sp.dma_start(wo0.rearrange("p (c n) -> p c n", c=C0), a["wo0"].rearrange("(c p) n -> p c n", p=P)).then_inc(ld["wo"], 16)
            sp.dma_start(bo0[:, :], a["bo0"].rearrange("(o n) -> o n", o=1).broadcast_to([P, D])).then_inc(ld["wo"], 16)
            sp.dma_start(gw0[:, :], a["gw0"]).then_inc(ld["gw"], 16)
            sp.dma_start(consts[:, :], a["consts"]).then_inc(ld_small, 16)
            sp.dma_start(gu0[:, :], a["gu0"]).then_inc(ld_moe0, 16)
            sp.dma_start(dn0[:, :], a["dn0"]).then_inc(ld_moe0, 16)
            for k, name in enumerate(("wq1", "wk1", "wv1", "wo1")):
                sp.dma_start(w1[:, k, :], a[name]).then_inc(ld_small, 16)
            sp.dma_start(b1[:, :], a["b1"]).then_inc(ld_small, 16)
            sp.dma_start(bv1[:, :], a["bv1"].rearrange("(o n) -> o n", o=1).broadcast_to([SK, D])).then_inc(ld_small, 16)
            sp.dma_start(bo1[:, :], a["bo1"].rearrange("(o n) -> o n", o=1).broadcast_to([P, D])).then_inc(ld_small, 16)
            sp.dma_start(gw1[:, :], a["gw1"]).then_inc(ld_small, 16)
            sp.dma_start(head_rows[:, :], a["head_rows"]).then_inc(ld_small, 16)
            sp.dma_start(mask_in[:, :], a["mask"]).then_inc(ld_small, 16)
            sp.wait_ge(zeros_set, 1)
            for L, rows in ((L0, xrows), (L1, xrows1)):
                sp.dma_start(rows.rearrange("(t p) d -> p t d", p=P),
                             zeros[:, :].unsqueeze(1).broadcast_to([P, L.tiles, D])).then_inc(L.zero_filled, 16)

            with sp.Fori(0, PAIRS) as i:
                sp.wait_ge(xh_done, i + 3)
                sp.dma_start(rows_all[:, bass.ds(2 * i, 2), :], xf[:, :, :]).then_inc(xf_stored, 16)

            def move_tiles(L, xrows, yrows):
                def tiles_of(rows, g):
                    return rows[bass.ds(g * HALF * P, HALF * P), :].rearrange("(t p) d -> p t d", p=P)

                def load(g, h):
                    sp.dma_start(xg[:, h * HALF:(h + 1) * HALF, :], tiles_of(xrows, g)).then_inc(L.rows_loaded[h], 16)

                def body(i, last=False):
                    for h in range(2):
                        g = 2 * i + h
                        if not last:
                            sp.wait_ge(L.tx_ready, L.steps // 2 * (g + 1))
                            load(g + 2, h)
                        sp.wait_ge(L.y_done, L.steps // 2 * (g + 1))
                        sp.dma_start(tiles_of(yrows, g), ysb[:, h * HALF:(h + 1) * HALF, :]).then_inc(L.rows_stored[h], 16)

                sp.wait_ge(L.tiles_ready, 1)
                sp.wait_ge(L.rows_placed, 16 * L.slots * NB)
                load(0, 0)
                load(1, 1)
                with sp.Fori(0, L.tiles // TURN - 1) as i:
                    body(i)
                body(L.tiles // TURN - 1, last=True)
                for h in range(2):
                    sp.wait_ge(L.rows_stored[h], 16 * L.tiles // TURN)

            move_tiles(L0, xrows, yrows)
            sp.wait_ge(comb_done, 6)
            sp.dma_start(gu1, a["gu1"]).then_inc(ld_moe1, 16)
            sp.dma_start(dn1, a["dn1"]).then_inc(ld_moe1, 16)
            for weights, name in ((shg, "shg"), (shu, "shu"), (shd, "shd")):
                sp.dma_start(weights, a[name]).then_inc(ld_moe1, 16)
            with sp.Fori(0, PAIRS) as i:
                sp.wait_ge(c["xh"], i + 4)
                sp.dma_start(rows_all[:, bass.ds(2 * i, 2), :], xf[:, :, :]).then_inc(c["stored"], 16)

            move_tiles(L1, xrows1, yrows1)
            for g in range(NB // GROUP):
                sp.wait_ge(final_done, g + 1)
                sp.dma_start(out[g * GROUP:(g + 1) * GROUP].rearrange("b s d -> s b d"),
                             x_res[:, g * GROUP:(g + 1) * GROUP, :]).then_inc(out_done, 16)
            sp.wait_ge(out_done, 16 * NB // GROUP)

        @block.gpsimd
        def _(pool):
            nc.gpsimd.memset(kbd[:, :, :, :], 0.0).then_inc(kz, 1)
            nc.gpsimd.memset(zeros[:, :], 0.0).then_inc(zeros_set, 1)
            nc.gpsimd.memset(ones[:, :], 1.0).then_inc(ones_set, 1)

            def copy_contexts(i):
                nc.gpsimd.tensor_copy(cpair[:, :], ctxT[:, bass.ds(i * 2 * SK, 2 * SK)]).then_inc(cp_ready, 1)

            def normalise(b, s):
                pool.wait_ge(rinv_done, b + 1)
                for k in range(2):
                    p = sc[:, s, k * HALF_HEADS * SK:(k + 1) * HALF_HEADS * SK].rearrange("p (h k) -> p h k", h=HALF_HEADS)
                    nc.gpsimd.tensor_tensor(p, p, rinv[:, s, k * HALF_HEADS:(k + 1) * HALF_HEADS].unsqueeze(2)
                                            .broadcast_to([P, HALF_HEADS, SK]), ALU.mult).then_inc(p_done, 1)

            pool.wait_ge(ld["ctx"], 16)
            copy_contexts(0)
            normalise(0, 0)
            with pool.Fori(0, PAIRS - 1) as i:
                pool.wait_ge(v_ready, 4 * i + 4)
                copy_contexts(i + 1)
                normalise(2 * i + 1, 1)
                normalise(2 * i + 2, 0)
            normalise(NB - 1, 1)

            def place_rows(L, xrows, scaled=None):
                pool.wait_ge(L.zero_filled, 16)
                pool.wait_ge(L.place_ready, 1)
                for n in range(L.slots * NB):
                    if scaled is not None and n % SCALE == 0:
                        pool.wait_ge(scaled, n // SCALE + 1)
                    nc.gpsimd.indirect_dma_start(xrows, bass.IndirectOffsetOnAxis(L.place[:, n:n + 1], 0), rows_all[:, n % NB, :],
                                                 None).then_inc(L.rows_placed, 16)

            pool.wait_ge(xf_stored, 16 * PAIRS)
            place_rows(L0, xrows)

            def copy_contexts1(i):
                nc.gpsimd.tensor_copy(cpair[:, :], ctxT[:, bass.ds(i * 2 * SK, 2 * SK)]).then_inc(cp_ready, 1)

            def mask_keys(b, i, s):
                pool.wait_ge(c["k_moved"], i + 1)
                if not (isinstance(b, int) and b < 2):
                    pool.wait_ge(c["s"], b - 1)
                nc.gpsimd.tensor_tensor(k1m[:, s, :].rearrange("p (h k) -> p h k", h=NH),
                                        k1T[:, s * SK:(s + 1) * SK].unsqueeze(1).broadcast_to([P, NH, SK]),
                                        head_rows[:, :].unsqueeze(2).broadcast_to([P, NH, SK]), ALU.mult).then_inc(c["k_masked"], 1)

            def spread_values(b, i, s):
                if not (isinstance(b, int) and b < 2):
                    pool.wait_ge(c["ot"], b - 1)
                pool.wait_ge(c["v_moved"], i + 1)
                flat = v1m[:, s, :, :].rearrange("p h d -> p (h d)")
                blocks = bass.AP(flat.tensor, flat.offset, [list(flat.ap[0]), [D + DK1, NH], [1, DK1]])
                nc.gpsimd.tensor_tensor(blocks, v1[:, s, :].rearrange("p (h d) -> p h d", h=NH),
                                        bv1[:, :].rearrange("p (h d) -> p h d", h=NH), ALU.add).then_inc(c["v_spread"], 1)

            def normalise1(b, s):
                pool.wait_ge(c["rinv"], b + 1)
                for k in range(2):
                    p = sc[:, s, k * HALF_HEADS * SK:(k + 1) * HALF_HEADS * SK].rearrange("p (h k) -> p h k", h=HALF_HEADS)
                    nc.gpsimd.tensor_tensor(p, p, rinv[:, s, k * HALF_HEADS:(k + 1) * HALF_HEADS].unsqueeze(2)
                                            .broadcast_to([P, HALF_HEADS, SK]), ALU.mult).then_inc(c["p"], 1)

            def fetch_results(i, s):
                if not (isinstance(i, int) and i == 0):
                    pool.wait_ge(comb_done, 2 * i + s - 1)
                copied = 2 * i + s + 1 if isinstance(i, int) else pool.to_reg(2 * i + s + 1)
                nc.gpsimd.tensor_copy(pair_place[:, s, :].unsqueeze(1),
                                      L0.place[:, :].rearrange("p (k b) -> p b k", k=2)[:, bass.ds(2 * i + s, 1), :]
                                      ).then_inc(pair_place_ready, 1)
                pool.wait_ge(L0.rows_stored[0], 16 * L0.tiles // TURN)
                pool.wait_ge(pair_place_ready, copied)
                for k in range(2):
                    nc.gpsimd.indirect_dma_start(yin[:, s, k, :], None, yrows,
                                                 bass.IndirectOffsetOnAxis(pair_place[:, s, k:k + 1], 0)).then_inc(yin_loaded[s], 16)

            for h in range(2):
                pool.wait_ge(L0.rows_stored[h], 16 * L0.tiles // TURN)
            fetch_results(0, 0)
            fetch_results(0, 1)
            nc.gpsimd.memset(v1m[:, :, :, :], 0.0).then_inc(v1z, 1)
            pool.wait_ge(v1z, 1)
            copy_contexts1(0)
            pool.wait_ge(ld_small, 16 * SMALL_LOADS)
            mask_keys(0, 0, 0)
            mask_keys(1, 0, 1)
            fetch_results(1, 0)
            fetch_results(1, 1)
            spread_values(0, 0, 0)
            pool.wait_ge(c["v"], 1)
            copy_contexts1(1)
            fetch_results(2, 0)
            fetch_results(2, 1)
            normalise1(0, 0)
            spread_values(1, 0, 1)

            def body1(i, last=False, fetch=True, copy=True):
                b0, b1 = 2 * i, 2 * i + 1
                if fetch:
                    fetch_results(i + 3, 0)
                if not last:
                    mask_keys(b0 + 2, i + 1, 0)
                normalise1(b1, 1)
                if fetch:
                    fetch_results(i + 3, 1)
                if copy:
                    pool.wait_ge(c["v"], i + 2)
                    copy_contexts1(i + 2)
                if not last:
                    mask_keys(b1 + 2, i + 1, 1)
                    spread_values(b0 + 2, i + 1, 0)
                    normalise1(b0 + 2, 0)
                    spread_values(b1 + 2, i + 1, 1)

            body1(0)
            with pool.Fori(1, PAIRS - 3) as i:
                body1(i)
            body1(PAIRS - 3, fetch=False)
            body1(PAIRS - 2, fetch=False, copy=False)
            body1(PAIRS - 1, last=True, fetch=False, copy=False)

            for g in range(POOLED):
                for k in range(4):
                    pool.wait_ge(sh["act"], 4 * g + k + 1)
                    if k == 0 and g:
                        pool.wait_ge(sh["down"], g)
                    nc.gpsimd.tensor_tensor(shared_h[:, k, :], shared_copy[:, k % 2, :], shared_gate[:, k % 2, :],
                                            ALU.mult).then_inc(sh["h"], 1)
            place_rows(L1, xrows1, rows_scaled)
            for h in range(2):
                pool.wait_ge(L1.rows_stored[h], 16 * L1.tiles // TURN)
            for b in range(NB):
                nc.gpsimd.indirect_dma_start(y1[:, b, :], None, yrows1, bass.IndirectOffsetOnAxis(L1.place[:, b:b + 1], 0)
                                             ).then_inc(y1_loaded[b // GROUP], 16)

        @block.scalar
        def _(act):
            def move_xT(turn, lo=0, hi=4):
                act.wait_ge(xt_ready, turn + 1)
                nc.scalar.copy(xT[:, lo * P:hi * P], ps[:, 4, lo * P:hi * P]).then_inc(xt_done, 1)

            def move_q(i):
                for n, bank in enumerate((7, 5, 6, 7)):
                    act.wait_ge(q_ready, 4 * i + n + 1)
                    for c in (2 * n, 2 * n + 1):
                        last = nc.scalar.activation(qT[:, c, :], ps[:, bank, (c % 2) * 256:(c % 2) * 256 + 256], ACT.Identity,
                                                    bias=bq0[:, c:c + 1])
                    last.then_inc(q_done, 1)

            def move_v(b, s, parts=(0, 1)):
                if not (isinstance(b, int) and b < 2):
                    act.wait_ge(ot_ready, 2 * b - 2)
                for n in parts:
                    bank = VALUE_BANKS[s][n]
                    act.wait_ge(v_ready, 2 * b + n + 1)
                    nc.scalar.copy(vv[:, s, n * 512:(n + 1) * 512], ps[0:SK, bank, :]).then_inc(v_done, 1)

            def move_pT(b, g):
                act.wait_ge(t_ready, 4 * b + g + 1)
                nc.scalar.copy(pT[:, g, :], ps[0:SK, TB + g % 2, :]).then_inc(pt_done, 1)

            def move_oT(b, half):
                act.wait_ge(ot_ready, 2 * b + half + 1)
                if not (isinstance(b, int) and b == 0) and half == 0:
                    act.wait_ge(wo_ready, b)
                nc.scalar.copy(oT[:, 4 * half:4 * half + 4, :].rearrange("p c q -> p (c q)"), ps[:, 5 + half, :]).then_inc(ot_done, 1)

            def exponentials(b, s):
                act.wait_ge(sub_done, b + 1)
                nc.scalar.activation(sc[:, s, :], sc[:, s, :], ACT.Exp, scale=float(DK0) ** -0.5).then_inc(exp_done, 1)

            def body(i, first=False, last=False):
                b0, b1 = 2 * i, 2 * i + 1
                move_pT(b0, 0)
                move_pT(b0, 1)
                move_pT(b0, 2)
                move_oT(b0, 0)
                move_pT(b0, 3)
                move_oT(b0, 1)
                move_xT(i + 1, 2 if last else 0, 2 if first else 4)
                exponentials(b1, 1)
                if not last:
                    move_q(i + 1)
                move_pT(b1, 0)
                move_pT(b1, 1)
                if not last:
                    move_v(b0 + 2, 0, (0,))
                move_pT(b1, 2)
                move_oT(b1, 0)
                move_pT(b1, 3)
                if not last:
                    exponentials(b0 + 2, 0)
                move_oT(b1, 1)
                if not last:
                    move_v(b0 + 2, 0, (1,))
                    move_v(b1 + 2, 1)

            act.wait_ge(ld["wq"], 32)
            move_xT(0, 0, 2)
            move_q(0)
            move_v(0, 0)
            exponentials(0, 0)
            move_v(1, 1)
            body(0, first=True)
            with act.Fori(1, PAIRS - 1) as i:
                body(i)
            body(PAIRS - 1, last=True)
            move_xT(PAIRS + 1, 2, 4)

            def experts(L, func):
                m, w = L.per_step, L.per_step * L.width
                half = w // 2

                def move_xT(j, s):
                    act.wait_ge(L.tx_ready, j + 1)
                    if past(j, 2):
                        act.wait_ge(L.up_ready, j - 1)
                    nc.scalar.copy(xgT[:, s, 0:m * P], ps[:, 4, 0:m * P]).then_inc(L.tx_done, 1)

                def gate(j, s):
                    act.wait_ge(L.gate_ready, j + 1)
                    if past(j, 2):
                        act.wait_ge(L.h_done, j - 1)
                    nc.scalar.activation(gact[:, s, 0:w], ps[:, 2 * s, 0:w], func).then_inc(L.act_done, 1)

                def move_hT(j, s):
                    act.wait_ge(L.th_ready, j + 1)
                    if past(j, 2):
                        act.wait_ge(L.y_ready, j - 1)
                    nc.scalar.copy(hT[:, s, half:w], ps[:, 6, 0:half]).then_inc(L.th_done[1], 1)

                def move_y(j, t, i):
                    act.wait_ge(L.y_ready, j + 1)
                    if t * m % HALF == 0 and past(i, 1):
                        act.wait_ge(L.rows_stored[t * m // HALF], 16 * i)
                    nc.scalar.copy(ysb[:, t * m:(t + 1) * m, :], ps[:, 7, 0:m * D].rearrange("p (t d) -> p t d", d=D)).then_inc(L.y_done, 1)

                def body(i, first=False, last=False):
                    for t in range(L.steps):
                        j = L.steps * i + t
                        gate(j, t % 2)
                        if not (first and t == 0):
                            move_hT(j - 1, (t - 1) % 2)
                        if not (last and t == L.steps - 1):
                            move_xT(j + 1, (t + 1) % 2)
                        if t:
                            move_y(j - 1, t - 1, i)
                        elif not first:
                            move_y(j - 1, L.steps - 1, i - 1)

                move_xT(0, 0)
                body(0, first=True)
                with act.Fori(1, L.tiles // TURN - 1) as i:
                    body(i)
                body(L.tiles // TURN - 1, last=True)
                move_hT(L.tiles // m - 1, 1)
                move_y(L.tiles // m - 1, L.steps - 1, L.tiles // TURN - 1)

            act.wait_ge(w_sub, 1)
            nc.scalar.activation(rt_small[:, 3, 0:NB], rt_small[:, 3, 0:NB], ACT.Exp)
            shifted = r_scratch[:, (L0.slots + 1) * NB * NE0:(L0.slots + 2) * NB * NE0]
            nc.scalar.activation(shifted, shifted, ACT.Exp).then_inc(w_exp, 1)
            experts(L0, ACT.Gelu)

            def move1(ready, count, dst, src, done, bias=None):
                act.wait_ge(ready, count)
                if bias is None:
                    nc.scalar.copy(dst, src).then_inc(done, 1)
                else:
                    nc.scalar.activation(dst, src, ACT.Identity, bias=bias).then_inc(done, 1)

            def move_xT1(turn, inputs=True, results=True):
                lo, hi = 0 if inputs else 2, 4 if results else 2
                act.wait_ge(c["xt"], turn + 1)
                nc.scalar.copy(xT[:, lo * P:hi * P], ps[:, 4, lo * P:hi * P]).then_inc(c["xt_moved"], 1)

            def keep_xT(i):
                act.wait_ge(c["xt_moved"], i + 4)
                nc.scalar.copy(xT_all[:, bass.ds(i * 2 * P, 2 * P)], xfT).then_inc(c["xt_kept"], 1)

            def move_logits1(i):
                move1(c["rl"], i + 1, logits1[:, bass.ds(2 * i, 2), :], ps[:, 5, RL:RL + 2 * NE1].rearrange("p (b e) -> p b e", e=NE1),
                      c["rl_moved"])

            def move_q1(i):
                move1(c["q"], i + 1, q1T, ps[:, 5, 0:2 * P], c["q_moved"], b1[:, 0:1])

            def move_k1(i):
                if not (isinstance(i, int) and i == 0):
                    act.wait_ge(c["k_masked"], 2 * i)
                move1(c["k"], i + 1, k1T, ps[:, 6, 0:2 * SK], c["k_moved"], b1[:, 1:2])

            def move_v1(i):
                if not (isinstance(i, int) and i == 0):
                    act.wait_ge(c["v_spread"], 2 * i)
                move1(c["v"], i + 1, v1[:, :, :].rearrange("p s d -> p (s d)"), ps[0:SK, 6, 0:2 * D], c["v_moved"])

            def move_pT1(b, g):
                move1(c["t"], 4 * b + g + 1, pT[:, g, :], ps[0:SK, TB + g % 2, :], c["pt"])

            def exponentials1(b, s):
                act.wait_ge(c["sub"], b + 1)
                nc.scalar.activation(sc[:, s, :], sc[:, s, :], ACT.Exp, scale=float(DK1) ** -0.5).then_inc(c["exp"], 1)

            def move_oT1(b, bank):
                if not (isinstance(b, int) and b == 0):
                    act.wait_ge(c["wo"], b)
                move1(c["ot"], b + 1, o1T, ps[:, bank, 0:P], c["ot_moved"])

            def body1(i, results=True, last=False):
                b0, b1_ = 2 * i, 2 * i + 1
                move_pT1(b0, 0)
                move_pT1(b0, 1)
                if not last:
                    move_k1(i + 1)
                move_pT1(b0, 2)
                exponentials1(b1_, 1)
                move_pT1(b0, 3)
                move_oT1(b0, 5)
                move_xT1(i + 1, inputs=not last, results=results)
                if not last:
                    move_v1(i + 1)
                    move_q1(i + 1)
                if results:
                    move_logits1(i - 2)
                move_pT1(b1_, 0)
                move_pT1(b1_, 1)
                if results:
                    keep_xT(i - 2)
                move_pT1(b1_, 2)
                move_pT1(b1_, 3)
                if not last:
                    exponentials1(b0 + 2, 0)
                move_oT1(b1_, 6)

            move_k1(0)
            move_xT1(0, results=False)
            move_q1(0)
            move_v1(0)
            exponentials1(0, 0)
            body1(0, results=False)
            body1(1, results=False)
            with act.Fori(2, PAIRS - 1) as i:
                body1(i)
            body1(PAIRS - 1, last=True)
            for i in (PAIRS - 2, PAIRS - 1):
                act.wait_ge(c["xt_kept"], i)
                move_xT1(i + 3, inputs=False)
                keep_xT(i)
                move_logits1(i)

            act.wait_ge(L1.step, 1)
            nc.scalar.activation(rt_small[:, 3, 0:NB], rt_small[:, 0, 0:NB], ACT.Exp, scale=-1.0).then_inc(top_exp, 1)

            def shared(g, pooled=False):
                for k in range(4):
                    s = k % 2
                    act.wait_ge(sh["gate"], 4 * g + k + 1)
                    if not (isinstance(g, int) and g == 0 and k < 2):
                        act.wait_ge(sh["h"], 4 * g + k - 1)
                    if pooled:
                        nc.scalar.activation(shared_gate[:, s, :], ps[:, 2 * s, :], ACT.Silu)
                        act.wait_ge(sh["up"], 4 * g + k + 1)
                        nc.scalar.copy(shared_copy[:, s, :], ps[:, 2 * s + 1, :]).then_inc(sh["act"], 1)
                    else:
                        nc.scalar.activation(shared_gate[:, s, :], ps[:, 2 * s, :], ACT.Silu).then_inc(sh["act"], 1)

            for g in range(POOLED):
                shared(g, pooled=True)
            with act.Fori(POOLED, EARLY) as g:
                shared(g)
            act.wait_ge(sh["down"], EARLY)
            experts(L1, ACT.Silu)
            with act.Fori(EARLY, NB // GROUP) as g:
                shared(g)

        @block.vector
        def _(dve):
            def row_of(b):
                return x_res[:, bass.ds(b, 1), :].rearrange("p o d -> p (o d)")

            def norm_rows(turn, inputs=True, results=True, second=False):
                rows, dsts = [], []
                if inputs:
                    rows += [row_of(2 * turn + s) for s in range(2)]
                    dsts += [xh[:, s, :] for s in range(2)]
                if results:
                    rows += [row_of(2 * turn - 4 + s) for s in range(2)]
                    dsts += [xf[:, s, :] for s in range(2)]
                free = []
                if not (isinstance(turn, int) and turn == 0):
                    free.append((xt_ready, turn))
                if results and not second:
                    free.append((xf_stored, 16 * (turn - 2)))
                statistics(dve, rows, ln_a)
                layernorm(dve, rows, dsts, ln_a, free).then_inc(xh_done, 1)

            def move_logits(i):
                nc.vector.tensor_copy(logits0[:, bass.ds(2 * i, 2), :], ps[:, 4, 0:2 * NE0].rearrange("p (b e) -> p b e", e=NE0)
                                      ).then_inc(rl_done, 1)

            def move_k(i, parts=(0, 1, 2)):
                for n in parts:
                    c0, c1, bank = KEY_GROUPS[n]
                    dve.wait_ge(k_ready, 3 * i + n + 1)
                    m = c1 - c0
                    for half in range(2):
                        lo = 64 * half
                        for s in range(2):
                            src = ps[lo:lo + 64, bank, 0:m * 2 * SK].rearrange("p (c s k) -> p c s k", c=m, s=2)[:, :, s, :]
                            last = nc.vector.tensor_tensor(kbd[lo:lo + 64, s, c0:c1, half * SK:(half + 1) * SK], src,
                                                           bk0[lo:lo + 64, c0:c1].unsqueeze(2).broadcast_to([64, m, SK]), ALU.add)
                    last.then_inc(k_done, 1)

            def subtract_max(b, s):
                dve.wait_ge(s_ready, b + 1)
                if not (isinstance(b, int) and b < 2):
                    dve.wait_ge(t_ready, 4 * b - 4)
                lo = ps[:, 0:2, 0:6 * SK].rearrange("p a (h k) -> p a h k", h=6)
                hi = ps[:, 2, 0:4 * SK].rearrange("p (h k) -> p h k", h=4)
                nc.vector.tensor_reduce(smax[:, s, 0:12].rearrange("p (a h) -> p a h", a=2), lo, AX_X, ALU.max)
                nc.vector.tensor_reduce(smax[:, s, 12:16], hi, AX_X, ALU.max).then_inc(max_done, 1)
                dve.wait_ge(max_done, b + 1)
                d = sc[:, s, :].rearrange("p (h k) -> p h k", h=NH)
                for k in range(2):
                    nc.vector.tensor_tensor(d[:, 6 * k:6 * k + 6, :], ps[:, k, 0:6 * SK].rearrange("p (h k) -> p h k", h=6),
                                            smax[:, s, 6 * k:6 * k + 6].unsqueeze(2).broadcast_to([P, 6, SK]), ALU.subtract)
                nc.vector.tensor_tensor(d[:, 12:16, :], hi, smax[:, s, 12:16].unsqueeze(2).broadcast_to([P, 4, SK]),
                                        ALU.subtract).then_inc(sub_done, 1)

            def sums(b, s):
                dve.wait_ge(exp_done, b + 1)
                nc.vector.tensor_reduce(ssum[:, s, :], sc[:, s, :].rearrange("p (h k) -> p h k", h=NH), AX_X, ALU.add).then_inc(sum_done, 1)
                dve.wait_ge(sum_done, b + 1)
                nc.vector.reciprocal(rinv[:, s, :], ssum[:, s, :]).then_inc(rinv_done, 1)

            def residual(b):
                row = row_of(b)
                nc.vector.tensor_tensor(row, row, bo0[:, :], ALU.add).then_inc(wo_part, 1)
                dve.wait_ge(wo_ready, b + 1)
                dve.wait_ge(wo_part, b + 1)
                nc.vector.tensor_tensor(row, ps[:, 7, 0:D], row, ALU.add).then_inc(wo_done, 1)

            def body(i, first=False, second=False, last=False):
                b0, b1 = 2 * i, 2 * i + 1
                if not first:
                    dve.drain()
                norm_rows(i + 1, inputs=not last, results=not first, second=second)
                subtract_max(b1, 1)
                residual(b0)
                if not last:
                    move_k(i + 1, (0, 1))
                sums(b1, 1)
                if not last:
                    move_k(i + 1, (2,))
                if not first:
                    dve.wait_ge(rl_ready, i)
                    move_logits(i - 1)
                if not last:
                    subtract_max(b0 + 2, 0)
                    sums(b0 + 2, 0)
                residual(b1)

            dve.wait_ge(ld["x0"], 16)
            norm_rows(0, results=False)
            dve.wait_ge(ld["wv"], 32)
            for c_ in range(C0):
                last = nc.vector.tensor_copy(oT[:, c_, :], bv0[:, c_:c_ + 1].broadcast_to([P, P]))
            last.then_inc(bias_spread, 1)
            dve.wait_ge(ld["wk"], 32)
            dve.wait_ge(kz, 1)
            move_k(0)
            subtract_max(0, 0)
            sums(0, 0)
            dve.wait_ge(ld["wo"], 32)
            dve.wait_ge(bias_ready, 1)
            nc.vector.tensor_tensor(bo0[:, :], ps[:, 7, 0:D], bo0[:, :], ALU.add).then_inc(bias_added, 1)
            dve.wait_ge(bias_added, 1)
            dve.wait_ge(ld["x"], 16)
            body(0, first=True)
            body(1, second=True)
            with dve.Fori(2, PAIRS - 1) as i:
                body(i)
            body(PAIRS - 1, last=True)
            dve.drain()
            norm_rows(PAIRS + 1, inputs=False)
            dve.wait_ge(rl_ready, PAIRS)
            move_logits(PAIRS - 1)

            def route(L, logits, first_expert):
                ne, nt, n = L.ne, L.tiles, NB * L.ne
                count = [0]

                def then(ins):
                    count[0] += 1
                    ins.then_inc(L.step, 1)
                    dve.wait_ge(L.step, count[0])

                def grid(k):
                    return r_scratch[:, k * n:(k + 1) * n].rearrange("p (b e) -> p b e", e=ne)

                def over_e(v):
                    return v.unsqueeze(2).broadcast_to([P, NB, ne])

                def over_b(v):
                    return v.unsqueeze(1).broadcast_to([P, NB, ne])

                masks, eq, rest = [grid(k) for k in range(L.slots)], grid(L.slots), grid(L.slots + 1)
                incl, pos = grid(L.slots + 2), grid(L.slots + 1)
                order = over_b(first_expert)
                tops = [rt_small[:, k, 0:NB] for k in range(2)]
                cand = rt_small[:, 2, 0:NB]
                left = logits
                for k in range(L.slots):
                    then(nc.vector.tensor_reduce(tops[k], left, AX_X, ALU.max))
                    then(nc.vector.tensor_tensor(eq, left, over_e(tops[k]), ALU.is_equal))
                    then(nc.vector.tensor_tensor(eq, eq, order, ALU.mult))
                    then(nc.vector.tensor_reduce(cand, eq, AX_X, ALU.max))
                    then(nc.vector.tensor_tensor(masks[k], order, over_e(cand), ALU.is_equal))
                    if k + 1 < L.slots:
                        then(nc.vector.scalar_tensor_tensor(out=rest, in0=masks[k], scalar=-3e38, in1=left, op0=ALU.mult, op1=ALU.add))
                        left = rest
                both = masks[0]
                if L.slots == 2:
                    then(nc.vector.tensor_tensor(eq, masks[0], masks[1], ALU.add))
                    both = eq
                nc.vector.tensor_copy(hold_mask[:, 0:n].rearrange("p (b e) -> p b e", e=ne), both).then_inc(L.mask_ready, 1)
                if L.slots == 2:
                    then(nc.vector.tensor_tensor(rt_small[:, 3, 0:NB], tops[1], tops[0], ALU.subtract))
                    nc.vector.tensor_tensor(rest, logits, over_e(tops[0]), ALU.subtract).then_inc(w_sub, 1)
                    dve.wait_ge(w_exp, 1)
                    e2, z, p2 = rt_small[:, 3, 0:NB], rt_small[:, 4, 0:NB], rt_small[:, 5, 0:NB]
                    then(nc.vector.tensor_reduce(z, rest, AX_X, ALU.add))
                    then(nc.vector.reciprocal(z, z))
                    then(nc.vector.tensor_tensor(p2, e2, z, ALU.mult))
                    then(nc.vector.tensor_tensor(e2, z, p2, ALU.add))
                    then(nc.vector.reciprocal(e2, e2))
                    then(nc.vector.tensor_tensor(topw[:, 0, :], z, e2, ALU.mult))
                    then(nc.vector.tensor_tensor(topw[:, 1, :], p2, e2, ALU.mult))
                dve.wait_ge(L.rank_ready, 2)
                totals = ps[:, 7, 0:n].rearrange("p (b e) -> p b e", e=ne)
                for e in range(ne):
                    last = nc.vector.tensor_tensor_scan(incl[:, :, e], ones[:, 0:NB], totals[:, :, e], 0.0, ALU.mult, ALU.add)
                then(last)
                fill, begin, end = (ne_small[:, k, 0:ne] for k in range(3))
                then(nc.vector.tensor_tensor(pos, incl, totals, ALU.subtract))
                then(nc.vector.tensor_scalar(rt_int[:, 0:ne], incl[:, NB - 1, :], (P - 1) / 2, 1.0 / P, ALU.add, ALU.mult))
                then(nc.vector.tensor_copy(fill, rt_int[:, 0:ne]))
                then(nc.vector.tensor_tensor_scan(end, ones[:, 0:ne], fill, 0.0, ALU.mult, ALU.add))
                then(nc.vector.tensor_tensor(begin, end, fill, ALU.subtract))
                then(nc.vector.tensor_scalar(begin, begin, float(P), None, ALU.mult))
                then(nc.vector.tensor_tensor(pos, pos, over_b(begin), ALU.add))
                then(nc.vector.tensor_tensor(pos, pos, ps[:, 6, 0:n].rearrange("p (b e) -> p b e", e=ne), ALU.add))
                m = L.slots * NB
                at = rt_small[:, 4, 0:m]
                for k in range(L.slots):
                    then(nc.vector.tensor_tensor(eq, masks[k], pos, ALU.mult))
                    then(nc.vector.tensor_reduce(at[:, k * NB:(k + 1) * NB], eq, AX_X, ALU.add))
                then(nc.vector.tensor_copy(L.place[:, 0:m], at))
                nc.vector.tensor_copy(ne_small[:, 0, 0:1], at[:, 0:1]).then_inc(L.place_ready, 1)
                if L.slots == 1:
                    scale = rt_small[:, 3, 0:NB]
                    dve.wait_ge(top_exp, 1)
                    then(nc.vector.tensor_scalar(scale, scale, 1.0, None, ALU.add))
                    then(nc.vector.reciprocal(scale, scale))
                    for n in range(0, NB, SCALE):
                        rows = rows_all[:, n:n + SCALE, :]
                        nc.vector.tensor_tensor(rows, rows, scale[:, n:n + SCALE].unsqueeze(2).broadcast_to([P, SCALE, D]),
                                                ALU.mult).then_inc(rows_scaled, 1)
                past = r_scratch[:, 0:nt * ne].rearrange("p (j e) -> p j e", e=ne)
                then(nc.vector.tensor_tensor(past, iota[:, 0:nt].unsqueeze(2).broadcast_to([P, nt, ne]),
                                             end.unsqueeze(1).broadcast_to([P, nt, ne]), ALU.is_ge))
                expert = r_scratch[:, 1024:1024 + nt]
                then(nc.vector.tensor_reduce(expert, past, AX_X, ALU.add))
                nc.vector.tensor_scalar(L.weights_at[:, :], expert, float(ne - 1), float(L.width), ALU.min, ALU.mult).then_inc(L.tiles_ready, 1)

            def experts(L):
                w = L.per_step * L.width
                half = w // 2

                def multiply(j, s):
                    dve.wait_ge(L.act_done, j + 1)
                    dve.wait_ge(L.up_ready, j + 1)
                    if past(j, 2):
                        dve.wait_ge(L.th_ready, j - 1)
                    nc.vector.tensor_tensor(hmul[:, s, 0:w], ps[:, 2 * s + 1, 0:w], gact[:, s, 0:w], ALU.mult).then_inc(L.h_done, 1)

                def move_hT(j, s):
                    dve.wait_ge(L.th_ready, j + 1)
                    if past(j, 2):
                        dve.wait_ge(L.y_ready, j - 1)
                    nc.vector.tensor_copy(hT[:, s, 0:half], ps[:, 5, 0:half]).then_inc(L.th_done[0], 1)

                def body(i, first=False):
                    for t in range(L.steps):
                        j = L.steps * i + t
                        if not (first and t == 0):
                            move_hT(j - 1, (t - 1) % 2)
                        multiply(j, t % 2)

                body(0, first=True)
                with dve.Fori(1, L.tiles // TURN) as i:
                    body(i)
                move_hT(L.tiles // L.per_step - 1, 1)

            dve.wait_ge(rl_done, PAIRS)
            dve.wait_ge(ld_small, 16 * SMALL_LOADS)
            dve.wait_ge(ones_set, 1)
            nc.vector.tensor_scalar(ne_small[:, 3, :], iota[:, 0:NH], -1.0, float(NE0), ALU.mult, ALU.add).then_inc(order_set, 1)
            dve.wait_ge(order_set, 1)
            dve.wait_ge(t_ready, 4 * NB)
            route(L0, logits0[:, :, :], ne_small[:, 3, 0:NE0])
            experts(L0)

            def combine(i):
                rows = [row_of(2 * i + s) for s in range(2)]
                for s in range(2):
                    dve.wait_ge(yin_loaded[s], 32 * (i + 1))
                    nc.vector.scalar_tensor_tensor(out=rows[s], in0=yin[:, s, 0, :], scalar=topw[:, 0, bass.ds(2 * i + s, 1)], in1=rows[s],
                                                   op0=ALU.mult, op1=ALU.add).then_inc(comb_part, 1)
                for s in range(2):
                    dve.wait_ge(comb_part, 2 * i + s + 1)
                    nc.vector.scalar_tensor_tensor(out=rows[s], in0=yin[:, s, 1, :], scalar=topw[:, 1, bass.ds(2 * i + s, 1)], in1=rows[s],
                                                   op0=ALU.mult, op1=ALU.add).then_inc(comb_done, 1)
                dve.drain()

            def rows_to_norm(turn, inputs, results):
                return [row_of(2 * turn + s) for s in range(2) if inputs] + [row_of(2 * turn - 6 + s) for s in range(2) if results]

            def norm_rows1(turn, inputs=True, results=True):
                dsts = [xh[:, s, :] for s in range(2) if inputs] + [xf[:, s, :] for s in range(2) if results]
                free = []
                if past(turn, 1):
                    free.append((c["xt"], turn))
                if results and past(turn, 4):
                    free.append((c["stored"], 16 * (turn - 3)))
                layernorm(dve, rows_to_norm(turn, inputs, results), dsts, ln_a, free).then_inc(c["xh"], 1)

            def subtract_max1(b, s):
                dve.wait_ge(c["s"], b + 1)
                if not (isinstance(b, int) and b < 2):
                    dve.wait_ge(c["t"], 4 * b - 4)
                lo = ps[:, 0:2, 0:6 * SK].rearrange("p a (h k) -> p a h k", h=6)
                hi = ps[:, 2, 0:4 * SK].rearrange("p (h k) -> p h k", h=4)
                nc.vector.tensor_reduce(smax[:, s, 0:12].rearrange("p (a h) -> p a h", a=2), lo, AX_X, ALU.max)
                nc.vector.tensor_reduce(smax[:, s, 12:16], hi, AX_X, ALU.max).then_inc(c["max"], 1)
                dve.wait_ge(c["max"], b + 1)
                d = sc[:, s, :].rearrange("p (h k) -> p h k", h=NH)
                for k, n in enumerate((6, 6, 4)):
                    last = nc.vector.tensor_tensor(d[:, 6 * k:6 * k + n, :], ps[:, k, 0:n * SK].rearrange("p (h k) -> p h k", h=n),
                                                   smax[:, s, 6 * k:6 * k + n].unsqueeze(2).broadcast_to([P, n, SK]), ALU.subtract)
                last.then_inc(c["sub"], 1)

            def sums1(b, s):
                dve.wait_ge(c["exp"], b + 1)
                nc.vector.tensor_reduce(ssum[:, s, :], sc[:, s, :].rearrange("p (h k) -> p h k", h=NH), AX_X, ALU.add).then_inc(c["sum"], 1)
                dve.wait_ge(c["sum"], b + 1)
                nc.vector.reciprocal(rinv[:, s, :], ssum[:, s, :]).then_inc(c["rinv"], 1)

            def residual1(b):
                row = row_of(b)
                nc.vector.tensor_tensor(row, row, bo1[:, :], ALU.add).then_inc(c["wo_part"], 1)
                dve.wait_ge(c["wo"], b + 1)
                dve.wait_ge(c["wo_part"], b + 1)
                nc.vector.tensor_tensor(row, ps[:, 7, 0:D], row, ALU.add).then_inc(c["x"], 1)

            def body1(i, inputs=True, results=True, more=True, last=False):
                b0, b1_ = 2 * i, 2 * i + 1
                subtract_max1(b1_, 1)
                if past(i, 1):
                    residual1(b0 - 1)
                dve.drain()
                statistics(dve, rows_to_norm(i + 2, inputs, results), ln_a)
                sums1(b1_, 1)
                residual1(b0)
                norm_rows1(i + 2, inputs=inputs, results=results)
                if not last:
                    subtract_max1(b0 + 2, 0)
                    if more:
                        combine(i + 3)
                    sums1(b0 + 2, 0)

            dve.wait_ge(ld_small, 16 * SMALL_LOADS)
            nc.vector.tensor_scalar(mask_add[:, :], mask_in[:, :], 0.0, -3e38, ALU.is_equal, ALU.mult).then_inc(mask_step, 1)
            nc.vector.tensor_copy(ident_bf[:, :], ident[:, :])
            dve.wait_ge(mask_step, 1)
            nc.vector.tensor_copy(mask_heads[:, :, :], mask_add[:, :].unsqueeze(1).broadcast_to([P, 6, SK]))
            none_left = rt_small[:, 0, 0:1]
            nc.vector.tensor_reduce(none_left, mask_add[:, :], AX_X, ALU.max).then_inc(mask_step, 1)
            dve.wait_ge(mask_step, 2)
            nc.vector.tensor_scalar(none_left, none_left, 10.0, None, ALU.mult).then_inc(mask_step, 1)
            dve.wait_ge(mask_step, 3)
            nc.vector.tensor_tensor(none_left, none_left, none_left, ALU.subtract).then_inc(mask_step, 1)
            dve.wait_ge(mask_step, 4)
            nc.vector.tensor_scalar(bo1[:, :], bo1[:, :], none_left, None, ALU.add).then_inc(mask_step, 1)
            dve.wait_ge(mask_step, 5)
            for i in range(2):
                combine(i)
                statistics(dve, rows_to_norm(i, True, False), ln_a)
                norm_rows1(i, results=False)
            subtract_max1(0, 0)
            combine(2)
            sums1(0, 0)
            body1(0, results=False)
            body1(1)
            with dve.Fori(2, PAIRS - 3) as i:
                body1(i)
            body1(PAIRS - 3, more=False)
            body1(PAIRS - 2, inputs=False, more=False)
            body1(PAIRS - 1, inputs=False, last=True)
            residual1(NB - 1)
            dve.drain()
            statistics(dve, rows_to_norm(PAIRS + 2, False, True), ln_a)
            norm_rows1(PAIRS + 2, inputs=False)

            dve.wait_ge(c["rl_moved"], PAIRS)
            dve.wait_ge(c["t"], 4 * NB)
            nc.vector.tensor_scalar(ne_small[:, 3, :], iota[:, 0:NH], -1.0, float(NE1), ALU.mult, ALU.add).then_inc(order_set, 1)
            dve.wait_ge(order_set, 2)
            dve.wait_ge(c["stored"], 16 * PAIRS)
            route(L1, logits1[:, :, :], ne_small[:, 3, 0:NE1])

            def add_shared(g, bank=4):
                dve.wait_ge(sh["down"], g + 1)
                rows = x_res[:, bass.ds(GROUP * g, GROUP), :]
                nc.vector.tensor_tensor(rows, ps[:, bank, :].rearrange("p (b d) -> p b d", d=D), rows, ALU.add).then_inc(sh["added"], 1)

            def shared(g):
                for k in range(4):
                    s = k % 2
                    dve.wait_ge(sh["act"], 4 * g + k + 1)
                    dve.wait_ge(sh["up"], 4 * g + k + 1)
                    if k == 0 and past(g, 1):
                        dve.wait_ge(sh["down"], g)
                    nc.vector.tensor_tensor(shared_h[:, k, :], ps[:, 2 * s + 1, :], shared_gate[:, s, :], ALU.mult).then_inc(sh["h"], 1)
                add_shared(g)

            for g in range(POOLED):
                add_shared(g, 4 + g)
            with dve.Fori(POOLED, EARLY) as g:
                shared(g)
            experts(L1)
            with dve.Fori(EARLY, NB // GROUP) as g:
                shared(g)
            for g in range(NB // GROUP):
                dve.wait_ge(y1_loaded[g], 16 * GROUP)
                dve.wait_ge(sh["added"], g + 1)
                rows = x_res[:, g * GROUP:(g + 1) * GROUP, :]
                nc.vector.tensor_tensor(rows, rows, y1[:, g * GROUP:(g + 1) * GROUP, :],
                                        ALU.add).then_inc(final_done, 1)

        @block.tensor
        def _(pe):
            def turn_rows(turn, inputs=True, results=True):
                pe.wait_ge(xh_done, turn + 1)
                for k in range(0 if inputs else 2, 4 if results else 2):
                    mm = nc.tensor.transpose(ps[:, 4, k * P:(k + 1) * P], (xh if k < 2 else xf)[:, k % 2, :], ident[:, :])
                mm.then_inc(xt_ready, 1)

            def queries(i, bank_free):
                pe.wait_ge(xt_done, i + 1)
                for n, bank in enumerate((7, 5, 6, 7)):
                    pe.wait_ge(*bank_free[n])
                    for c in (2 * n, 2 * n + 1):
                        mm = nc.tensor.matmul(ps[:, bank, (c % 2) * 256:(c % 2) * 256 + 256], wq0[:, c * P:(c + 1) * P], xhT[:, :],
                                              start=True, stop=True)
                    mm.then_inc(q_ready, 1)

            def keys(i, last_free):
                pe.wait_ge(cp_ready, i + 1)
                for n, (c0, c1, bank) in enumerate(KEY_GROUPS):
                    if n == 2:
                        pe.wait_ge(*last_free)
                    for c in range(c0, c1):
                        o = (c - c0) * 2 * SK
                        mm = nc.tensor.matmul(ps[:, bank, o:o + 2 * SK], wk0[:, c * P:(c + 1) * P], cpair[:, :], start=True, stop=True)
                    mm.then_inc(k_ready, 1)

            def value_half(s, n, bank_free):
                pe.wait_ge(*bank_free)
                nc.tensor.matmul(ps[0:SK, VALUE_BANKS[s][n], :], cpair[:, s * SK:(s + 1) * SK], wv0[:, n * 512:(n + 1) * 512],
                                 start=True, stop=True).then_inc(v_ready, 1)

            def scores(b, s, i, chunks=range(C0)):
                for c in chunks:
                    if c == 0:
                        pe.wait_ge(q_done, 4 * i + 3)
                        pe.wait_ge(k_done, 3 * i + 2)
                        if past(b, 1):
                            pe.wait_ge(sub_done, b)
                    if c == 6:
                        pe.wait_ge(q_done, 4 * i + 4)
                        pe.wait_ge(k_done, 3 * i + 3)
                    o = (c % 3) * 2 * SK
                    mm = nc.tensor.matmul(ps[:, c // 3, o:o + 2 * SK], qT[:, c, s * P:(s + 1) * P], kbd[:, s, c, :], start=True, stop=True)
                if C0 - 1 in chunks:
                    mm.then_inc(s_ready, 1)

            def transpose_probs(b, s, g):
                if g % 2 == 0:
                    pe.wait_ge(p_done, 2 * b + g // 2 + 1)
                if g >= 2:
                    pe.wait_ge(pt_done, 4 * b + g - 1)
                for k in range(4):
                    h = 4 * g + k
                    mm = nc.tensor.transpose(ps[0:SK, TB + g % 2, k * P:(k + 1) * P], sc[:, s, h * SK:(h + 1) * SK], ident[:, :])
                mm.then_inc(t_ready, 1)

            def weigh_values(b, s, g):
                pe.wait_ge(pt_done, 4 * b + g + 1)
                for k in range(4):
                    h = 4 * g + k
                    lo = 64 * (h % 2)
                    o = ((h // 2) % 4) * P
                    mm = nc.tensor.matmul(ps[lo:lo + 64, 5 + g // 2, o:o + P], vv[:, s, h * DK0:(h + 1) * DK0],
                                          pT[:, g, k * P:(k + 1) * P], start=True, stop=True)
                if g % 2:
                    mm.then_inc(ot_ready, 1)

            def attend_begin(b, s, banks_free):
                for wait in banks_free:
                    pe.wait_ge(*wait)
                transpose_probs(b, s, 0)
                transpose_probs(b, s, 1)

            def attend_middle(b, s):
                weigh_values(b, s, 0)
                transpose_probs(b, s, 2)
                weigh_values(b, s, 1)
                transpose_probs(b, s, 3)

            def attend_end(b, s):
                weigh_values(b, s, 2)
                weigh_values(b, s, 3)

            def project(b, bank_free):
                if bank_free:
                    pe.wait_ge(*bank_free)
                pe.wait_ge(ot_done, 2 * b + 2)
                for c in range(C0):
                    mm = nc.tensor.matmul(ps[:, 7, 0:D], oT[:, c, :], wo0[:, c * D:(c + 1) * D], start=c == 0, stop=c == C0 - 1)
                mm.then_inc(wo_ready, 1)

            def router_logits(i, turn):
                pe.wait_ge(xt_done, turn + 1)
                for s in range(2):
                    mm = nc.tensor.matmul(ps[:, 4, s * NE0:(s + 1) * NE0], xfT[:, s * P:(s + 1) * P], gw0[:, :],
                                          start=True, stop=True)
                mm.then_inc(rl_ready, 1)

            def body(i, first=False, last=False):
                b0, b1 = 2 * i, 2 * i + 1
                if not first:
                    project(b0 - 1, (v_done, 4 * i + 1))
                attend_begin(b0, 0, [(v_done, 4 * i + 3)])
                scores(b1, 1, i, range(0, C0 // 2))
                pe.wait_ge(v_done, 4 * i + 4)
                attend_middle(b0, 0)
                scores(b1, 1, i, range(C0 // 2, C0))
                attend_end(b0, 0)
                turn_rows(i + 1, inputs=not last, results=not first)
                project(b0, (wo_done, b0) if not first else (bias_added, 1))
                if not last:
                    keys(i + 1, (pt_done, 4 * b0 + 3))
                    queries(i + 1, [(wo_done, b0 + 1), (k_done, 3 * i + 4), (k_done, 3 * i + 5), (q_done, 4 * i + 5)])
                if not first:
                    router_logits(i - 1, i + 1)
                if not last:
                    scores(b0 + 2, 0, i + 1)
                banks_free = [] if last else [(k_done, 3 * i + 6), (q_done, 4 * i + 8)]
                if not first:
                    banks_free.append((rl_done, i))
                attend_begin(b1, 1, banks_free)
                if not last:
                    value_half(0, 0, (q_done, 4 * i + 8))
                attend_middle(b1, 1)
                if not last:
                    value_half(0, 1, (pt_done, 4 * b1 + 3))
                attend_end(b1, 1)
                if not last:
                    value_half(1, 0, (pt_done, 4 * b1 + 4))
                    value_half(1, 1, (ot_done, 2 * b1 + 1))
                else:
                    project(b1, (wo_done, b1))

            pe.wait_ge(ld["id"], 16)
            turn_rows(0, results=False)
            pe.wait_ge(ld["wk"], 32)
            keys(0, (ld["wk"], 32))
            pe.wait_ge(ld["wq"], 32)
            queries(0, [(ld["wq"], 32), (k_done, 1), (k_done, 2), (q_done, 1)])
            scores(0, 0, 0)
            pe.wait_ge(ld["wv"], 32)
            value_half(0, 0, (q_done, 4))
            value_half(0, 1, (k_done, 3))
            value_half(1, 0, (xt_done, 1))
            value_half(1, 1, (q_done, 4))
            pe.wait_ge(ld["wo"], 32)
            pe.wait_ge(bias_spread, 1)
            pe.wait_ge(v_done, 1)
            for c_ in range(C0):
                mm = nc.tensor.matmul(ps[:, 7, 0:D], oT[:, c_, :], wo0[:, c_ * D:(c_ + 1) * D], start=c_ == 0, stop=c_ == C0 - 1)
            mm.then_inc(bias_ready, 1)
            pe.wait_ge(ld["gw"], 16)
            body(0, first=True)
            with pe.Fori(1, PAIRS - 1) as i:
                body(i)
            body(PAIRS - 1, last=True)
            pe.wait_ge(ot_done, 2 * NB)
            turn_rows(PAIRS + 1, inputs=False)
            router_logits(PAIRS - 1, PAIRS + 1)

            def ranks(L):
                pe.wait_ge(L.mask_ready, 1)
                n = NB * L.ne
                nc.tensor.matmul(ps[:, 6, 0:n], tri, hold_mask[:, 0:n], start=True, stop=True).then_inc(L.rank_ready, 1)
                nc.tensor.matmul(ps[:, 7, 0:n], ones[:, :], hold_mask[:, 0:n], start=True, stop=True).then_inc(L.rank_ready, 1)

            def experts(L, up_w, down_w):
                m, w, chunks = L.per_step, L.width, L.width // P
                gate_w, up_w = up_w[:, 0:L.ne * w], up_w[:, L.ne * w:2 * L.ne * w]

                def turn_rows(j, t, i):
                    if past(j, 1):
                        pe.wait_ge(L.tx_done, j)
                    if t * m % HALF == 0:
                        pe.wait_ge(L.rows_loaded[t * m // HALF], 16 * (i + 1))
                    for k in range(m):
                        mm = nc.tensor.transpose(ps[:, 4, k * P:(k + 1) * P], xg[:, t * m + k, :], ident[:, :])
                    mm.then_inc(L.tx_ready, 1)

                def weights_at(j):
                    return [pe.value_load(L.weights_at[0:1, bass.ds(j * m + k, 1)], min_val=0, max_val=(L.ne - 1) * w)
                            for k in range(m)]

                def product(j, s, bank, weights, at, ready):
                    for k in range(m):
                        mm = nc.tensor.matmul(ps[:, bank, k * w:(k + 1) * w], xgT[:, s, k * P:(k + 1) * P], weights[:, bass.ds(at[k], w)],
                                              start=True, stop=True)
                    mm.then_inc(ready, 1)

                def turn_hidden(j, s):
                    pe.wait_ge(L.h_done, j + 1)
                    if past(j, 1):
                        for done in L.th_done:
                            pe.wait_ge(done, j)
                    n = m * chunks // 2
                    for k in range(2 * n):
                        mm = nc.tensor.transpose(ps[:, 5 + k // n, (k % n) * P:(k % n + 1) * P], hmul[:, s, k * P:(k + 1) * P], ident[:, :])
                    mm.then_inc(L.th_ready, 1)

                def down(j, s, at):
                    for done in L.th_done:
                        pe.wait_ge(done, j + 1)
                    if past(j, 1):
                        pe.wait_ge(L.y_done, j)
                    for k in range(m):
                        for c in range(chunks):
                            o = k * w + c * P
                            mm = nc.tensor.matmul(ps[:, 7, k * D:(k + 1) * D], hT[:, s, o:o + P], down_w[:, c * D:][:, bass.ds(at[k], D)],
                                                  start=c == 0, stop=c == chunks - 1)
                    mm.then_inc(L.y_ready, 1)

                def body(i, first=False, last=False):
                    at = None if first else weights_at(L.steps * i - 1)
                    next_at = weights_at(L.steps * i)
                    for t in range(L.steps):
                        j, s = L.steps * i + t, t % 2
                        last_at, at = at, next_at
                        pe.wait_ge(L.tx_done, j + 1)
                        if past(j, 2):
                            pe.wait_ge(L.h_done, j - 1)
                        product(j, s, 2 * s, gate_w, at, L.gate_ready)
                        if not (first and t == 0):
                            turn_hidden(j - 1, 1 - s)
                        product(j, s, 2 * s + 1, up_w, at, L.up_ready)
                        if t < L.steps - 1:
                            next_at = weights_at(j + 1)
                            turn_rows(j + 1, t + 1, i)
                        elif not last:
                            turn_rows(j + 1, 0, i + 1)
                        if not (first and t == 0):
                            down(j - 1, 1 - s, last_at)
                    return at

                pe.wait_ge(L.tiles_ready, 1)
                turn_rows(0, 0, 0)
                body(0, first=True)
                middle = L.tiles // TURN - 2
                start = 1 + middle % 2
                if middle % 2:
                    body(1)
                with pe.Fori(0, middle // 2) as i:
                    body(i * 2 + start)
                    body(i * 2 + start + 1)
                at = body(L.tiles // TURN - 1, last=True)
                turn_hidden(L.tiles // m - 1, 1)
                down(L.tiles // m - 1, 1, at)

            pe.wait_ge(ld_small, 16 * SMALL_LOADS)
            pe.wait_ge(ones_set, 1)
            ranks(L0)
            pe.wait_ge(ld_moe0, 32)
            experts(L0, gu0, dn0)

            def turn_rows1(turn, inputs=True, results=True):
                pe.wait_ge(c["xh"], turn + 1)
                for k in range(0 if inputs else 2, 4 if results else 2):
                    mm = nc.tensor.transpose(ps[:, 4, k * P:(k + 1) * P], (xh if k < 2 else xf)[:, k % 2, :], ident[:, :])
                mm.then_inc(c["xt"], 1)

            def queries1(i):
                pe.wait_ge(c["xt_moved"], i + 1)
                nc.tensor.matmul(ps[:, 5, 0:2 * P], wq1, xhT, start=True, stop=True).then_inc(c["q"], 1)

            def keys1(i):
                pe.wait_ge(cp_ready, PAIRS + i + 1)
                nc.tensor.matmul(ps[:, 6, 0:2 * SK], wk1, cpair[:, :], start=True, stop=True).then_inc(c["k"], 1)

            def values1(i):
                pe.wait_ge(c["k_moved"], i + 1)
                for s in range(2):
                    mm = nc.tensor.matmul(ps[0:SK, 6, s * D:(s + 1) * D], cpair[:, s * SK:(s + 1) * SK], wv1, start=True, stop=True)
                mm.then_inc(c["v"], 1)

            def scores1(b, s):
                pe.wait_ge(c["k_masked"], b + 1)
                if not (isinstance(b, int) and b == 0):
                    pe.wait_ge(c["sub"], b)
                for k, n in enumerate((6, 6, 4)):
                    nc.tensor.matmul(ps[:, k, 0:n * SK], q1T[:, s * P:(s + 1) * P], k1m[:, s, 6 * k * SK:(6 * k + n) * SK],
                                     start=True, stop=False)
                    mm = nc.tensor.matmul(ps[:, k, 0:n * SK], ident_bf[:, :], mask_heads[:, 0:n, :].rearrange("p h k -> p (h k)"),
                                          start=False, stop=True)
                mm.then_inc(c["s"], 1)

            def transpose_probs1(b, s, g):
                if g % 2 == 0:
                    pe.wait_ge(c["p"], 2 * b + g // 2 + 1)
                if g >= 2:
                    pe.wait_ge(c["pt"], 4 * b + g - 1)
                for k in range(4):
                    h = 4 * g + k
                    mm = nc.tensor.transpose(ps[0:SK, TB + g % 2, k * P:(k + 1) * P], sc[:, s, h * SK:(h + 1) * SK], ident[:, :])
                mm.then_inc(c["t"], 1)

            def weigh_values1(b, s, g, bank):
                pe.wait_ge(c["pt"], 4 * b + g + 1)
                for k in range(4):
                    h = 4 * g + k
                    mm = nc.tensor.matmul(ps[:, bank, 0:P], v1m[:, s, h, :], pT[:, g, k * P:(k + 1) * P], start=h == 0, stop=h == NH - 1)
                if g == 3:
                    mm.then_inc(c["ot"], 1)

            def attend1_begin(b, s):
                transpose_probs1(b, s, 0)
                transpose_probs1(b, s, 1)

            def attend1(b, s, bank):
                pe.wait_ge(c["v_spread"], b + 1)
                weigh_values1(b, s, 0, bank)
                transpose_probs1(b, s, 2)
                weigh_values1(b, s, 1, bank)
                transpose_probs1(b, s, 3)
                weigh_values1(b, s, 2, bank)
                weigh_values1(b, s, 3, bank)

            def project1(b):
                if past(b, 1):
                    pe.wait_ge(c["x"], b)
                pe.wait_ge(c["ot_moved"], b + 1)
                nc.tensor.matmul(ps[:, 7, 0:D], o1T, wo1, start=True, stop=True).then_inc(c["wo"], 1)

            def router_logits1(i):
                pe.wait_ge(c["xt_moved"], i + 4)
                for s in range(2):
                    mm = nc.tensor.matmul(ps[:, 5, RL + s * NE1:RL + (s + 1) * NE1], xfT[:, s * P:(s + 1) * P], gw1[:, :],
                                          start=True, stop=True)
                mm.then_inc(c["rl"], 1)

            def body1(i, first=False, results=True, last=False):
                b0, b1_ = 2 * i, 2 * i + 1
                scores1(b1_, 1)
                pe.wait_ge(c["xt_moved"], i + 1)
                attend1_begin(b0, 0)
                if not first:
                    project1(b0 - 1)
                if not last:
                    pe.wait_ge(*((c["v_moved"], 1) if first else (c["ot_moved"], b0)))
                    keys1(i + 1)
                attend1(b0, 0, 5)
                turn_rows1(i + 1, inputs=not last, results=results)
                project1(b0)
                if not last:
                    values1(i + 1)
                if results:
                    router_logits1(i - 2)
                if not last:
                    queries1(i + 1)
                pe.wait_ge(c["xt_moved"], i + 2)
                attend1_begin(b1_, 1)
                if not last:
                    pe.wait_ge(c["q_moved"], i + 2)
                    scores1(b0 + 2, 0)
                    pe.wait_ge(c["v_moved"], i + 2)
                attend1(b1_, 1, 6)

            pe.wait_ge(L0.y_done, L0.tiles)
            pe.wait_ge(ld_small, 16 * SMALL_LOADS)
            keys1(0)
            turn_rows1(0, results=False)
            queries1(0)
            values1(0)
            pe.wait_ge(c["q_moved"], 1)
            pe.wait_ge(mask_step, 2)
            scores1(0, 0)
            body1(0, first=True, results=False)
            body1(1, results=False)
            with pe.Fori(2, PAIRS - 1) as i:
                body1(i)
            body1(PAIRS - 1, last=True)
            project1(NB - 1)
            for i in (PAIRS - 2, PAIRS - 1):
                turn_rows1(i + 3, inputs=False)
                router_logits1(i)

            pe.wait_ge(ld_moe1, 16 * 5)

            def shared_up(g, k, first=False):
                rows = xT_all[:, bass.ds(g * GROUP * P, GROUP * P)]
                s = k % 2
                if not (first and k < 2):
                    pe.wait_ge(sh["h"], 4 * g + k - 1)
                nc.tensor.matmul(ps[:, 2 * s, :], shg[:, k * P:(k + 1) * P], rows, start=True, stop=True).then_inc(sh["gate"], 1)
                nc.tensor.matmul(ps[:, 2 * s + 1, :], shu[:, k * P:(k + 1) * P], rows, start=True, stop=True).then_inc(sh["up"], 1)

            def shared(g, first=False, last=False, bank=4):
                for k in range(2 if first else 1, 4):
                    shared_up(g, k)
                if not last:
                    shared_up(g + 1, 0)
                pe.wait_ge(sh["h"], 4 * g + 4)
                if past(g, POOLED):
                    pe.wait_ge(sh["added"], g)
                for t in range(GROUP):
                    for k in range(4):
                        mm = nc.tensor.matmul(ps[:, bank, t * D:(t + 1) * D], shared_h[:, k, t * P:(t + 1) * P], shd[:, k * D:(k + 1) * D],
                                              start=k == 0, stop=k == 3)
                mm.then_inc(sh["down"], 1)

            pe.wait_ge(c["xt_kept"], PAIRS)
            pe.wait_ge(c["rl_moved"], PAIRS)
            shared_up(0, 0, first=True)
            shared_up(0, 1, first=True)
            ranks(L1)
            for g in range(POOLED):
                shared(g, first=g == 0, bank=4 + g)
            with pe.Fori(POOLED, EARLY - 1) as g:
                shared(g)
            shared(EARLY - 1, last=True)
            pe.wait_ge(sh["added"], EARLY)
            experts(L1, gu1, dn1)
            pe.wait_ge(L1.tx_done, L1.tiles // L1.per_step)
            pe.wait_ge(L1.h_done, L1.tiles // L1.per_step)
            shared_up(EARLY, 0)
            with pe.Fori(EARLY, NB // GROUP - 1) as g:
                shared(g)
            shared(NB // GROUP - 1, last=True)


def lay_out(inputs):
    import numpy as np
    d = {k: np.asarray(v) for k, v in inputs.items()}
    iota = np.broadcast_to(np.arange(P, dtype=np.float32), (P, P))
    consts = np.concatenate([iota, np.triu(np.ones((P, P), np.float32), 1)], 1)
    turned = lambda w: np.ascontiguousarray(np.asarray(w).T)
    up = np.asarray(d["L0_ffn_gate_up_w"])
    down = np.asarray(d["L0_ffn_down_w"])
    return {
        "x": d["x"], "ctxT": np.ascontiguousarray(d["ctx_1024"].reshape(-1, D).T), "ident": np.eye(P, dtype=np.float32),
        "wq0": d["L0_xattn_Wq"], "bq0": np.ascontiguousarray(d["L0_xattn_bq"].reshape(C0, P).T),
        "wk0": d["L0_xattn_Wk"], "bk0": np.ascontiguousarray(d["L0_xattn_bk"].reshape(C0, P).T),
        "wv0": d["L0_xattn_Wv"], "bv0": np.ascontiguousarray(d["L0_xattn_bv"].reshape(C0, P).T), "wo0": d["L0_xattn_Wo"], "bo0": d["L0_xattn_bo"],
        "gw0": np.ascontiguousarray(d["L0_ffn_gate_w"].T), "consts": consts,
        "wq1": turned(d["L1_xattn_Wq"]), "wk1": turned(d["L1_xattn_Wk"]), "wv1": turned(d["L1_xattn_Wv"]),
        "wo1": turned(d["L1_xattn_Wo"]), "b1": np.ascontiguousarray(np.stack([d["L1_xattn_bq"], d["L1_xattn_bk"]], 1)),
        "bv1": d["L1_xattn_bv"], "bo1": d["L1_xattn_bo"], "gw1": turned(d["L1_ffn_router_w"]),
        "head_rows": np.repeat(np.eye(NH, dtype=np.float32), DK1, axis=0), "mask": d["mask_SxS2_ik0"],
        "gu1": np.ascontiguousarray(np.asarray(d["L1_ffn_gate_up_proj"]).reshape(NE1, D, 2, D).transpose(1, 2, 0, 3).reshape(D, -1)),
        "dn1": np.ascontiguousarray(np.asarray(d["L1_ffn_down_proj"]).transpose(1, 0, 2).reshape(P, -1)),
        "shg": turned(d["L1_ffn_shared_gate_w"]), "shu": turned(d["L1_ffn_shared_up_w"]),
        "shd": np.ascontiguousarray(np.asarray(d["L1_ffn_shared_down_w"]).reshape(D, 4, P).transpose(2, 1, 0).reshape(P, -1)),
        "gu0": np.ascontiguousarray(up.reshape(NE0, 2, -1, D).transpose(3, 1, 0, 2).reshape(D, -1)),
        "dn0": np.ascontiguousarray(down.transpose(2, 0, 1).reshape(4, P, NE0, D).transpose(1, 2, 0, 3).reshape(P, -1)),
    }


def kernel(**inputs):
    import concourse.bacc as bacc
    from concourse.bass_utils import run_bass_kernel_spmd

    nc = bacc.Bacc("TRN2", target_bir_lowering=False, num_devices=1)
    arrays = lay_out(inputs)
    args = {n: nc.dram_tensor(f"in_{n}", v.shape, mybir.dt.from_np(v.dtype), kind="ExternalInput").ap() for n, v in arrays.items()}
    out = nc.dram_tensor("out_x", (NB, P, D), F32, kind="ExternalOutput").ap()
    build(nc, args, out)
    r = run_bass_kernel_spmd(nc, [{f"in_{n}": v for n, v in arrays.items()}], core_ids=[0])
    return r.results[0]["out_x"]
```
